# Optimizing a Trainium2 kernel written in Bass

```python
import numpy as np
import jax
import jax.numpy as jnp

def _softmax(x, axis=-1):
    return jax.nn.softmax(x, axis=axis)

def _gelu(x):
    return jax.nn.gelu(x, approximate=True)

def _silu(x):
    return jax.nn.silu(x)

def _sigmoid(x):
    return jax.nn.sigmoid(x)

def _layernorm(x, axis=-1, eps=1e-05):
    m = jnp.mean(x, axis=axis, keepdims=True)
    v = jnp.var(x, axis=axis, keepdims=True)
    return (x - m) / jnp.sqrt(v + eps)

def _scatter_add(tgt, idx, src, axis=0):
    return tgt.at[idx].add(src)

def _segment_sum(src, seg, n):
    return jax.ops.segment_sum(src, seg, n)
kernel_name = 'mk_xattn_ffn_d2_seqx_r4_227c76'

def setup_inputs(seed: int=0):
    np.random.seed(seed)
    _w = jnp.asarray

    def _rec_inputs():
        import jax
        import jax.numpy as jnp
        _rk = jax.random.key(seed)
        x = -0.0002928 + 1 * jax.random.normal(jax.random.fold_in(_rk, 1), (1, 2048, 256), jnp.float32)
        _lenS = 2048 - jax.random.randint(jax.random.fold_in(_rk, 7), (1,), 0, max(1, 2048 // 4) + 1, jnp.int32)
        _lenS2 = 1601 - jax.random.randint(jax.random.fold_in(_rk, 8), (1,), 0, max(1, 1601 // 4) + 1, jnp.int32)
        _ctx_1024P = jax.random.normal(jax.random.fold_in(_rk, 11), (1, 16, 256), jnp.float32)
        _ctx_1024c = jax.random.dirichlet(jax.random.fold_in(_rk, 511), 0.3 * jnp.ones((16,), jnp.float32), (1, 1601))
        _ctx_1024t = jnp.einsum('bsk,bkd->bsd', _ctx_1024c, _ctx_1024P)
        _ctx_1024t = _ctx_1024t * jax.lax.rsqrt(jnp.mean(jnp.square(_ctx_1024t)) + 1e-12) * 0.953939
        ctx_1024 = -1.39393e-06 + 0.999914 * (_ctx_1024t + 0.3 * jax.random.normal(jax.random.fold_in(_rk, 611), (1, 1601, 256), jnp.float32))
        _validS = jnp.arange(2048)[None, :] < _lenS[:, None]
        _validS2 = jnp.arange(1601)[None, :] < _lenS2[:, None]
        _causal = jnp.tril(jnp.ones((2048, 2048), dtype=bool))
        mask_BxS2_ik0 = jnp.where(jnp.broadcast_to(_validS2[:, :], (1, 1601)), 0, 1).astype(jnp.int32)
        return (x, ctx_1024, mask_BxS2_ik0)
    x, ctx_1024, mask_BxS2_ik0 = _rec_inputs()

    def _L0_xattn_setup():
        import jax, jax.numpy as jnp
        import numpy as np
        B, SQ, SKV, D, H = (2, 512, 512, 256, 16)
        W = D // H

        def _heads(x):
            b, s, _ = x.shape
            return x.reshape(b, s, H, W).transpose(0, 2, 1, 3)
        key = jax.random.key(seed)
        ks = jax.random.split(key, 10)
        s = 1.0 / np.sqrt(D)
        return {'x_q': jax.random.normal(ks[0], (B, SQ, D), jnp.float32), 'x_k': jax.random.normal(ks[1], (B, SKV, D), jnp.float32), 'x_v': jax.random.normal(ks[2], (B, SKV, D), jnp.float32), 'mask': jax.random.randint(ks[3], (B, SKV), 0, 2, jnp.int32), 'Wq': jax.random.normal(ks[4], (D, D), jnp.float32) * s, 'bq': jnp.zeros((D,), jnp.float32), 'Wk': jax.random.normal(ks[5], (D, D), jnp.float32) * s, 'bk': jnp.zeros((D,), jnp.float32), 'Wv': jax.random.normal(ks[6], (D, D), jnp.float32) * s, 'bv': jnp.zeros((D,), jnp.float32)}
    _L0_xattn_all = _L0_xattn_setup()
    _L0_xattn_in = {k: v for k, v in _L0_xattn_all.items() if k in ('Wq', 'bq', 'Wk', 'bk', 'Wv', 'bv')}
    del _L0_xattn_all

    def _L0_ffn_setup():
        import math
        import jax, jax.numpy as jnp
        import numpy as np
        B, T, D, H, E, K, S = (4, 1024, 256, 512, 16, 2, 2)
        ROUTE_SCALE = 1.0

        def _swiglu(x, w1, w3, w2):
            return jax.nn.silu(x @ w1) * (x @ w3) @ w2
        key = jax.random.key(seed)
        ks = jax.random.split(key, 9)
        s = 0.02
        return {'x': jax.random.normal(ks[0], (B, T, D), jnp.float32), 'gate_w': jax.random.normal(ks[1], (D, E), jnp.float32) * s, 'gate_b': jnp.zeros((E,), jnp.float32), 'ew1': jax.random.normal(ks[2], (E, D, H), jnp.float32) * s, 'ew3': jax.random.normal(ks[3], (E, D, H), jnp.float32) * s, 'ew2': jax.random.normal(ks[4], (E, H, D), jnp.float32) * s, 'sw1': jax.random.normal(ks[5], (S, D, H), jnp.float32) * s, 'sw3': jax.random.normal(ks[6], (S, D, H), jnp.float32) * s, 'sw2': jax.random.normal(ks[7], (S, H, D), jnp.float32) * s}
    _L0_ffn_all = _L0_ffn_setup()
    _L0_ffn_in = {k: v for k, v in _L0_ffn_all.items() if k in ('gate_w', 'gate_b', 'ew1', 'ew3', 'ew2', 'sw1', 'sw3', 'sw2')}
    del _L0_ffn_all

    def _L1_xattn_setup():
        import jax, jax.numpy as jnp
        import numpy as np
        DIM = 256
        SCALE_DIM = 4
        QK_DIM = DIM // SCALE_DIM
        B, S = (4, 1024)
        key = jax.random.key(seed)
        ks = jax.random.split(key, 8)
        std = 1.0 / np.sqrt(DIM)
        return {'q': jax.random.normal(ks[0], (B, S, DIM), jnp.float32), 'k': jax.random.normal(ks[1], (B, S, DIM), jnp.float32), 'v': jax.random.normal(ks[2], (B, S, DIM), jnp.float32), 'Wq': jax.random.normal(ks[3], (QK_DIM, DIM), jnp.float32) * std, 'bq': jnp.zeros((QK_DIM,), jnp.float32), 'Wk': jax.random.normal(ks[4], (QK_DIM, DIM), jnp.float32) * std, 'bk': jnp.zeros((QK_DIM,), jnp.float32), 'Wv': jax.random.normal(ks[5], (DIM, DIM), jnp.float32) * std, 'bv': jnp.zeros((DIM,), jnp.float32)}
    _L1_xattn_all = _L1_xattn_setup()
    _L1_xattn_in = {k: v for k, v in _L1_xattn_all.items() if k in ('Wq', 'bq', 'Wk', 'bk', 'Wv', 'bv')}
    del _L1_xattn_all

    def _L1_ffn_setup():
        import jax, jax.numpy as jnp
        import numpy as np
        EPS = 1e-05

        def rmsnorm(x):
            var = jnp.mean(jnp.square(x), axis=-1, keepdims=True)
            return x * jax.lax.rsqrt(var + 1e-06)

        def activation_quant(x):
            scale = 127.0 / jnp.clip(jnp.max(jnp.abs(x), axis=-1, keepdims=True), EPS, None)
            return jnp.clip(jnp.round(x * scale), -128, 127) / scale

        def weight_quant(w):
            scale = 1.0 / jnp.clip(jnp.mean(jnp.abs(w)), EPS, None)
            return jnp.clip(jnp.round(w * scale), -1, 1) / scale

        def bitlinear(x, w, b):
            xn = rmsnorm(x)
            xq = xn + jax.lax.stop_gradient(activation_quant(xn) - xn)
            wq = w + jax.lax.stop_gradient(weight_quant(w) - w)
            return jnp.einsum('bsi,oi->bso', xq, wq) + b
        key = jax.random.key(seed)
        k1, k2, k3 = jax.random.split(key, 3)
        B, S, D, H = (4, 512, 256, 1024)
        x = jax.random.normal(k1, (B, S, D), dtype=jnp.float32)
        w1 = jax.random.normal(k2, (H, D), dtype=jnp.float32) * D ** (-0.5)
        b1 = jnp.zeros((H,), dtype=jnp.float32)
        w2 = jax.random.normal(k3, (D, H), dtype=jnp.float32) * H ** (-0.5)
        b2 = jnp.zeros((D,), dtype=jnp.float32)
        return {'x': x, 'w1': w1, 'b1': b1, 'w2': w2, 'b2': b2}
    _L1_ffn_all = _L1_ffn_setup()
    _L1_ffn_in = {k: v for k, v in _L1_ffn_all.items() if k in ('w1', 'b1', 'w2', 'b2')}
    del _L1_ffn_all
    return {'x': x, 'ctx_1024': ctx_1024, 'mask_BxS2_ik0': mask_BxS2_ik0, 'L0_xattn_Wq': _L0_xattn_in['Wq'], 'L0_xattn_bq': _L0_xattn_in['bq'], 'L0_xattn_Wk': _L0_xattn_in['Wk'], 'L0_xattn_bk': _L0_xattn_in['bk'], 'L0_xattn_Wv': _L0_xattn_in['Wv'], 'L0_xattn_bv': _L0_xattn_in['bv'], 'L0_ffn_gate_w': _L0_ffn_in['gate_w'], 'L0_ffn_gate_b': _L0_ffn_in['gate_b'], 'L0_ffn_ew1': _L0_ffn_in['ew1'], 'L0_ffn_ew3': _L0_ffn_in['ew3'], 'L0_ffn_ew2': _L0_ffn_in['ew2'], 'L0_ffn_sw1': _L0_ffn_in['sw1'], 'L0_ffn_sw3': _L0_ffn_in['sw3'], 'L0_ffn_sw2': _L0_ffn_in['sw2'], 'L1_xattn_Wq': _L1_xattn_in['Wq'], 'L1_xattn_bq': _L1_xattn_in['bq'], 'L1_xattn_Wk': _L1_xattn_in['Wk'], 'L1_xattn_bk': _L1_xattn_in['bk'], 'L1_xattn_Wv': _L1_xattn_in['Wv'], 'L1_xattn_bv': _L1_xattn_in['bv'], 'L1_ffn_w1': _L1_ffn_in['w1'], 'L1_ffn_b1': _L1_ffn_in['b1'], 'L1_ffn_w2': _L1_ffn_in['w2'], 'L1_ffn_b2': _L1_ffn_in['b2']}

def reference(x, ctx_1024, mask_BxS2_ik0, L0_xattn_Wq, L0_xattn_bq, L0_xattn_Wk, L0_xattn_bk, L0_xattn_Wv, L0_xattn_bv, L0_ffn_gate_w, L0_ffn_gate_b, L0_ffn_ew1, L0_ffn_ew3, L0_ffn_ew2, L0_ffn_sw1, L0_ffn_sw3, L0_ffn_sw2, L1_xattn_Wq, L1_xattn_bq, L1_xattn_Wk, L1_xattn_bk, L1_xattn_Wv, L1_xattn_bv, L1_ffn_w1, L1_ffn_b1, L1_ffn_w2, L1_ffn_b2):
    import jax
    import jax.numpy as jnp

    def _L0_xattn_ref(x_q, x_k, x_v, mask, Wq, bq, Wk, bk, Wv, bv):
        import jax, jax.numpy as jnp
        import numpy as np
        B, SQ, SKV, D, H = (2, 512, 512, 256, 16)
        W = D // H

        def _heads(x):
            b, s, _ = x.shape
            return x.reshape(b, s, H, W).transpose(0, 2, 1, 3)
        q = _heads(x_q @ Wq.T + bq)
        k = _heads(x_k @ Wk.T + bk)
        v = _heads(x_v @ Wv.T + bv)
        scores = jnp.einsum('bhqw,bhkw->bhqk', q, k) / np.sqrt(W).astype(np.float32)
        m = mask[:, None, None, :].astype(scores.dtype)
        scores = scores - 10000.0 * (1.0 - m)
        p = jax.nn.softmax(scores, axis=-1)
        h = jnp.einsum('bhqk,bhkw->bhqw', p, v)
        return h.transpose(0, 2, 1, 3).reshape(x_q.shape[0], x_q.shape[1], D)

    def _L0_ffn_ref(x, gate_w, gate_b, ew1, ew3, ew2, sw1, sw3, sw2):
        import math
        import jax, jax.numpy as jnp
        import numpy as np
        B, T, D, H, E, K, S = (4, 1024, 256, 512, 16, 2, 2)
        ROUTE_SCALE = 1.0

        def _swiglu(x, w1, w3, w2):
            return jax.nn.silu(x @ w1) * (x @ w3) @ w2
        Bx, Tx, Dx = x.shape
        flat = x.reshape(-1, Dx)
        N = flat.shape[0]
        n_experts = gate_w.shape[1]
        logits = flat @ gate_w
        scores = jax.nn.softmax(logits.astype(jnp.float32), -1) + gate_b
        _, topi = jax.lax.top_k(scores, K)
        weights = jnp.take_along_axis(logits, topi, axis=-1) * ROUTE_SCALE
        weights = weights.astype(flat.dtype)
        capacity = math.ceil(N * K / n_experts * 1.25)

        def per_expert(gid, w1, w3, w2):
            match = topi == gid
            assigned = match.any(-1)
            w_tok = jnp.sum(jnp.where(match, weights, 0.0), -1)
            wm = jnp.where(assigned, w_tok, -jnp.inf)
            vals, idx = jax.lax.top_k(wm, capacity)
            valid = assigned[idx]
            xs = flat[idx]
            y = _swiglu(xs, w1, w3, w2) * jnp.where(valid, vals, 0.0)[:, None]
            return (idx, y)
        idxs, ys = jax.vmap(per_expert)(jnp.arange(n_experts), ew1, ew3, ew2)
        out = jnp.zeros_like(flat).at[idxs.reshape(-1)].add(ys.reshape(-1, Dx))
        shared = jax.vmap(lambda w1, w3, w2: _swiglu(flat, w1, w3, w2))(sw1, sw3, sw2)
        out = out + shared.mean(0)
        return out.reshape(Bx, Tx, Dx)

    def _L1_xattn_ref(q, k, v, Wq, bq, Wk, bk, Wv, bv):
        import jax, jax.numpy as jnp
        import numpy as np
        DIM = 256
        SCALE_DIM = 4
        QK_DIM = DIM // SCALE_DIM
        B, S = (4, 1024)
        scale = jnp.asarray(np.sqrt(QK_DIM), q.dtype)
        qp = jnp.einsum('bsd,ed->bse', q, Wq) + bq
        kp = jnp.einsum('bsd,ed->bse', k, Wk) + bk
        vp = jnp.einsum('bsd,ed->bse', v, Wv) + bv
        z = jnp.einsum('bqe,bke->bqk', qp, kp)
        z = jax.nn.sigmoid(z / scale)
        return jnp.einsum('bqk,bkd->bqd', z, vp)

    def _L1_ffn_ref(x, w1, b1, w2, b2):
        import jax, jax.numpy as jnp
        import numpy as np
        EPS = 1e-05

        def rmsnorm(x):
            var = jnp.mean(jnp.square(x), axis=-1, keepdims=True)
            return x * jax.lax.rsqrt(var + 1e-06)

        def activation_quant(x):
            scale = 127.0 / jnp.clip(jnp.max(jnp.abs(x), axis=-1, keepdims=True), EPS, None)
            return jnp.clip(jnp.round(x * scale), -128, 127) / scale

        def weight_quant(w):
            scale = 1.0 / jnp.clip(jnp.mean(jnp.abs(w)), EPS, None)
            return jnp.clip(jnp.round(w * scale), -1, 1) / scale

        def bitlinear(x, w, b):
            xn = rmsnorm(x)
            xq = xn + jax.lax.stop_gradient(activation_quant(xn) - xn)
            wq = w + jax.lax.stop_gradient(weight_quant(w) - w)
            return jnp.einsum('bsi,oi->bso', xq, wq) + b
        h = bitlinear(x, w1, b1)
        h = jax.nn.gelu(h, approximate=False)
        return bitlinear(h, w2, b2)
    x = x + _L0_xattn_ref(_layernorm(x, axis=-1), ctx_1024, ctx_1024, mask_BxS2_ik0, L0_xattn_Wq, L0_xattn_bq, L0_xattn_Wk, L0_xattn_bk, L0_xattn_Wv, L0_xattn_bv)
    x = x + _L0_ffn_ref(_layernorm(x, axis=-1), L0_ffn_gate_w, L0_ffn_gate_b, L0_ffn_ew1, L0_ffn_ew3, L0_ffn_ew2, L0_ffn_sw1, L0_ffn_sw3, L0_ffn_sw2)
    x = x + _L1_xattn_ref(_layernorm(x, axis=-1), ctx_1024, ctx_1024, L1_xattn_Wq, L1_xattn_bq, L1_xattn_Wk, L1_xattn_bk, L1_xattn_Wv, L1_xattn_bv)
    x = x + _L1_ffn_ref(_layernorm(x, axis=-1), L1_ffn_w1, L1_ffn_b1, L1_ffn_w2, L1_ffn_b2)
    return x

_drawn_inputs = setup_inputs


def setup_inputs(seed=0):
    import zlib

    import numpy as np

    out = dict(_drawn_inputs(seed))
    spreads = {'L0_xattn_bq': (0.0, 0.8),
     'L0_xattn_bk': (0.0, 2.0),
     'L0_xattn_bv': (0.0, 0.1),
     'L0_ffn_gate_b': (0.0, 0.8),
     'L1_xattn_bq': (0.0, 0.352),
     'L1_xattn_bk': (0.0, 0.1),
     'L1_xattn_bv': (0.0, 0.1),
     'L1_ffn_b1': (0.0, 2.0),
     'L1_ffn_b2': (0.0, 2.0)}
    factors = {'L0_ffn_gate_w': 8.0,
     'L0_ffn_ew1': 8.0,
     'L0_ffn_ew3': 8.0,
     'L0_ffn_ew2': 8.0,
     'L0_ffn_sw1': 8.0,
     'L0_ffn_sw3': 8.0,
     'L0_ffn_sw2': 8.0,
     'L1_ffn_w1': 44.347,
     'L1_ffn_w2': 38.409}
    for name, (base, spread) in spreads.items():
        noise = np.random.default_rng([zlib.crc32(name.encode()), seed]).standard_normal(out[name].shape)
        drawn = base * np.exp(spread * noise) if base else spread * noise
        out[name] = jnp.asarray(drawn.astype(out[name].dtype))
    for name, factor in factors.items():
        out[name] = (out[name] * factor).astype(out[name].dtype)
    return out
```

```python
from contextlib import ExitStack

import concourse.bass as bass
from concourse import mybir

F32 = mybir.dt.float32
BF16 = mybir.dt.bfloat16
I32 = mybir.dt.int32
U32 = mybir.dt.uint32
ALU = mybir.AluOpType
ACT = mybir.ActivationFunctionType
AX = mybir.AxisListType

P = 128
BANK = 512

N = 2048
D = 256
DC = D // P
NT = N // P
S = 1601
KT = -(-S // P)
TAIL = S - (KT - 1) * P
EPS_LN = 1e-5

H = 16
W = D // H
GROUPS = 4
HG = H // GROUPS
QB = N // BANK
STEPS = GROUPS * QB
QT = BANK // P
HEAD_PE = 32

THIRDS_K = (0, 1, 0, 2, 0, 1)
THIRDS_Q = (0, 0, 1, 0, 2, 1)
ROWS_PROD = W * len(THIRDS_K)
ROWS_MASKED = ROWS_PROD + 2
ROWS_ALL = ROWS_MASKED + 3
MASK_RAW = 10000.0 * W ** 0.5
SCORE_SCALE = W ** -0.5

MAX_CHUNK = 404
MAX_AT = (0, 404, 808, 1212)
RING = 4
UNITS = QT * HG
CHUNKS = UNITS * len(MAX_AT)
LEAD = 28


def key_rows(t):
    return P if t < KT - 1 else TAIL


def sub(flat, start, count):
    return flat[:, bass.ds(start, count)]


class Memory:

    def __init__(self, nc, scope):
        self.nc, self.scope = nc, scope

    def sb(self, name, shape, dt=F32):
        return self.scope.enter_context(self.nc.sbuf_tensor(name, shape, dt))

    def ps(self, name, shape, dt=F32):
        return self.scope.enter_context(self.nc.psum_tensor(name, shape, dt))

    def sem(self, name):
        return self.scope.enter_context(self.nc.semaphore(name))


def make_identity(pool, ident, zeroed, made):
    pool.memset(ident[:, :], 0.0).then_inc(zeroed, 1)
    pool.wait_ge(zeroed, 1)
    pool.affine_select(out=ident[:, :], in_=ident[:, :], compare_op=ALU.not_equal, fill=1.0, base=0,
                       pattern=[[-1, P]], channel_multiplier=1).then_inc(made, 1)


def project(nc, a, keep, x_tok, q_parts_dram, k_parts_dram):
    with ExitStack() as scope:
        m = Memory(nc, scope)
        ctxT = m.sb("ctxT", [P, DC, S])
        wq, wk, wv = (m.sb(f"w{c}_0", [P, DC, D]) for c in "qkv")
        bq, bk = m.sb("bq_col", [P, DC]), m.sb("bk_col", [P, DC])
        bv = m.sb("bv_rows", [P, D])
        mask_i = m.sb("mask_int", [1, S], I32)
        mask_raw = mask_i[:, :].bitcast(F32)
        mask_hi = m.sb("mask_hi", [1, S], BF16)
        mask_lo = m.sb("mask_lo", [1, S], BF16)
        stats = m.sb("ln_stats", [P, NT, 6])
        meanvar = m.sb("ln_meanvar", [P, NT, 2])
        std = m.sb("ln_std", [P, NT])
        rstd = m.sb("ln_rstd", [P, NT])
        eps = m.sb("ln_eps", [P, 1])
        projT = m.sb("projT", [P, DC, N])
        normed = projT[:, :, :].rearrange("p c n -> p (c n)").rearrange("p (t d) -> p t d", t=NT)
        normedT = m.sb("normedT", [P, DC, N])
        halves = normedT[:, :, :].rearrange("p c n -> p (c n)").bitcast(BF16).rearrange("p (i c n) -> p i c n", i=2, c=DC)
        third = [halves[:, 0], halves[:, 1], m.sb("third2", [P, DC, N], BF16)[:, :, :]]
        bank = [m.ps(f"proj_bank{i}", [P, BANK]) for i in range(4)]

        x_in, ctx_in, mask_in = (m.sem(s) for s in ("x_in", "ctx_in", "mask_in"))
        wq_in, wk_in, wv_in, b_in, bv_in = (m.sem(s) for s in ("wq_in", "wk_in", "wv_in", "b_in", "bv_in"))
        ident_zero, ident_made = m.sem("ident_zero"), m.sem("ident_made")
        stats_done, std_done, norm_done = m.sem("stats_done"), m.sem("std_done"), m.sem("norm_done")
        bank_full, bank_free_act, bank_free_dve = m.sem("bank_full"), m.sem("bank_free_act"), m.sem("bank_free_dve")
        split, mask_split, q_out, k_out = m.sem("split"), m.sem("mask_split"), m.sem("q_out"), m.sem("k_out")
        steps, aug_set, aug_in, values_set = m.sem("own_steps"), m.sem("aug_set"), m.sem("aug_in"), m.sem("values_set")

        FILLS_T = DC * (NT // 4)
        FILLS_P = DC * QB
        FILLS_QK = 2 * FILLS_P
        FILLS_V = KT

        n_act = FILLS_T + FILLS_QK

        block = scope.enter_context(nc.Block())

        @block.sync
        def _(sp):
            sp.dma_start(x_tok[:, :, :], a["x"].rearrange("b (t p) d -> p (b t) d", p=P)).then_inc(x_in, 16)
            sp.dma_start(wq[:, :, :], a["wqT"].rearrange("(c p) n -> p c n", p=P)).then_inc(wq_in, 16)
            sp.dma_start(bq[:, :], a["bq"].rearrange("(c p) -> p c", p=P), allow_slow_non_contiguous=True).then_inc(b_in, 16)
            sp.dma_start(bk[:, :], a["bk"].rearrange("(c p) -> p c", p=P), allow_slow_non_contiguous=True).then_inc(b_in, 16)
            sp.dma_start(mask_i[:, :], a["mask"]).then_inc(mask_in, 16)
            sp.dma_start(wk[:, :, :], a["wkT"].rearrange("(c p) n -> p c n", p=P)).then_inc(wk_in, 16)
            sp.dma_start(ctxT[:, :, :], a["ctxT"].rearrange("(c p) n -> p c n", p=P)).then_inc(ctx_in, 16)
            sp.dma_start(wv[:, :, :], a["wvT"].rearrange("(c p) n -> p c n", p=P)).then_inc(wv_in, 16)
            sp.dma_start(bv[:, :], a["bv"].partition_broadcast(P)).then_inc(bv_in, 16)
            for i in range(3):
                sp.wait_ge(split, i + 1)
                sp.dma_start(q_parts_dram[i].rearrange("(c p) n -> p c n", p=P), third[i][:, :, :]).then_inc(q_out, 16)
            for i in range(3):
                sp.wait_ge(split, 3 + i + 1)
                sp.dma_start(k_parts_dram[i].rearrange("(c p) n -> p c n", p=P), third[i][:, :, 0:S]).then_inc(k_out, 16)
            sp.wait_ge(k_out, 16 * 3)
            sp.wait_ge(q_out, 16 * 3)
            sp.wait_ge(aug_set, 2)
            for r, i in enumerate(THIRDS_K):
                sp.dma_start(keep["k_aug"][W * r:W * (r + 1), :, :],
                             k_parts_dram[i].rearrange("(h w) n -> w h n", w=W)).then_inc(aug_in, 16)
            sp.wait_ge(mask_split, 3)
            for h in range(H):
                sp.dma_start(keep["k_aug"][ROWS_PROD:ROWS_PROD + 1, h, :], mask_hi[:, :]).then_inc(aug_in, 16)
                sp.dma_start(keep["k_aug"][ROWS_PROD + 1:ROWS_PROD + 2, h, :], mask_lo[:, :]).then_inc(aug_in, 16)
            sp.wait_ge(aug_in, 16 * (len(THIRDS_K) + 2 * H))

        @block.gpsimd
        def _(pool):
            make_identity(pool, keep["ident"], ident_zero, ident_made)
            pool.wait_ge(ident_made, 1)
            pool.tensor_copy(keep["ident_bf"][:, :], keep["ident"][:, :]).then_inc(ident_made, 1)
            pool.wait_ge(ident_made, 2)
            pool.memset(keep["q_aug"][ROWS_PROD:P, :, :], 1.0).then_inc(aug_set, 1)
            pool.wait_ge(aug_set, 1)
            pool.memset(keep["k_aug"][ROWS_PROD:P, :, :], 1.0).then_inc(aug_set, 1)
            pool.wait_ge(aug_set, 2)
            pool.memset(keep["values_flat"][:, :], 0.0).then_inc(values_set, 1)
            pool.wait_ge(values_set, 1)
            pool.memset(keep["values"][:, :, :, :, W:W + 1], 1.0).then_inc(values_set, 1)

        @block.tensor
        def _(pe):
            fills = 0

            def take_bank():
                if fills >= 4:
                    seen = fills - 3
                    if seen <= n_act:
                        pe.wait_ge(bank_free_act, seen)
                    else:
                        pe.wait_ge(bank_free_act, n_act)
                        pe.wait_ge(bank_free_dve, seen - n_act)
                return bank[fills % 4]

            pe.wait_ge(ident_made, 1)
            for g in range(NT // 4):
                pe.wait_ge(norm_done, 4 * (g + 1))
                for c in range(DC):
                    b = take_bank()
                    for j in range(4):
                        last = pe.transpose(b[:, j * P:(j + 1) * P], normed[:, 4 * g + j, c * P:(c + 1) * P],
                                            keep["ident"][:, :])
                    last.then_inc(bank_full, 1)
                    fills += 1
            pe.wait_ge(wq_in, 16)
            for which, src, w in (("q", normedT, wq), ("k", ctxT, wk)):
                if which == "q":
                    pe.wait_ge(bank_free_act, FILLS_T)
                else:
                    pe.wait_ge(ctx_in, 16)
                    pe.wait_ge(wk_in, 16)
                width = N if which == "q" else S
                for mm in range(DC):
                    for n0 in range(0, width, BANK):
                        n1 = min(width, n0 + BANK)
                        b = take_bank()
                        for c in range(DC):
                            last = pe.matmul(b[:, 0:n1 - n0], w[:, c, mm * P:(mm + 1) * P], src[:, c, n0:n1],
                                             start=(c == 0), stop=(c == DC - 1))
                        last.then_inc(bank_full, 1)
                        fills += 1
            pe.wait_ge(wv_in, 16)
            for t in range(KT):
                b = take_bank()
                for c in range(DC):
                    last = pe.matmul(b[0:key_rows(t), 0:D], ctxT[:, c, t * P:t * P + key_rows(t)], wv[:, c, :],
                                     start=(c == 0), stop=(c == DC - 1))
                last.then_inc(bank_full, 1)
                fills += 1

        @block.scalar
        def _(act):
            act.wait_ge(stats_done, 2 * NT + 1)
            act.activation(std[:, :], meanvar[:, :, 1], ACT.Sqrt, bias=eps[:, 0:1]).then_inc(std_done, 1)
            fills = 0
            for g in range(NT // 4):
                for c in range(DC):
                    act.wait_ge(bank_full, fills + 1)
                    act.activation(normedT[:, c, g * BANK:(g + 1) * BANK], bank[fills % 4][:, :], ACT.Copy
                                   ).then_inc(bank_free_act, 1)
                    fills += 1
            act.wait_ge(b_in, 32)
            for which, bias, width in (("q", bq, N), ("k", bk, S)):
                if which == "k":
                    act.wait_ge(split, 3)
                for mm in range(DC):
                    for n0 in range(0, width, BANK):
                        n1 = min(width, n0 + BANK)
                        act.wait_ge(bank_full, fills + 1)
                        act.activation(projT[:, mm, n0:n1], bank[fills % 4][:, 0:n1 - n0], ACT.Identity,
                                       bias=bias[:, mm:mm + 1]).then_inc(bank_free_act, 1)
                        fills += 1

        @block.vector
        def _(dve):
            dve.memset(eps[:, :], EPS_LN).then_inc(stats_done, 1)
            dve.wait_ge(x_in, 16)
            for t in range(NT):
                dve.bn_stats(stats[:, t, :], x_tok[:, t, :]).then_inc(stats_done, 1)
            for t in range(NT):
                dve.wait_ge(stats_done, t + 2)
                dve.bn_aggr(meanvar[:, t, :], stats[:, t, :]).then_inc(stats_done, 1)
            dve.wait_ge(std_done, 1)
            dve.reciprocal(rstd[:, :], std[:, :]).then_inc(std_done, 1)
            dve.wait_ge(std_done, 2)
            dve.wait_ge(stats_done, 2 * NT + 1)
            for t in range(NT):
                dve.tensor_scalar(normed[:, t, :], x_tok[:, t, :], meanvar[:, t, 0:1], rstd[:, t:t + 1],
                                  ALU.subtract, ALU.mult).then_inc(norm_done, 1)
            dve.wait_ge(mask_in, 16)
            dve.tensor_scalar(mask_raw, mask_i[:, :], MASK_RAW, -MASK_RAW, ALU.mult, ALU.add).then_inc(mask_split, 1)
            dve.wait_ge(mask_split, 1)
            dve.tensor_copy(mask_hi[:, :], mask_raw).then_inc(mask_split, 1)
            dve.wait_ge(mask_split, 2)
            dve.tensor_tensor(mask_lo[:, :], mask_raw, mask_hi[:, :], ALU.subtract).then_inc(mask_split, 1)

            for which, width in (("q", N), ("k", S)):
                base = FILLS_T + (FILLS_P if which == "q" else FILLS_QK)
                dve.wait_ge(bank_free_act, base)
                if which == "k":
                    dve.wait_ge(q_out, 16 * 3)
                s0 = 0 if which == "q" else 3
                full = projT[:, :, 0:width]
                dve.tensor_copy(third[0][:, :, 0:width], full).then_inc(split, 1)
                dve.wait_ge(split, s0 + 1)
                dve.tensor_tensor(full, full, third[0][:, :, 0:width], ALU.subtract).then_inc(steps, 1)
                dve.wait_ge(steps, s0 // 3 + 1)
                dve.tensor_copy(third[1][:, :, 0:width], full).then_inc(split, 1)
                dve.wait_ge(split, s0 + 2)
                dve.tensor_tensor(third[2][:, :, 0:width], full, third[1][:, :, 0:width], ALU.subtract
                                  ).then_inc(split, 1)
            dve.wait_ge(bv_in, 16)
            dve.wait_ge(values_set, 1)
            for t in range(KT):
                rows = key_rows(t)
                f = n_act + t
                dve.wait_ge(bank_full, f + 1)
                dve.tensor_tensor(keep["values"][0:rows, :, t, :, 0:W],
                                  bank[f % 4][0:rows, 0:D].rearrange("p (g h w) -> p g h w", g=GROUPS, h=HG),
                                  bv[0:rows, :].rearrange("p (g h w) -> p g h w", g=GROUPS, h=HG),
                                  ALU.add).then_inc(bank_free_dve, 1)


def attend(nc, keep, x_tok, q_parts_dram):
    with ExitStack() as scope:
        m = Memory(nc, scope)
        q_aug = keep["q_aug"][:, :, :].rearrange("p s n -> p (s n)")
        k_flat = keep["k_aug"][:, :, :].rearrange("p h n -> p (h n)")
        values = keep["values_flat"]
        ident, ident_bf = keep["ident"], keep["ident_bf"]
        vals = m.sb("group_values", [P, KT, HG, HEAD_PE])
        probs = [m.sb(f"probs{i}", [P, HG, BANK]) for i in range(3)]
        acc_sb = m.sb("acc_sb", [P, BANK])
        max_part = m.sb("max_part", [P, UNITS, len(MAX_AT)])
        max_raw = m.sb("max_raw", [P, UNITS])
        max_rest = m.sb("max_rest", [P, UNITS])
        max_thirds = m.sb("max_thirds", [P, QT, 3, HG], BF16)
        max_rows = m.sb("max_rows", [3 * HG, BANK], BF16)
        recip = m.sb("recip", [P, QT, HG])
        head_out = m.sb("head_out", [P, QT, HG, W])
        scores = [m.ps(f"scores{i}", [P, 2, BANK]) for i in range(2)]
        max_bank = [m.ps(f"max_bank{i}", [P, BANK]) for i in range(2)]
        acc = m.ps("acc", [P, BANK])
        turn = m.ps("turn", [P, QT, P])
        turn_bf = turn[:, :, :].rearrange("p a b -> p (a b)").bitcast(BF16)

        score_free = m.sem("score_free")
        q_in = m.sem("q_in")
        score_ready = m.sem("score_ready")
        probs_free = m.sem("probs_free")
        max_free = m.sem("max_free")
        max_ready = m.sem("max_ready")
        acc_free = m.sem("acc_free")
        turned = m.sem("turned")
        added = m.sem("added")
        thirds_ready = m.sem("thirds_ready")
        rows_turned = m.sem("rows_turned")
        rows_ready = m.sem("rows_ready")
        max_placed = m.sem("max_placed")
        vals_ready = m.sem("vals_ready")
        max_chain = m.sem("max_chain")
        out_chain = m.sem("out_chain")

        CHAIN_MAX, CHAIN_OUT = 4, 2
        Q_LOAD = 16 * len(THIRDS_Q)
        HALF = KT // 2 + 1
        TURN_AFTER = 2
        OUT_AT = 5 * (TURN_AFTER + 1) + 1
        ROWS_LATER = 7
        ROWS_TILE = 10

        def chunk_plan(it, ahead):
            taken = LEAD if not isinstance(it, int) or it > 0 else 0
            first = [(1, c) for c in range(taken, CHUNKS)] if ahead >= 1 else []
            return first + ([(2, c) for c in range(LEAD)] if ahead >= 2 else [])

        def chunks_before(it):
            return CHUNKS if isinstance(it, int) and it == 0 else CHUNKS * it + CHUNKS + LEAD

        def is_first(it):
            return isinstance(it, int) and it == 0

        block = scope.enter_context(nc.Block())

        @block.tensor
        def _(pe):
            pe.sem_inc(probs_free, 3)
            pe.sem_inc(score_ready, 1)
            pe.sem_inc(turned, 1)

            def max_chunk(it, c, count):
                u, k = divmod(c, len(MAX_AT))
                qt, h = divmod(u, HG)
                n = min(MAX_CHUNK, S - MAX_AT[k])
                pe.wait_ge(max_free, count + 1)
                pe.matmul(max_bank[c % 2][:, 0:n],
                          q_aug[0:ROWS_MASKED, bass.ds(it % RING * (HG * BANK) + h * BANK + qt * P, P)],
                          k_flat[0:ROWS_MASKED, bass.ds(it // QB * (HG * S) + h * S + MAX_AT[k], n)],
                          start=True, stop=True).then_inc(max_ready, 1)

            def turn_rows(count):
                pe.wait_ge(thirds_ready, count + 1)
                if not is_first(count):
                    pe.wait_ge(added, count)
                for qt in range(QT):
                    last = pe.transpose(turn_bf[0:3 * HG, qt * P:(qt + 1) * P],
                                        max_thirds[:, qt, :, :].rearrange("p a b -> p (a b)"), ident_bf[:, :])
                last.then_inc(rows_turned, 1)

            def turn_sums(count, rows_before):
                pe.wait_ge(acc_free, count + 2)
                pe.wait_ge(added, count + 1)
                pe.wait_ge(rows_ready, rows_before)
                for qt in range(QT):
                    last = pe.transpose(turn[:, qt, :], acc_sb[:, qt * P:(qt + 1) * P], ident[:, :])
                last.then_inc(turned, 1)

            def score(it, t, h):
                pair, j = divmod(h, 2)
                rows = key_rows(t % KT)
                if j == 0:
                    pe.wait_ge(score_free, 2 * KT * it + 2 * t + pair + 1)
                at = it + t // KT
                last = pe.matmul(scores[pair][0:rows, j, :],
                                 k_flat[0:ROWS_ALL, bass.ds(at // QB * (HG * S) + h * S + t % KT * P, rows)],
                                 q_aug[0:ROWS_ALL, bass.ds(at % RING * (HG * BANK) + h * BANK, BANK)],
                                 start=True, stop=True)
                if j == 1:
                    last.then_inc(score_ready, 1)

            def weigh(it, t):
                rows = key_rows(t)
                pe.wait_ge(score_free, 2 * KT * it + 2 * t + 4)
                if t == 0:
                    pe.wait_ge(vals_ready, 2 * it + 1)
                    pe.wait_ge(acc_free, it + 1)
                if t == HALF:
                    pe.wait_ge(vals_ready, 2 * it + 2)
                slot = 2 if t == KT - 1 else t % 2
                for h in range(HG):
                    last = pe.matmul(acc[HEAD_PE * h:HEAD_PE * (h + 1), :], vals[0:rows, t, h, :],
                                     probs[slot][0:rows, h, :], start=(t == 0), stop=(t == KT - 1),
                                     tile_position=(0, HEAD_PE * h))
                last.then_inc(probs_free, 1)

            def step(it, ahead):
                plan = chunk_plan(it, ahead)
                complete = sum(k == 1 for k, _ in plan)
                slots = 5 * KT
                rate = max(len(plan), CHUNKS)
                done = 0

                def some_chunks(slot):
                    nonlocal done
                    while done < len(plan) and done < -(-(slot + 1) * rate // slots):
                        k, c = plan[done]
                        if (k, c) == (2, 0):
                            pe.wait_ge(q_in, Q_LOAD * (it + 3))
                        max_chunk(it + k, c, chunks_before(it) + done)
                        done += 1
                        if ahead >= 1 and done == min(complete + ROWS_LATER, len(plan)):
                            turn_rows(it + 1)

                for t in range(KT):
                    if t == KT - 1 and ahead >= 1:
                        pe.wait_ge(max_placed, 16 * it + 32)
                    for h in range(HG):
                        if t < KT - 1 or ahead >= 1:
                            score(it, t + 1, h)
                        some_chunks(5 * t + h)
                    weigh(it, t)
                    if t == TURN_AFTER and not is_first(it):
                        turn_sums(it - 1, it + 1)
                    some_chunks(5 * t + 4)

            pe.wait_ge(q_in, Q_LOAD)
            for c in range(CHUNKS):
                max_chunk(0, c, c)
            pe.wait_ge(q_in, 2 * Q_LOAD)
            turn_rows(0)
            pe.wait_ge(max_placed, 16)
            for h in range(HG):
                score(0, 0, h)
            step(0, 2)
            with pe.Fori(1, STEPS - 2) as it:
                step(it, 2)
            step(STEPS - 2, 1)
            step(STEPS - 1, 0)
            turn_sums(STEPS - 1, STEPS)

        @block.scalar
        def _(act):
            act.sem_inc(score_free, 2)
            act.sem_inc(acc_free, 1)

            def copy_rows(count):
                act.wait_ge(rows_turned, count + 1)
                if not is_first(count):
                    act.wait_ge(max_placed, 16 * count)
                act.activation(max_rows[:, :], turn_bf[0:3 * HG, 0:BANK], ACT.Copy).then_inc(rows_ready, 1)

            def copy_sums(count):
                act.wait_ge(probs_free, KT * count + KT + 3)
                act.wait_ge(turned, count + 1)
                act.activation(acc_sb[:, :], acc[:, :], ACT.Copy).then_inc(acc_free, 1)

            def step(it, ahead):
                for t in range(KT):
                    rows = key_rows(t)
                    slot = 2 if t == KT - 1 else t % 2
                    back = {0: 1, 1: 2, KT - 1: 3}.get(t, t + 2)
                    act.wait_ge(probs_free, KT * it + back)
                    for pair in range(2):
                        act.wait_ge(score_ready, 2 * KT * it + 2 * t + pair + 2)
                        act.activation(probs[slot][0:rows, 2 * pair:2 * pair + 2, :], scores[pair][0:rows, :, :],
                                       ACT.Exp, scale=SCORE_SCALE).then_inc(score_free, 1)
                    if t == 0 and not is_first(it):
                        copy_sums(it - 1)
                    if t == ROWS_TILE and ahead >= 1:
                        copy_rows(it + 1)

            copy_rows(0)
            step(0, 2)
            with act.Fori(1, STEPS - 2) as it:
                step(it, 2)
            step(STEPS - 2, 1)
            step(STEPS - 1, 0)
            copy_sums(STEPS - 1)

        @block.gpsimd
        def _(pool):
            def place_values(count, half):
                lo, hi = (0, HALF) if half == 0 else (HALF, KT)
                if not is_first(count):
                    pool.wait_ge(probs_free, KT * (count - 1) + hi + 3)
                pool.tensor_copy(vals[:, lo:hi, :, :].rearrange("p t h w -> p (t h w)"),
                                 values[:, bass.ds(count // QB * (KT * HG * HEAD_PE) + lo * (HG * HEAD_PE),
                                                   (hi - lo) * HG * HEAD_PE)]).then_inc(vals_ready, 1)

            place_values(0, 0)
            place_values(0, 1)
            with pool.Fori(1, STEPS) as it:
                place_values(it, 0)
                place_values(it, 1)

        @block.vector
        def _(dve):
            dve.sem_inc(max_free, 2)
            dve.sem_inc(added, 1)

            def reduce_chunk(c, count):
                u, k = divmod(c, len(MAX_AT))
                n = min(MAX_CHUNK, S - MAX_AT[k])
                dve.wait_ge(max_ready, count + 1)
                dve.tensor_reduce(max_part[:, u, k:k + 1], max_bank[c % 2][:, 0:n], AX.X, ALU.max
                                  ).then_inc(max_free, 1)

            th = [max_thirds[:, :, i, :] for i in range(3)]
            raw, rest = (x[:, :].rearrange("p (q h) -> p q h", h=HG) for x in (max_raw, max_rest))

            def split_maxima(count, reduced, part):
                if part == 0:
                    dve.wait_ge(max_free, reduced + 2)
                    dve.tensor_reduce(max_raw[:, :], max_part[:, :, :], AX.X, ALU.max).then_inc(max_chain, 1)
                    dve.wait_ge(max_chain, CHAIN_MAX * count + 1)
                    return
                if part == 1:
                    if not is_first(count):
                        dve.wait_ge(rows_turned, count)
                    dve.tensor_scalar(th[0], raw, -1.0, None, ALU.mult).then_inc(max_chain, 1)
                    return
                dve.wait_ge(max_chain, CHAIN_MAX * count + part)
                if part == 2:
                    dve.scalar_tensor_tensor(rest, raw, -1.0, th[0], ALU.mult, ALU.subtract).then_inc(max_chain, 1)
                if part == 3:
                    dve.tensor_copy(th[1], rest).then_inc(max_chain, 1)
                if part == 4:
                    dve.tensor_tensor(th[2], rest, th[1], ALU.subtract).then_inc(thirds_ready, 1)

            sums = turn[:, :, :].rearrange("p q (h w) -> p q h w", h=HG)

            def add_sums(count, part):
                if part == 0:
                    dve.wait_ge(turned, count + 2)
                    dve.reciprocal(recip[:, :, :], sums[:, :, :, W]).then_inc(out_chain, 1)
                if part == 1:
                    dve.wait_ge(out_chain, CHAIN_OUT * count + 1)
                    dve.tensor_tensor(head_out[:, :, :, :], sums[:, :, :, 0:W],
                                      recip[:, :, :].rearrange("p q (h o) -> p q h o", o=1).broadcast_to([P, QT, HG, W]),
                                      ALU.mult).then_inc(out_chain, 1)
                if part == 2:
                    dve.wait_ge(out_chain, CHAIN_OUT * count + 2)
                    xv = x_tok[:, bass.ds(count % QB * QT, QT), bass.ds(count // QB * (HG * W), HG * W)]
                    dve.tensor_tensor(xv, xv, head_out[:, :, :, :].rearrange("p q h w -> p q (h w)"), ALU.add
                                      ).then_inc(added, 1)

            def step(it, ahead):
                plan = chunk_plan(it, ahead)
                complete = sum(k == 1 for k, _ in plan)
                base = chunks_before(it)
                for n in range(max(len(plan), OUT_AT + 3, complete + 5)):
                    if n < len(plan):
                        reduce_chunk(plan[n][1], base + n)
                    if not is_first(it) and OUT_AT <= n < OUT_AT + 3:
                        add_sums(it - 1, n - OUT_AT)
                    if ahead >= 1 and complete - 1 <= n < complete + 4:
                        split_maxima(it + 1, base + complete, n - complete + 1)

            for c in range(CHUNKS):
                reduce_chunk(c, c)
            for part in range(5):
                split_maxima(0, CHUNKS, part)
            step(0, 2)
            with dve.Fori(1, STEPS - 2) as it:
                step(it, 2)
            step(STEPS - 2, 1)
            step(STEPS - 1, 0)
            for part in range(3):
                add_sums(STEPS - 1, part)

        @block.sync
        def _(sp):
            def load_queries(count):
                if not is_first(count):
                    sp.wait_ge(q_in, Q_LOAD * count)
                for r, i in enumerate(THIRDS_Q):
                    sp.dma_start(
                        q_aug[W * r:W * (r + 1), bass.ds(count % RING * (HG * BANK), HG * BANK)].rearrange("p (h n) -> p h n", h=HG),
                        q_parts_dram[i, bass.ds(count // QB * (HG * W), HG * W), bass.ds(count % QB * BANK, BANK)].rearrange("(h w) n -> w h n", h=HG)
                    ).then_inc(q_in, 16)

            def place(count):
                sp.wait_ge(rows_ready, count + 1)
                sp.dma_start(
                    q_aug[ROWS_MASKED:ROWS_ALL, bass.ds(count % RING * (HG * BANK), HG * BANK)],
                    max_rows[:, :]).then_inc(max_placed, 16)

            for count in range(RING - 1):
                load_queries(count)
            place(0)
            with sp.Fori(0, STEPS - RING + 1) as it:
                sp.wait_ge(score_ready, 2 * KT * it + 1)
                load_queries(it + RING - 1)
                place(it + 1)
            for count in range(STEPS - RING + 2, STEPS):
                place(count)
            sp.wait_ge(max_placed, 16 * STEPS)


E = 16
F = 512
FC = F // P
SHARED = 2
TOP = 2
CAP = -(-N * TOP * 5 // (E * 4))
CAP_TILES = -(-CAP // P)
SLOTS = E * CAP
CHUNK_TOK = N // (P // E)
NCH = N // CHUNK_TOK
KEY_BITS = 16
KEY_ABOVE = 131072.0

C_SUM, C_BEFORE = 0, P
C_BASE = 2 * P
C_EXPERT = C_BASE + 1
C_DUMMY = C_EXPERT + E
C_ALL = C_DUMMY + TOP * NT


def shape_constants(np):
    c = np.zeros((P, C_ALL), np.float32)
    e, chunk = np.arange(P) // NCH, np.arange(P) % NCH
    same = e[:, None] == e[None, :]
    c[:, C_SUM:C_SUM + P] = same
    c[:, C_BEFORE:C_BEFORE + P] = same & (chunk[:, None] < chunk[None, :])
    c[:, C_BASE] = e * CAP + 1
    c[:, C_EXPERT:C_EXPERT + E] = np.arange(E)
    t = np.arange(NT)[None, :] * P + np.arange(P)[:, None]
    for k in range(TOP):
        c[:, C_DUMMY + k * NT:C_DUMMY + (k + 1) * NT] = SLOTS + k * N + t
    return c


class Norm:

    def __init__(self, m, tag, normed):
        self.stats = m.sb(f"{tag}_stats", [P, NT, 6])
        self.meanvar = m.sb(f"{tag}_meanvar", [P, NT, 2])
        self.std, self.rstd = m.sb(f"{tag}_std", [P, NT]), m.sb(f"{tag}_rstd", [P, NT])
        self.eps = m.sb(f"{tag}_eps", [P, 1])
        self.normed = normed
        self.stats_done = m.sem(f"{tag}_stats_done")
        self.std_done = m.sem(f"{tag}_std_done")
        self.rstd_done = m.sem(f"{tag}_rstd_done")
        self.norm_done = m.sem(f"{tag}_norm_done")

    def on_vector(self, dve, x_tok):
        dve.memset(self.eps[:, :], EPS_LN).then_inc(self.stats_done, 1)
        for t in range(NT):
            dve.bn_stats(self.stats[:, t, :], x_tok[:, t, :]).then_inc(self.stats_done, 1)
        for t in range(NT):
            dve.wait_ge(self.stats_done, t + 2)
            dve.bn_aggr(self.meanvar[:, t, :], self.stats[:, t, :]).then_inc(self.stats_done, 1)
        dve.wait_ge(self.std_done, 1)
        dve.reciprocal(self.rstd[:, :], self.std[:, :]).then_inc(self.rstd_done, 1)
        dve.wait_ge(self.rstd_done, 1)
        dve.wait_ge(self.stats_done, 2 * NT + 1)
        for t in range(NT):
            dve.tensor_scalar(self.normed[:, t, :], x_tok[:, t, :], self.meanvar[:, t, 0:1], self.rstd[:, t:t + 1],
                              ALU.subtract, ALU.mult).then_inc(self.norm_done, 1)

    def on_scalar(self, act):
        act.wait_ge(self.stats_done, 2 * NT + 1)
        act.activation(self.std[:, :], self.meanvar[:, :, 1], ACT.Sqrt, bias=self.eps[:, 0:1]).then_inc(self.std_done, 1)


def route_and_share(nc, a, keep, x_tok, normed, slots_in_dram, route):
    with ExitStack() as scope:
        m = Memory(nc, scope)
        ident = keep["ident"]
        norm = Norm(m, "ln2", normed)
        tokT = m.sb("tokT", [P, DC, N])
        sw1, sw3 = (m.sb(n, [P, SHARED, DC, F]) for n in ("sw1_sb", "sw3_sb"))
        sw2 = m.sb("sw2_sb", [P, SHARED, FC, D])
        gate_w, gate_b = m.sb("gate_w_sb", [P, DC, E]), m.sb("gate_b_rows", [P, E])
        const = m.sb("const", [P, C_ALL])
        zeros = m.sb("zeros", [P, 2560])
        silu = [m.sb(f"silu{i}", [P, BANK]) for i in range(2)]
        hidden = [m.sb(f"hidden{i}", [P, SHARED * FC, BANK]) for i in range(2)]
        gu = [m.ps(f"gu{i}", [P, 2, BANK]) for i in range(2)]
        y_bank = [m.ps(f"y_bank{i}", [P, BANK]) for i in range(2)]
        small = m.ps("small", [P, BANK])
        wide = m.ps("wide", [P, BANK])

        logits, gates, onehot1, onehot2, work, key = (m.sb(n, [P, NT, E]) for n in
                                                      ("logits", "gates", "onehot1", "onehot2", "work", "rkey"))
        col = m.sb("col", [P, NT])
        col2 = m.sb("col2", [P, NT])
        chosen_logit = [m.sb(f"chosen_logit{k}", [P, NT]) for k in range(TOP)]
        bits, sign = m.sb("bits", [P, NT, E], I32), m.sb("sign", [P, NT, E], I32)
        hi_tok, lo_tok = m.sb("hi_tok", [P, 2, E, NCH]), m.sb("lo_tok", [P, 2, E, NCH])
        slot_tok = m.sb("slot_tok", [P, NT, E])
        hi, lo = m.sb("hi", [P, CHUNK_TOK]), m.sb("lo", [P, CHUNK_TOK])
        above, equal, r1, r2, r3 = (m.sb(n, [P, CHUNK_TOK]) for n in ("above", "equal", "r1", "r2", "r3"))
        ones = m.sb("ones_row", [P, CHUNK_TOK])
        cand, step_sz, cnt, inc = (m.sb(n, [P, 1]) for n in ("cand", "step_sz", "cnt", "inc"))
        totals = m.sb("totals", [P, 2])
        offs = m.sb("offs", [P, 4])

        sh_in, gate_in, const_in = m.sem("sh_in"), m.sem("gate_in"), m.sem("const_in")
        zero_set, zero_out = m.sem("zero_set"), m.sem("zero_out")
        t_full, t_free = m.sem("t_full"), m.sem("t_free")
        logits_ready, shifted, expd = m.sem("logits_ready"), m.sem("shifted"), m.sem("expd")
        gu_ready, silu_done, h_done = m.sem("gu_ready"), m.sem("silu_done"), m.sem("h_done")
        y_ready, y_done = m.sem("y_ready"), m.sem("y_done")
        keys_ready, keys_turned = m.sem("keys_ready"), m.sem("keys_turned")
        counted, summed = m.sem("counted"), m.sem("summed")
        totals_ready, offs_ready = m.sem("totals_ready"), m.sem("offs_ready")
        slots_ready, slots_turned = m.sem("slots_ready"), m.sem("slots_turned")
        idx_ready, sent = m.sem("idx_ready"), m.sem("sent")
        chain = m.sem("route_chain")

        UB = SHARED * FC
        BLOCKS = N // BANK
        KEYS_AT = (0, 6)
        OFFS_AT, TURN_AT = (3, 1), (3, 3)

        block = scope.enter_context(nc.Block())

        @block.sync
        def _(sp):
            sp.dma_start(gate_w[:, :, :], a["gate_w"].rearrange("(c p) e -> p c e", p=P)).then_inc(gate_in, 16)
            sp.dma_start(gate_b[:, :], a["gate_b"].partition_broadcast(P)).then_inc(gate_in, 16)
            for s in range(SHARED):
                sp.dma_start(sw1[:, s], a["sw1"][s].rearrange("(c p) f -> p c f", p=P)).then_inc(sh_in, 16)
                sp.dma_start(sw3[:, s], a["sw3"][s].rearrange("(c p) f -> p c f", p=P)).then_inc(sh_in, 16)
                sp.dma_start(sw2[:, s], a["sw2"][s].rearrange("(c p) f -> p c f", p=P)).then_inc(sh_in, 16)
            sp.dma_start(const[:, :], a["const"]).then_inc(const_in, 16)
            sp.wait_ge(zero_set, 1)
            for i in range(SLOTS * D // (P * 2560)):
                r = P * 2560 // D
                sp.dma_start(slots_in_dram[i * r:(i + 1) * r, :].rearrange("(p k) d -> p (k d)", p=P), zeros[:, :]
                             ).then_inc(zero_out, 16)
            sp.wait_ge(zero_out, 16 * (SLOTS * D // (P * 2560)))

        @block.gpsimd
        def _(pool):
            pool.memset(zeros[:, :], 0.0).then_inc(zero_set, 1)
            pool.wait_ge(zero_out, 16 * (SLOTS * D // (P * 2560)))
            pool.wait_ge(idx_ready, TOP)
            pool.wait_ge(norm.norm_done, NT)
            for k in range(TOP):
                for t in range(NT):
                    pool.indirect_dma_start(
                        out=slots_in_dram[:, :], out_offset=bass.IndirectOffsetOnAxis(ap=route["send"][k][:, t:t + 1], axis=0),
                        in_=normed[:, t, :], in_offset=None).then_inc(sent, 16)
            pool.wait_ge(sent, 16 * TOP * NT)

        @block.tensor
        def _(pe):
            for f in range(DC * NT // 4):
                g, c = divmod(f, DC)
                pe.wait_ge(norm.norm_done, 4 * (g + 1))
                if f >= 4:
                    pe.wait_ge(t_free, f - 3)
                b = gu[f % 4 // 2][:, f % 2, :]
                for j in range(4):
                    last = pe.transpose(b[:, j * P:(j + 1) * P], normed[:, 4 * g + j, c * P:(c + 1) * P], ident[:, :])
                last.then_inc(t_full, 1)
            pe.wait_ge(t_free, DC * NT // 4)
            pe.wait_ge(gate_in, 32)
            for t in range(NT):
                for c in range(DC):
                    last = pe.matmul(small[:, t * E:(t + 1) * E], tokT[:, c, t * P:(t + 1) * P], gate_w[:, c, :],
                                     start=(c == 0), stop=(c == DC - 1))
            last.then_inc(logits_ready, 1)
            pe.wait_ge(sh_in, 16 * 3 * SHARED)
            pe.wait_ge(const_in, 16)

            def unit(blk, u):
                n = UB * blk + u
                s, f = divmod(u, FC)
                if n >= 2:
                    pe.wait_ge(h_done, n - 1)
                for j, w in enumerate((sw1, sw3)):
                    for c in range(DC):
                        last = pe.matmul(gu[n % 2][:, j, :], w[:, s, c, f * P:(f + 1) * P],
                                         tokT[:, c, blk * BANK:(blk + 1) * BANK], start=(c == 0), stop=(c == DC - 1))
                last.then_inc(gu_ready, 1)

            def down(blk):
                pe.wait_ge(h_done, UB * (blk + 1))
                for tt in range(BANK // P):
                    t = 4 * blk + tt
                    if t >= 2:
                        pe.wait_ge(y_done, t - 1)
                    for u in range(UB):
                        s, f = divmod(u, FC)
                        last = pe.matmul(y_bank[tt % 2][:, 0:D], hidden[blk % 2][:, u, tt * P:(tt + 1) * P],
                                         sw2[:, s, f, :], start=(u == 0), stop=(u == UB - 1))
                    last.then_inc(y_ready, 1)

            counts = 0
            for blk in range(BLOCKS):
                for u in range(UB):
                    unit(blk, u)
                    if u == 1 and blk > 0:
                        down(blk - 1)
                    if (blk, u) == KEYS_AT:
                        pe.wait_ge(keys_ready, 1)
                        for j, src in enumerate((hi_tok, lo_tok)):
                            for s in range(2):
                                last = pe.transpose(wide[:, j * CHUNK_TOK + s * P:j * CHUNK_TOK + (s + 1) * P],
                                                    src[:, s].rearrange("p e c -> p (e c)"), ident[:, :])
                        last.then_inc(keys_turned, 1)
                    if blk in (1, 2):
                        for _ in range(KEY_BITS // UB):
                            counts += 1
                            pe.wait_ge(counted, counts)
                            pe.matmul(small[:, 0:1], const[:, C_SUM:C_SUM + P], cnt[:, :], start=True, stop=True
                                      ).then_inc(summed, 1)
                    if (blk, u) == OFFS_AT:
                        pe.wait_ge(totals_ready, 1)
                        pe.matmul(small[:, 0:2], const[:, C_BEFORE:C_BEFORE + P], totals[:, :], start=True, stop=True)
                        pe.matmul(small[:, 2:4], const[:, C_SUM:C_SUM + P], totals[:, :], start=True, stop=True
                                  ).then_inc(offs_ready, 1)
                    if (blk, u) == TURN_AT:
                        pe.wait_ge(slots_ready, 1)
                        for s in range(2):
                            last = pe.transpose(wide[:, s * P:(s + 1) * P], r1[:, s * P:(s + 1) * P], ident[:, :])
                        last.then_inc(slots_turned, 1)
            down(BLOCKS - 1)

        @block.scalar
        def _(act):
            norm.on_scalar(act)
            for f in range(DC * NT // 4):
                g, c = divmod(f, DC)
                act.wait_ge(t_full, f + 1)
                act.activation(tokT[:, c, g * BANK:(g + 1) * BANK], gu[f % 4 // 2][:, f % 2, :], ACT.Copy
                               ).then_inc(t_free, 1)
            act.wait_ge(shifted, 1)
            act.activation(gates[:, :, :], work[:, :, :], ACT.Exp).then_inc(expd, 1)
            for n in range(UB * BLOCKS):
                act.wait_ge(gu_ready, n + 1)
                if n >= 2:
                    act.wait_ge(h_done, n - 1)
                act.activation(silu[n % 2][:, :], gu[n % 2][:, 0, :], ACT.Silu).then_inc(silu_done, 1)

        @block.vector
        def _(dve):
            made = 0

            def link(ins):
                nonlocal made
                made += 1
                ins.then_inc(chain, 1)
                dve.wait_ge(chain, made)

            def over_experts(x):
                return x[:, :].rearrange("p (t o) -> p t o", o=1).broadcast_to([P, NT, E])

            def over_tokens(x):
                return x.rearrange("p (o e) -> p o e", o=1).broadcast_to([P, NT, E])

            def unit(n):
                dve.wait_ge(silu_done, n + 1)
                if n >= 2 * UB:
                    dve.wait_ge(y_ready, 4 * (n // UB - 1))
                dve.tensor_tensor(hidden[n // UB % 2][:, n % UB, :], silu[n % 2][:, :], gu[n % 2][:, 1, :], ALU.mult
                                  ).then_inc(h_done, 1)

            def down(blk):
                for tt in range(4):
                    t = 4 * blk + tt
                    dve.wait_ge(y_ready, t + 1)
                    dve.scalar_tensor_tensor(x_tok[:, t, :], y_bank[tt % 2][:, 0:D], 1.0 / SHARED, x_tok[:, t, :],
                                             ALU.mult, ALU.add).then_inc(y_done, 1)

            def choose():
                dve.wait_ge(logits_ready, 1)
                link(dve.tensor_copy(logits[:, :, :], small[:, 0:NT * E].rearrange("p (t e) -> p t e", e=E)))
                link(dve.tensor_reduce(col[:, :], logits[:, :, :], AX.X, ALU.max))
                dve.tensor_tensor(work[:, :, :], logits[:, :, :], over_experts(col), ALU.subtract).then_inc(shifted, 1)
                dve.wait_ge(expd, 1)
                link(dve.tensor_reduce(col[:, :], gates[:, :, :], AX.X, ALU.add))
                link(dve.reciprocal(col2[:, :], col[:, :]))
                link(dve.tensor_tensor(gates[:, :, :], gates[:, :, :], over_experts(col2), ALU.mult))
                link(dve.tensor_tensor(gates[:, :, :], gates[:, :, :], over_tokens(gate_b[:, :]), ALU.add))
                for k, onehot in enumerate((onehot1, onehot2)):
                    link(dve.tensor_reduce(col[:, :], gates[:, :, :], AX.X, ALU.max))
                    link(dve.tensor_tensor(work[:, :, :], gates[:, :, :], over_experts(col), ALU.is_equal))
                    link(dve.scalar_tensor_tensor(key[:, :, :], work[:, :, :], -float(2 * E),
                                                  over_tokens(const[:, C_EXPERT:C_EXPERT + E]), ALU.mult, ALU.add))
                    link(dve.tensor_reduce(col[:, :], key[:, :, :], AX.X, ALU.min))
                    link(dve.tensor_tensor(onehot[:, :, :], key[:, :, :], over_experts(col), ALU.is_equal))
                    link(dve.tensor_tensor(work[:, :, :], logits[:, :, :], onehot[:, :, :], ALU.mult))
                    link(dve.tensor_reduce(chosen_logit[k][:, :], work[:, :, :], AX.X, ALU.add))
                    if k == 0:
                        link(dve.scalar_tensor_tensor(gates[:, :, :], onehot[:, :, :], -1e30, gates[:, :, :],
                                                      ALU.mult, ALU.add))

            def order_keys():
                raw = logits[:, :, :].bitcast(I32)
                link(dve.tensor_scalar(sign[:, :, :], raw, 31, 0x7FFFFFFF, ALU.arith_shift_right, ALU.bitwise_and))
                link(dve.tensor_tensor(bits[:, :, :], raw, sign[:, :, :], ALU.bitwise_xor))
                link(dve.tensor_scalar(sign[:, :, :], bits[:, :, :], 16, None, ALU.arith_shift_right))
                link(dve.tensor_scalar(bits[:, :, :], bits[:, :, :], 0xFFFF, None, ALU.bitwise_and))
                link(dve.tensor_tensor(work[:, :, :], onehot1[:, :, :], onehot2[:, :, :], ALU.add))
                link(dve.scalar_tensor_tensor(key[:, :, :], sign[:, :, :], 32769.0, work[:, :, :], ALU.add, ALU.mult))
                for s in range(2):
                    v = key[:, :, :].rearrange("p (c s) e -> p s e c", s=2)[:, s]
                    link(dve.tensor_copy(hi_tok[:, s], v))
                    v = bits[:, :, :].rearrange("p (c s) e -> p s e c", s=2)[:, s]
                    if s == 0:
                        link(dve.tensor_copy(lo_tok[:, s], v))
                    else:
                        dve.tensor_copy(lo_tok[:, s], v).then_inc(keys_ready, 1)

            def start_search():
                dve.memset(cand[:, :], 2.0 ** (KEY_BITS - 1)).then_inc(chain, 1)
                nonlocal made
                made += 1
                link(dve.memset(step_sz[:, :], 2.0 ** (KEY_BITS - 1)))

            searches = 0

            def search(key_of):
                nonlocal searches
                searches += 1
                dve.tensor_scalar(r3[:, :], key_of[:, :], cand[:, 0:1], None, ALU.is_ge, ALU.add, accum_out=cnt[:, :]
                                  ).then_inc(counted, 1)
                dve.wait_ge(summed, searches)
                link(dve.tensor_scalar(inc[:, :], small[:, 0:1], float(CAP), step_sz[:, 0:1], ALU.is_ge, ALU.mult))
                link(dve.tensor_scalar(step_sz[:, :], step_sz[:, :], 0.5, None, ALU.mult))
                link(dve.scalar_tensor_tensor(cand[:, :], inc[:, :], step_sz[:, 0:1], cand[:, :], ALU.subtract, ALU.add))

            def lower_keys():
                link(dve.tensor_scalar(cand[:, :], cand[:, :], -0.5, None, ALU.add))
                link(dve.tensor_scalar(above[:, :], hi[:, :], cand[:, 0:1], None, ALU.is_gt))
                link(dve.tensor_scalar(equal[:, :], hi[:, :], cand[:, 0:1], None, ALU.is_equal))
                link(dve.scalar_tensor_tensor(r1[:, :], lo[:, :], 1.0, equal[:, :], ALU.add, ALU.mult))
                link(dve.scalar_tensor_tensor(r2[:, :], above[:, :], KEY_ABOVE, r1[:, :], ALU.mult, ALU.add))
                link(dve.tensor_scalar(lo[:, :], r2[:, :], -1.0, None, ALU.add))

            def rank():
                link(dve.tensor_scalar(cand[:, :], cand[:, :], -0.5, None, ALU.add))
                link(dve.tensor_scalar(r3[:, :], hi[:, :], 0.0, None, ALU.is_gt))
                link(dve.scalar_tensor_tensor(above[:, :], lo[:, :], cand[:, 0:1], r3[:, :], ALU.is_gt, ALU.mult))
                link(dve.scalar_tensor_tensor(equal[:, :], lo[:, :], cand[:, 0:1], r3[:, :], ALU.is_equal, ALU.mult))
                link(dve.memset(ones[:, :], 1.0))
                link(dve.tensor_tensor_scan(r1[:, :], ones[:, :], above[:, :], 0.0, ALU.mult, ALU.add))
                link(dve.tensor_tensor_scan(r2[:, :], ones[:, :], equal[:, :], 0.0, ALU.mult, ALU.add))
                link(dve.tensor_copy(totals[:, 0:1], r1[:, CHUNK_TOK - 1:CHUNK_TOK]))
                dve.tensor_copy(totals[:, 1:2], r2[:, CHUNK_TOK - 1:CHUNK_TOK]).then_inc(totals_ready, 1)

            def place():
                dve.wait_ge(offs_ready, 1)
                base = const[:, C_BASE:C_BASE + 1]
                link(dve.tensor_copy(offs[:, :], small[:, 0:4]))
                link(dve.scalar_tensor_tensor(r1[:, :], r1[:, :], offs[:, 0:1], above[:, :], ALU.add, ALU.subtract))
                link(dve.scalar_tensor_tensor(r2[:, :], r2[:, :], offs[:, 1:2], equal[:, :], ALU.add, ALU.subtract))
                link(dve.tensor_scalar(r2[:, :], r2[:, :], offs[:, 2:3], None, ALU.add))
                link(dve.scalar_tensor_tensor(r3[:, :], r2[:, :], float(CAP), equal[:, :], ALU.is_lt, ALU.mult))
                link(dve.scalar_tensor_tensor(r2[:, :], r2[:, :], base, r3[:, :], ALU.add, ALU.mult))
                link(dve.scalar_tensor_tensor(r1[:, :], r1[:, :], base, above[:, :], ALU.add, ALU.mult))
                dve.tensor_tensor(r1[:, :], r1[:, :], r2[:, :], ALU.add).then_inc(slots_ready, 1)

            def address():
                dve.wait_ge(slots_turned, 1)
                for s in range(2):
                    link(dve.tensor_copy(slot_tok[:, :, :].rearrange("p (c s) e -> p s e c", s=2)[:, s],
                                         wide[:, s * P:(s + 1) * P].rearrange("p (e c) -> p e c", e=E)))
                for k, onehot in enumerate((onehot1, onehot2)):
                    dummy = const[:, C_DUMMY + k * NT:C_DUMMY + (k + 1) * NT]
                    link(dve.tensor_tensor(work[:, :, :], slot_tok[:, :, :], onehot[:, :, :], ALU.mult))
                    link(dve.tensor_reduce(col[:, :], work[:, :, :], AX.X, ALU.add))
                    link(dve.tensor_scalar(col2[:, :], col[:, :], 0.0, None, ALU.is_gt))
                    link(dve.tensor_tensor(route["weight"][k][:, :], chosen_logit[k][:, :], col2[:, :], ALU.mult))
                    link(dve.tensor_scalar(route["fetch"][k][:, :], col[:, :], -1.0, 0.0, ALU.add, ALU.max))
                    link(dve.scalar_tensor_tensor(col[:, :], col[:, :], -1.0, dummy, ALU.add, ALU.subtract))
                    link(dve.tensor_tensor(col[:, :], col[:, :], col2[:, :], ALU.mult))
                    dve.tensor_tensor(route["send"][k][:, :], col[:, :], dummy, ALU.add).then_inc(idx_ready, 1)
                    dve.wait_ge(idx_ready, k + 1)

            norm.on_vector(dve, x_tok)
            dve.wait_ge(gate_in, 32)
            dve.wait_ge(const_in, 16)
            choose()
            order_keys()
            for blk in range(BLOCKS):
                for u in range(UB):
                    unit(UB * blk + u)
                    if u == 1 and blk > 0:
                        down(blk - 1)
                    if (blk, u) == KEYS_AT:
                        dve.wait_ge(keys_turned, 1)
                        link(dve.tensor_copy(hi[:, :], wide[:, 0:CHUNK_TOK]))
                        link(dve.tensor_copy(lo[:, :], wide[:, CHUNK_TOK:2 * CHUNK_TOK]))
                    if blk in (1, 2):
                        if u == 0:
                            start_search()
                        for _ in range(KEY_BITS // UB):
                            search((hi, lo)[blk - 1])
                        if u == UB - 1 and blk == 1:
                            lower_keys()
                        if u == UB - 1 and blk == 2:
                            rank()
                    if (blk, u) == OFFS_AT:
                        place()
                    if (blk, u) == TURN_AT:
                        address()
            down(BLOCKS - 1)


def run_experts(nc, a, keep, slots_in_dram, slots_out_dram):
    with ExitStack() as scope:
        m = Memory(nc, scope)
        ident = keep["ident"]
        w1, w3 = ([m.sb(f"{n}_{i}", [P, DC, F]) for i in range(2)] for n in ("ew1", "ew3"))
        w2 = [m.sb(f"ew2_{i}", [P, FC, D]) for i in range(2)]
        rows = [m.sb(f"slot_rows{i}", [P, CAP_TILES, D]) for i in range(2)]
        rowsT = [m.sb(f"slot_rowsT{i}", [P, DC, CAP]) for i in range(2)]
        silu = [m.sb(f"esilu{i}", [P, CAP]) for i in range(2)]
        hidden = [m.sb(f"ehidden{i}", [P, FC, CAP]) for i in range(2)]
        y_sb = [m.sb(f"y_sb{i}", [P, CAP_TILES, D]) for i in range(2)]
        gu = [m.ps(f"egu{i}", [P, 2, BANK]) for i in range(2)]
        turn = m.ps("eturn", [P, DC, BANK])
        y_bank = [m.ps(f"ey_bank{i}", [P, BANK]) for i in range(2)]

        w_in = [m.sem(f"expert_w_in{i}") for i in range(2)]
        rows_in = [m.sem(f"rows_in{i}") for i in range(2)]
        turned, rowsT_ready = m.sem("rows_turned"), m.sem("rowsT_ready")
        gu_ready, silu_done = m.sem("egu_ready"), m.sem("esilu_done")
        h_done = m.sem("eh_done")
        y_ready, y_copied = m.sem("ey_ready"), m.sem("ey_copied")
        y_out = m.sem("y_out")
        TAIL_CAP = CAP - (CAP_TILES - 1) * P
        full = CAP_TILES - 1
        sizes = [P] * full + [TAIL_CAP]

        block = scope.enter_context(nc.Block())

        def expert_slots(dram, e, t):
            return dram[bass.ds(e * CAP + t * P, sizes[t]), :]

        @block.sync
        def _(sp):
            def load(e, i):
                sp.dma_start(w1[i][:, :, :], a["ew1"][bass.ds(e, 1)].rearrange("o (c p) f -> p (o c) f", p=P)).then_inc(w_in[i], 16)
                sp.dma_start(w3[i][:, :, :], a["ew3"][bass.ds(e, 1)].rearrange("o (c p) f -> p (o c) f", p=P)).then_inc(w_in[i], 16)
                sp.dma_start(w2[i][:, :, :], a["ew2"][bass.ds(e, 1)].rearrange("o (c p) f -> p (o c) f", p=P)).then_inc(w_in[i], 16)

            def load_rows(e, i):
                for t in range(CAP_TILES):
                    sp.dma_start(rows[i][0:sizes[t], t, :], expert_slots(slots_in_dram, e, t)).then_inc(rows_in[i], 16)

            for i in range(2):
                load(i, i)
                load_rows(i, i)
            with sp.Fori(0, E // 2 - 1) as r:
                for i in range(2):
                    e = 2 * r + i
                    sp.wait_ge(y_ready, CAP_TILES * (e + 1))
                    load(e + 2, i)
                    load_rows(e + 2, i)

        @block.tensor
        def _(pe):
            def turn_rows(e, i, r):
                pe.wait_ge(rows_in[i], 16 * CAP_TILES * (r + 1))
                if not isinstance(e, int) or e > 0:
                    pe.wait_ge(rowsT_ready, DC * e)
                for c in range(DC):
                    for t, n in enumerate(sizes):
                        last = pe.transpose(turn[:, c, t * P:t * P + n], rows[i][0:n, t, c * P:(c + 1) * P],
                                            ident[0:n, 0:n])
                    last.then_inc(turned, 1)

            def up(e, i, r):
                pe.wait_ge(rowsT_ready, DC * (e + 1))
                pe.wait_ge(w_in[i], 48 * (r + 1))
                for f in range(FC):
                    pe.wait_ge(h_done, FC * e + f + 1)
                    for j, w in enumerate((w1, w3)):
                        for c in range(DC):
                            last = pe.matmul(gu[f % 2][:, j, 0:CAP], w[i][:, c, f * P:(f + 1) * P], rowsT[i][:, c, :],
                                             start=(c == 0), stop=(c == DC - 1))
                    last.then_inc(gu_ready, 1)

            def down(e, i):
                pe.wait_ge(h_done, FC * (e + 1) + 2)
                for t, n in enumerate(sizes):
                    pe.wait_ge(y_copied, CAP_TILES * e + t + 1)
                    for f in range(FC):
                        last = pe.matmul(y_bank[(CAP_TILES * i + t) % 2][0:n, 0:D], hidden[i][:, f, t * P:t * P + n],
                                         w2[i][:, f, :], start=(f == 0), stop=(f == FC - 1))
                    last.then_inc(y_ready, 1)

            turn_rows(0, 0, 0)
            with pe.Fori(0, E // 2 - 1) as r:
                for i in range(2):
                    e = 2 * r + i
                    up(e, i, r)
                    turn_rows(e + 1, 1 - i, r + i)
                    down(e, i)
            r = E // 2 - 1
            up(E - 2, 0, r)
            turn_rows(E - 1, 1, r)
            down(E - 2, 0)
            up(E - 1, 1, r)
            down(E - 1, 1)

        @block.scalar
        def _(act):
            act.sem_inc(y_copied, 2)

            def copy_turned(e, i):
                for c in range(DC):
                    act.wait_ge(turned, DC * e + c + 1)
                    act.activation(rowsT[i][:, c, :], turn[:, c, 0:CAP], ACT.Copy).then_inc(rowsT_ready, 1)

            def activate(e, i):
                for f in range(FC):
                    act.wait_ge(gu_ready, FC * e + f + 1)
                    act.wait_ge(h_done, FC * e + f + 1)
                    act.activation(silu[f % 2][:, :], gu[f % 2][:, 0, 0:CAP], ACT.Silu).then_inc(silu_done, 1)

            def copy_out(e, i):
                for t, n in enumerate(sizes):
                    act.wait_ge(y_ready, CAP_TILES * e + t + 1)
                    act.activation(y_sb[i][0:n, t, :], y_bank[(CAP_TILES * i + t) % 2][0:n, 0:D], ACT.Copy
                                   ).then_inc(y_copied, 1)
                act.wait_ge(y_copied, CAP_TILES * (e + 1) + 2)
                for t, n in enumerate(sizes):
                    act.dma_start(expert_slots(slots_out_dram, e, t), y_sb[i][0:n, t, :]).then_inc(y_out, 16)

            copy_turned(0, 0)
            with act.Fori(0, E // 2 - 1) as r:
                for i in range(2):
                    e = 2 * r + i
                    activate(e, i)
                    copy_turned(e + 1, 1 - i)
                    copy_out(e, i)
                    act.wait_ge(y_out, 16 * CAP_TILES * (e + 1))
            activate(E - 2, 0)
            copy_turned(E - 1, 1)
            copy_out(E - 2, 0)
            activate(E - 1, 1)
            copy_out(E - 1, 1)
            act.wait_ge(y_out, 16 * CAP_TILES * E)

        @block.vector
        def _(dve):
            dve.sem_inc(h_done, 2)

            def gate(e, i):
                for f in range(FC):
                    dve.wait_ge(silu_done, FC * e + f + 1)
                    dve.tensor_tensor(hidden[i][:, f, :], silu[f % 2][:, :], gu[f % 2][:, 1, 0:CAP], ALU.mult
                                      ).then_inc(h_done, 1)

            with dve.Fori(0, E // 2) as r:
                for i in range(2):
                    gate(2 * r + i, i)



QK = 64
ZQ = 256
ZB = N // ZQ
ZT = ZQ // P
HID = 1024
HC = HID // P
RMS_EPS, QUANT_EPS = 1e-6, 1e-5
ROUND = 12582912.0
LEVELS = 127.0


def combine_and_attend(nc, a, keep, x_tok, slots_out_dram, route):
    with ExitStack() as scope:
        m = Memory(nc, scope)
        ident = keep["ident"]
        got = [m.sb(f"got{k}", [P, NT, D]) for k in range(TOP)]
        ctxT = m.sb("ctxT_1", [P, DC, S])
        wq, wk = m.sb("wq_1", [P, DC, QK]), m.sb("wk_1", [P, DC, QK])
        wv = m.sb("wv_1", [P, DC, D])
        bq, bk, bv = m.sb("bq_1", [QK, 1]), m.sb("bk_1", [QK, 1]), m.sb("bv_1", [P, D])
        qT, kT = m.sb("qT_1", [P, N]), m.sb("kT_1", [P, S])
        v = m.sb("v_1", [P, KT, D])
        norm = Norm(m, "ln3", got[0])
        tokT = got[1][:, :, :].rearrange("p t d -> p (t d)").rearrange("p (c n) -> p c n", c=DC)
        z = [m.sb(f"z{i}", [P, KT, ZQ]) for i in range(2)]
        bank = [m.ps(f"l1_bank{i}", [P, BANK]) for i in range(4)]
        z_bank = [m.ps(f"z_bank{i}", [P, BANK]) for i in range(2)]
        o_bank = [m.ps(f"o_bank{i}", [P, BANK]) for i in range(2)]

        fetched = [m.sem(f"fetched{k}") for k in range(TOP)]
        added, padded = m.sem("expert_added"), m.sem("padded")
        kin, vin, qin = m.sem("k1_in"), m.sem("v1_in"), m.sem("q1_in")
        bank_full = m.sem("l1_bank_full")
        by_act, by_dve = m.sem("l1_bank_free_act"), m.sem("l1_bank_free_dve")
        z_ready, z_done = m.sem("z_ready"), m.sem("z_done")
        o_ready, o_done = m.sem("o_ready"), m.sem("o_done")

        FILLS_K = -(-S // BANK)
        FILLS_V = KT
        FILLS_T = DC * NT // 4
        FILLS_Q = N // BANK

        block = scope.enter_context(nc.Block())

        @block.gpsimd
        def _(pool):
            pool.memset(qT[QK:P, :], 0.0).then_inc(padded, 1)
            pool.wait_ge(padded, 1)
            pool.memset(kT[QK:P, :], 0.0).then_inc(padded, 1)
            for k in range(TOP):
                for t in range(NT):
                    pool.indirect_dma_start(
                        out=got[k][:, t, :], out_offset=None, in_=slots_out_dram[:, :],
                        in_offset=bass.IndirectOffsetOnAxis(ap=route["fetch"][k][:, t:t + 1], axis=0)
                    ).then_inc(fetched[k], 16)

        @block.sync
        def _(sp):
            sp.dma_start(wk[:, :, :], a["wk1T"].rearrange("(c p) n -> p c n", p=P)).then_inc(kin, 16)
            sp.dma_start(bk[:, :], a["bk1"].rearrange("(p o) -> p o", o=1), allow_slow_non_contiguous=True).then_inc(kin, 16)
            sp.dma_start(ctxT[:, :, :], a["ctxT"].rearrange("(c p) n -> p c n", p=P)).then_inc(kin, 16)
            sp.dma_start(wv[:, :, :], a["wv1T"].rearrange("(c p) n -> p c n", p=P)).then_inc(vin, 16)
            sp.dma_start(bv[:, :], a["bv1"].partition_broadcast(P)).then_inc(vin, 16)
            sp.dma_start(wq[:, :, :], a["wq1T"].rearrange("(c p) n -> p c n", p=P)).then_inc(qin, 16)
            sp.dma_start(bq[:, :], a["bq1"].rearrange("(p o) -> p o", o=1), allow_slow_non_contiguous=True).then_inc(qin, 16)

        @block.tensor
        def _(pe):
            fills = 0

            def take_bank():
                if fills >= 4:
                    seen = fills - 3
                    pe.wait_ge(by_act, min(seen, FILLS_K) + max(0, seen - FILLS_K - FILLS_V))
                    if seen > FILLS_K:
                        pe.wait_ge(by_dve, min(seen - FILLS_K, FILLS_V))
                return bank[fills % 4]

            pe.wait_ge(kin, 48)
            for n0 in range(0, S, BANK):
                n1 = min(S, n0 + BANK)
                b = take_bank()
                for c in range(DC):
                    last = pe.matmul(b[0:QK, 0:n1 - n0], wk[:, c, :], ctxT[:, c, n0:n1], start=(c == 0), stop=(c == DC - 1))
                last.then_inc(bank_full, 1)
                fills += 1
            pe.wait_ge(vin, 32)
            for t in range(KT):
                b = take_bank()
                for c in range(DC):
                    last = pe.matmul(b[0:key_rows(t), 0:D], ctxT[:, c, t * P:t * P + key_rows(t)], wv[:, c, :],
                                     start=(c == 0), stop=(c == DC - 1))
                last.then_inc(bank_full, 1)
                fills += 1
            for g in range(NT // 4):
                pe.wait_ge(norm.norm_done, 4 * (g + 1))
                for c in range(DC):
                    b = take_bank()
                    for j in range(4):
                        last = pe.transpose(b[:, j * P:(j + 1) * P], norm.normed[:, 4 * g + j, c * P:(c + 1) * P], ident[:, :])
                    last.then_inc(bank_full, 1)
                    fills += 1
            pe.wait_ge(qin, 32)
            pe.wait_ge(by_act, FILLS_K + FILLS_T)
            for n0 in range(0, N, BANK):
                b = take_bank()
                for c in range(DC):
                    last = pe.matmul(b[0:QK, :], wq[:, c, :], tokT[:, c, n0:n0 + BANK], start=(c == 0), stop=(c == DC - 1))
                last.then_inc(bank_full, 1)
                fills += 1
            pe.wait_ge(by_act, FILLS_K + FILLS_T + FILLS_Q)
            pe.wait_ge(padded, 2)

            def score(b, i, t):
                rows = key_rows(t)
                pe.wait_ge(z_done, KT * b + t + 1)
                pe.matmul(z_bank[(KT * i + t) % 2][0:rows, 0:ZQ], kT[:, t * P:t * P + rows], qT[:, bass.ds(b * ZQ, ZQ)],
                          start=True, stop=True).then_inc(z_ready, 1)

            def weigh(b, i, k):
                tt, t = divmod(k, KT)
                rows = key_rows(t)
                if t == 0:
                    pe.wait_ge(o_done, ZT * b + tt + 1)
                if tt == 0:
                    pe.wait_ge(z_done, KT * b + t + 3)
                last = pe.matmul(o_bank[tt][:, 0:D], z[i][0:rows, t, tt * P:(tt + 1) * P], v[0:rows, t, :],
                                 start=(t == 0), stop=(t == KT - 1))
                if t == KT - 1:
                    last.then_inc(o_ready, 1)

            def block_step(b, i):
                for t in range(KT):
                    score(b, i, t)
                    for j in range(ZT):
                        weigh(b - 1, 1 - i, ZT * t + j)

            for t in range(KT):
                score(0, 0, t)
            with pe.Fori(0, ZB // 2 - 1) as r:
                block_step(2 * r + 1, 1)
                block_step(2 * r + 2, 0)
            block_step(ZB - 1, 1)
            for k in range(ZT * KT):
                weigh(ZB - 1, 1, k)

        @block.scalar
        def _(act):
            fills = 0
            act.sem_inc(z_done, 2)
            act.wait_ge(kin, 48)
            for n0 in range(0, S, BANK):
                n1 = min(S, n0 + BANK)
                act.wait_ge(bank_full, fills + 1)
                act.activation(kT[0:QK, n0:n1], bank[fills % 4][0:QK, 0:n1 - n0], ACT.Identity, bias=bk[:, 0:1]).then_inc(by_act, 1)
                fills += 1
            fills += FILLS_V
            norm.on_scalar(act)
            for g in range(NT // 4):
                for c in range(DC):
                    act.wait_ge(bank_full, fills + 1)
                    act.activation(tokT[:, c, g * BANK:(g + 1) * BANK], bank[fills % 4][:, :], ACT.Copy).then_inc(by_act, 1)
                    fills += 1
            act.wait_ge(qin, 32)
            for n0 in range(0, N, BANK):
                act.wait_ge(bank_full, fills + 1)
                act.activation(qT[0:QK, n0:n0 + BANK], bank[fills % 4][0:QK, :], ACT.Identity, bias=bq[:, 0:1]).then_inc(by_act, 1)
                fills += 1

            def squash(b, i):
                for t in range(KT):
                    rows = key_rows(t)
                    act.wait_ge(z_ready, KT * b + t + 1)
                    act.activation(z[i][0:rows, t, :], z_bank[(KT * i + t) % 2][0:rows, 0:ZQ], ACT.Sigmoid, scale=QK ** -0.5
                                   ).then_inc(z_done, 1)

            squash(0, 0)
            squash(1, 1)
            with act.Fori(0, ZB // 2 - 1) as r:
                act.wait_ge(o_ready, ZT * (2 * r + 1))
                squash(2 * r + 2, 0)
                act.wait_ge(o_ready, ZT * (2 * r + 2))
                squash(2 * r + 3, 1)

        @block.vector
        def _(dve):
            dve.sem_inc(o_done, 2)
            dve.wait_ge(vin, 32)
            for t in range(KT):
                rows, f = key_rows(t), FILLS_K + t
                dve.wait_ge(bank_full, f + 1)
                dve.tensor_tensor(v[0:rows, t, :], bank[f % 4][0:rows, 0:D], bv[0:rows, :], ALU.add).then_inc(by_dve, 1)
            for k in range(TOP):
                dve.wait_ge(fetched[k], 16 * NT)
                for t in range(NT):
                    if k:
                        dve.wait_ge(added, t + 1)
                    dve.scalar_tensor_tensor(x_tok[:, t, :], got[k][:, t, :], route["weight"][k][:, t:t + 1],
                                             x_tok[:, t, :], ALU.mult, ALU.add).then_inc(added, 1)
            dve.wait_ge(added, TOP * NT)
            norm.on_vector(dve, x_tok)

            def add_out(b):
                for tt in range(ZT):
                    dve.wait_ge(o_ready, ZT * b + tt + 1)
                    xv = x_tok[:, bass.ds(b * ZT + tt, 1), :].rearrange("p o d -> p (o d)")
                    dve.tensor_tensor(xv, xv, o_bank[tt][:, 0:D], ALU.add).then_inc(o_done, 1)

            with dve.Fori(0, ZB) as b:
                add_out(b)


def feed_forward(nc, a, keep, x_tok, out):
    with ExitStack() as scope:
        m = Memory(nc, scope)
        ident_bf = keep["ident_bf"]
        w1, w2 = m.sb("ff_w1", [P, DC, HID]), m.sb("ff_w2", [P, HC, D])
        t1, t2 = m.sb("ternary1", [P, DC, HID], BF16), m.sb("ternary2", [P, HC, D], BF16)
        b1, b2 = m.sb("b1_rows", [P, HID]), m.sb("b2_rows", [P, D])
        ones = m.sb("ones_sq", [P, P])
        w_abs, w_mean, w_scale = m.sb("w_abs", [P, 2]), m.sb("w_mean", [P, 2]), m.sb("w_scale", [P, 2])
        q1 = m.sb("q1", [P, NT, D], BF16)
        q1T = m.sb("q1T", [P, DC, N], BF16)
        h = m.sb("h", [P, NT, HID])
        norm = Norm(m, "ln4", h[:, 0:NT * D // HID, :].rearrange("p t n -> p (t n)").rearrange("p (t d) -> p t d", t=NT))
        squares = m.sb("squares", [P, HID])
        q2f = [m.sb(f"q2f{i}", [P, HID]) for i in range(2)]
        q2 = [m.sb(f"q2_{i}", [P, HID], BF16) for i in range(2)]
        q2T = [m.sb(f"q2T_{i}", [P, HC, P], BF16) for i in range(2)]
        ssq, big, rstd, factor, back = ([m.sb(f"{n}{i}", [P, NT]) for i in range(2)] for n in
                                        ("ssq", "big", "rms", "factor", "back"))
        eps = m.sb("rms_eps", [P, 1])
        pre = [m.ps(f"pre{i}", [P, 2, BANK]) for i in range(2)]
        turn = [m.ps(f"fturn{i}", [P, 2 * BANK], BF16) for i in range(2)]
        y_bank = [m.ps(f"fy_bank{i}", [P, BANK]) for i in range(2)]

        w_in, b_in = m.sem("ff_w_in"), m.sem("ff_b_in")
        chain = m.sem("ff_chain")
        w_counted, w_summed = m.sem("w_counted"), m.sem("w_summed")
        squared, rooted = m.sem("squared"), m.sem("rooted")
        root_in = m.sem("root_in")
        quantized, tern_ready = m.sem("quantized"), m.sem("tern_ready")
        t_full, t_free = m.sem("ff_t_full"), m.sem("ff_t_free")
        b2_added = m.sem("b2_added")
        pre_ready, pre_read = m.sem("pre_ready"), m.sem("pre_read")
        gelu_done, h_seen = m.sem("gelu_done"), m.sem("h_seen")
        rounded, q2_ready = m.sem("rounded"), m.sem("q2_ready")
        turned2, q2T_ready = m.sem("turned2"), m.sem("q2T_ready")
        y_ready, y_done = m.sem("fy_ready"), m.sem("fy_done")
        stored = m.sem("stored")

        GT = 4

        block = scope.enter_context(nc.Block())

        @block.sync
        def _(sp):
            sp.dma_start(w1[:, :, :], a["w1T"].rearrange("(c p) n -> p c n", p=P)).then_inc(w_in, 16)
            sp.dma_start(w2[:, :, :], a["w2T"].rearrange("(c p) n -> p c n", p=P)).then_inc(w_in, 16)
            sp.dma_start(b1[:, :], a["b1"].partition_broadcast(P)).then_inc(b_in, 16)
            sp.dma_start(b2[:, :], a["b2"].partition_broadcast(P)).then_inc(b_in, 16)
            for g in range(NT // GT):
                sp.wait_ge(y_done, GT * (g + 1) + 2)
                sp.dma_start(out.rearrange("b (t p) d -> p (b t) d", p=P)[:, GT * g:GT * (g + 1), :],
                             x_tok[:, GT * g:GT * (g + 1), :]).then_inc(stored, 16)
            sp.wait_ge(stored, 16 * (NT // GT))

        @block.gpsimd
        def _(pool):
            pool.wait_ge(b_in, 32)
            pool.wait_ge(norm.norm_done, NT)
            for t in range(NT):
                if t:
                    pool.wait_ge(b2_added, t)
                pool.tensor_tensor(x_tok[:, t, :], x_tok[:, t, :], b2[:, :], ALU.add).then_inc(b2_added, 1)

        @block.tensor
        def _(pe):
            pe.wait_ge(w_counted, 3)
            pe.matmul(y_bank[0][:, 0:2], ones[:, :], w_abs[:, :], start=True, stop=True).then_inc(w_summed, 1)
            for f in range(DC * NT // GT):
                g, c = divmod(f, DC)
                pe.wait_ge(quantized, GT * (g + 1))
                if f >= 2:
                    pe.wait_ge(t_free, f - 1)
                for j in range(GT):
                    last = pe.transpose(turn[f % 2][:, j * P:(j + 1) * P], q1[:, GT * g + j, c * P:(c + 1) * P],
                                        ident_bf[:, :])
                last.then_inc(t_full, 1)
            pe.wait_ge(t_free, DC * NT // GT)
            pe.wait_ge(tern_ready, 2)
            with pe.Fori(0, NT // 2) as r:
                for i in range(2):
                    pe.wait_ge(pre_read, 2 * r + i + 1)
                    for half in range(2):
                        for c in range(DC):
                            last = pe.matmul(pre[i][:, half, :],
                                             q1T[:, c, bass.ds(r * (2 * P) + i * P, P)],
                                             t1[:, c, half * BANK:(half + 1) * BANK], start=(c == 0), stop=(c == DC - 1))
                    last.then_inc(pre_ready, 1)

            def turn_hidden(t, i):
                pe.wait_ge(q2_ready, t + 1)
                if not isinstance(t, int) or t >= 2:
                    pe.wait_ge(q2T_ready, t - 1)
                for c in range(HC):
                    last = pe.transpose(turn[i][:, c * P:(c + 1) * P], q2[i][:, c * P:(c + 1) * P], ident_bf[:, :])
                last.then_inc(turned2, 1)

            def down(t, i):
                pe.wait_ge(q2T_ready, t + 1)
                pe.wait_ge(y_done, t + 1)
                for c in range(HC):
                    last = pe.matmul(y_bank[i][:, 0:D], q2T[i][:, c, :], t2[:, c, :], start=(c == 0), stop=(c == HC - 1))
                last.then_inc(y_ready, 1)

            turn_hidden(0, 0)
            turn_hidden(1, 1)
            with pe.Fori(0, NT // 2 - 1) as r:
                for i in range(2):
                    down(2 * r + i, i)
                    turn_hidden(2 * r + i + 2, i)
            down(NT - 2, 0)
            down(NT - 1, 1)

        @block.scalar
        def _(act):
            norm.on_scalar(act)
            for t in range(NT):
                act.wait_ge(norm.norm_done, t + 1)
                if t:
                    act.wait_ge(squared, t)
                act.activation(squares[:, 0:D], norm.normed[:, t, :], ACT.Square, accum_out=ssq[0][:, t:t + 1]).then_inc(squared, 1)
            act.wait_ge(squared, NT)
            act.wait_ge(root_in, 1)
            act.activation(rstd[0][:, :], ssq[0][:, :], ACT.Sqrt, bias=eps[:, 0:1], scale=1.0 / D).then_inc(rooted, 1)
            for f in range(DC * NT // GT):
                g, c = divmod(f, DC)
                act.wait_ge(t_full, f + 1)
                act.activation(q1T[:, c, g * BANK:(g + 1) * BANK], turn[f % 2][:, 0:BANK], ACT.Copy).then_inc(t_free, 1)
            with act.Fori(0, NT) as t:
                act.wait_ge(pre_read, t + 3)
                hv = h[:, bass.ds(t, 1), :].rearrange("p o d -> p (o d)")
                act.activation(hv, hv, ACT.Gelu).then_inc(gelu_done, 1)
                act.wait_ge(gelu_done, t + 1)
                act.wait_ge(squared, t + NT)
                act.activation(squares[:, :], hv, ACT.Square, accum_out=ssq[1][:, bass.ds(t, 1)]).then_inc(squared, 1)
            act.wait_ge(squared, 2 * NT)
            act.activation(rstd[1][:, :], ssq[1][:, :], ACT.Sqrt, bias=eps[:, 0:1], scale=1.0 / HID).then_inc(rooted, 1)

            def to_bf16(t, i):
                act.wait_ge(rounded, t + 1)
                act.activation(q2[i][:, :], q2f[i][:, :], ACT.Copy, bias=-ROUND).then_inc(q2_ready, 1)

            def copy_turned(t, i):
                act.wait_ge(turned2, t + 1)
                act.activation(q2T[i][:, :, :].rearrange("p c n -> p (c n)"), turn[i][:, :], ACT.Copy).then_inc(q2T_ready, 1)

            to_bf16(0, 0)
            to_bf16(1, 1)
            copy_turned(0, 0)
            copy_turned(1, 1)
            with act.Fori(0, NT // 2 - 1) as r:
                for i in range(2):
                    to_bf16(2 * r + i + 2, i)
                    act.wait_ge(y_ready, 2 * r + i + 1)
                    copy_turned(2 * r + i + 2, i)

        @block.vector
        def _(dve):
            made = 0

            def link(ins):
                nonlocal made
                made += 1
                ins.then_inc(chain, 1)
                dve.wait_ge(chain, made)

            def scales(i):
                link(dve.reciprocal(rstd[i][:, :], rstd[i][:, :]))
                link(dve.tensor_tensor(back[i][:, :], big[i][:, :], rstd[i][:, :], ALU.mult))
                link(dve.tensor_scalar(back[i][:, :], back[i][:, :], QUANT_EPS, 1.0 / LEVELS, ALU.max, ALU.mult))
                link(dve.reciprocal(factor[i][:, :], back[i][:, :]))
                link(dve.tensor_tensor(factor[i][:, :], factor[i][:, :], rstd[i][:, :], ALU.mult))
                link(dve.tensor_scalar(back[i][:, :], back[i][:, :], w_mean[:, i:i + 1], None, ALU.mult))

            link(dve.memset(eps[:, :], RMS_EPS))
            norm.on_vector(dve, x_tok)
            for t in range(NT):
                dve.wait_ge(norm.norm_done, t + 1)
                dve.tensor_reduce(big[0][:, t:t + 1], norm.normed[:, t, :], AX.X, ALU.max, apply_absolute_value=True
                                  ).then_inc(root_in, 1)
            dve.memset(ones[:, :], 1.0).then_inc(w_counted, 1)
            dve.wait_ge(w_in, 32)
            for i, w in enumerate((w1, w2)):
                dve.tensor_reduce(w_abs[:, i:i + 1], w[:, :, :].rearrange("p c n -> p (c n)"), AX.X, ALU.add,
                                  apply_absolute_value=True).then_inc(w_counted, 1)
            dve.wait_ge(w_summed, 1)
            link(dve.tensor_scalar(w_mean[:, :], y_bank[0][:, 0:2], 1.0 / (D * HID), QUANT_EPS, ALU.mult, ALU.max))
            link(dve.reciprocal(w_scale[:, :], w_mean[:, :]))
            dve.wait_ge(rooted, 1)
            dve.wait_ge(root_in, NT)
            scales(0)
            for t in range(NT):
                if t >= 2:
                    dve.wait_ge(quantized, t - 1)
                link(dve.tensor_scalar(q2f[t % 2][:, 0:D], norm.normed[:, t, :], factor[0][:, t:t + 1], ROUND, ALU.mult, ALU.add))
                link(dve.tensor_scalar(q2f[t % 2][:, 0:D], q2f[t % 2][:, 0:D], ROUND + LEVELS, ROUND - LEVELS - 1,
                                       ALU.min, ALU.max))
                dve.tensor_scalar(q1[:, t, :], q2f[t % 2][:, 0:D], -ROUND, None, ALU.add).then_inc(quantized, 1)
            for i, (w, tern) in enumerate(((w1, t1), (w2, t2))):
                flat = w[:, :, :].rearrange("p c n -> p (c n)")
                link(dve.tensor_scalar(flat, flat, w_scale[:, i:i + 1], ROUND, ALU.mult, ALU.add))
                link(dve.tensor_scalar(flat, flat, ROUND + 1.0, ROUND - 1.0, ALU.min, ALU.max))
                dve.tensor_scalar(tern[:, :, :].rearrange("p c n -> p (c n)"), flat, -ROUND, None, ALU.add
                                  ).then_inc(tern_ready, 1)
            dve.wait_ge(b_in, 32)
            dve.sem_inc(pre_read, 2)
            dve.sem_inc(y_done, 2)

            def bias(t, i):
                dve.wait_ge(pre_ready, t + 1)
                dve.scalar_tensor_tensor(h[:, bass.ds(t, 1), :].rearrange("p o (a n) -> p (o a) n", a=2), pre[i][:, :, :],
                                         back[0][:, bass.ds(t, 1)], b1[:, :].rearrange("p (a n) -> p a n", a=2),
                                         ALU.mult, ALU.add).then_inc(pre_read, 1)

            def largest(t):
                dve.wait_ge(gelu_done, t + 1)
                dve.tensor_reduce(big[1][:, bass.ds(t, 1)], h[:, bass.ds(t, 1), :].rearrange("p o d -> p (o d)"), AX.X,
                                  ALU.max, apply_absolute_value=True).then_inc(h_seen, 1)

            dve.wait_ge(quantized, NT)
            dve.wait_ge(squared, NT)
            bias(0, 0)
            bias(1, 1)
            with dve.Fori(0, NT // 2 - 1) as r:
                for i in range(2):
                    largest(2 * r + i)
                    bias(2 * r + i + 2, i)
            largest(NT - 2)
            largest(NT - 1)
            dve.wait_ge(rooted, 2)
            dve.wait_ge(h_seen, NT)
            scales(1)

            def quantize(t, i):
                if not isinstance(t, int) or t >= 2:
                    dve.wait_ge(q2_ready, t - 1)
                hv = h[:, bass.ds(t, 1), :].rearrange("p o d -> p (o d)")
                dve.tensor_scalar(hv, hv, factor[1][:, bass.ds(t, 1)], ROUND, ALU.mult, ALU.add).then_inc(h_seen, 1)
                dve.wait_ge(h_seen, t + NT + 1)
                dve.tensor_scalar(q2f[i][:, :], hv, ROUND + LEVELS, ROUND - LEVELS - 1, ALU.min, ALU.max
                                  ).then_inc(rounded, 1)

            def finish(t, i):
                dve.wait_ge(y_ready, t + 1)
                xv = x_tok[:, bass.ds(t, 1), :].rearrange("p o d -> p (o d)")
                dve.scalar_tensor_tensor(xv, y_bank[i][:, 0:D], back[1][:, bass.ds(t, 1)], xv, ALU.mult, ALU.add
                                         ).then_inc(y_done, 1)

            dve.wait_ge(b2_added, NT)
            for t in range(2):
                quantize(t, t)
            with dve.Fori(0, NT // 2 - 1) as r:
                for i in range(2):
                    quantize(2 * r + i + 2, i)
                    finish(2 * r + i, i)
            finish(NT - 2, 0)
            finish(NT - 1, 1)


def build(nc, a, out):
    q_parts_dram = nc.dram_tensor("q_parts", (3, D, N), BF16, kind="Internal").ap()
    k_parts_dram = nc.dram_tensor("k_parts", (3, D, S), BF16, kind="Internal").ap()
    with ExitStack() as scope:
        m = Memory(nc, scope)
        x_tok = m.sb("x_tok", [P, NT, D])
        ident, ident_bf = m.sb("ident", [P, P]), m.sb("ident_bf", [P, P], BF16)
        with ExitStack() as inner:
            mi = Memory(nc, inner)
            values = mi.sb("values", [P, GROUPS * KT * HG * HEAD_PE])
            keep = {
                "ident": ident, "ident_bf": ident_bf,
                "q_aug": mi.sb("q_aug", [P, RING, HG * BANK], BF16),
                "k_aug": mi.sb("k_aug", [P, H, S], BF16),
                "values_flat": values,
                "values": values[:, :].rearrange("p (g t h w) -> p g t h w", g=GROUPS, t=KT, h=HG),
            }
            project(nc, a, keep, x_tok, q_parts_dram, k_parts_dram)
            attend(nc, keep, x_tok, q_parts_dram)
        slots_in = nc.dram_tensor("slots_in", (SLOTS + TOP * N, D), F32, kind="Internal").ap()
        slots_out = nc.dram_tensor("slots_out", (SLOTS, D), F32, kind="Internal").ap()
        route = {
            "send": [m.sb(f"send{k}", [P, NT], U32) for k in range(TOP)],
            "fetch": [m.sb(f"fetch{k}", [P, NT], U32) for k in range(TOP)],
            "weight": [m.sb(f"weight{k}", [P, NT]) for k in range(TOP)],
        }
        keep = {"ident": ident, "ident_bf": ident_bf}
        with ExitStack() as inner:
            normed = Memory(nc, inner).sb("ln2_normed", [P, NT, D])
            route_and_share(nc, a, keep, x_tok, normed, slots_in, route)
        run_experts(nc, a, keep, slots_in, slots_out)
        combine_and_attend(nc, a, keep, x_tok, slots_out, route)
        feed_forward(nc, a, keep, x_tok, out)


def kernel(**inputs):
    import numpy as _np
    import concourse.bacc as _bacc
    from concourse import mybir as _mybir
    from concourse.bass_utils import run_bass_kernel_spmd as _run

    given = {k: _np.asarray(v) for k, v in inputs.items()}
    laid = {
        "x": given["x"],
        "ctxT": given["ctx_1024"][0].T,
        "mask": given["mask_BxS2_ik0"],
        "wqT": given["L0_xattn_Wq"].T,
        "wkT": given["L0_xattn_Wk"].T,
        "wvT": given["L0_xattn_Wv"].T,
        "bq": given["L0_xattn_bq"],
        "bk": given["L0_xattn_bk"],
        "bv": given["L0_xattn_bv"],
        "gate_w": given["L0_ffn_gate_w"],
        "gate_b": given["L0_ffn_gate_b"],
        "ew1": given["L0_ffn_ew1"],
        "ew3": given["L0_ffn_ew3"],
        "ew2": given["L0_ffn_ew2"],
        "sw1": given["L0_ffn_sw1"],
        "sw3": given["L0_ffn_sw3"],
        "sw2": given["L0_ffn_sw2"],
        "wq1T": given["L1_xattn_Wq"].T,
        "wk1T": given["L1_xattn_Wk"].T,
        "wv1T": given["L1_xattn_Wv"].T,
        "bq1": given["L1_xattn_bq"],
        "bk1": given["L1_xattn_bk"],
        "bv1": given["L1_xattn_bv"],
        "w1T": given["L1_ffn_w1"].T,
        "b1": given["L1_ffn_b1"],
        "w2T": given["L1_ffn_w2"].T,
        "b2": given["L1_ffn_b2"],
        "const": shape_constants(_np),
    }
    nc = _bacc.Bacc("TRN2", target_bir_lowering=False, num_devices=1)
    arrays, aps = {}, {}
    for name, a in laid.items():
        a = _np.ascontiguousarray(a)
        arrays[f"in_{name}"] = a
        aps[name] = nc.dram_tensor(f"in_{name}", a.shape, _mybir.dt.from_np(a.dtype), kind="ExternalInput").ap()
    out = nc.dram_tensor("out_x", (1, N, D), F32, kind="ExternalOutput").ap()
    build(nc, aps, out)
    r = _run(nc, [arrays], core_ids=[0])
    return r.results[0]["out_x"]
```

```python
from contextlib import ExitStack

import concourse.bass as bass
from concourse import mybir

F32 = mybir.dt.float32
BF16 = mybir.dt.bfloat16
I32 = mybir.dt.int32
U32 = mybir.dt.uint32
ALU = mybir.AluOpType
ACT = mybir.ActivationFunctionType
AX = mybir.AxisListType

P = 128
BANK = 512

N = 2048
D = 256
DC = D // P
NT = N // P
S = 1601
KT = -(-S // P)
TAIL = S - (KT - 1) * P
EPS_LN = 1e-5

H = 16
W = D // H
GROUPS = 4
HG = H // GROUPS
QB = N // BANK
STEPS = GROUPS * QB
QT = BANK // P
HEAD_PE = 32

THIRDS_K = (0, 1, 0, 2, 0, 1)
THIRDS_Q = (0, 0, 1, 0, 2, 1)
ROWS_PROD = W * len(THIRDS_K)
ROWS_MASKED = ROWS_PROD + 2
ROWS_ALL = ROWS_MASKED + 3
MASK_RAW = 10000.0 * W ** 0.5
SCORE_SCALE = W ** -0.5

WHOLE = S // BANK
REST = S - WHOLE * BANK
RING = 4
CHUNKS_QT = HG * WHOLE + 1
CHUNKS = QT * CHUNKS_QT
BANKS = 3
PLACES = KT * HG
LEAD = 24


def key_rows(t):
    return P if t < KT - 1 else TAIL


def sub(flat, start, count):
    return flat[:, bass.ds(start, count)]


class Memory:

    def __init__(self, nc, scope):
        self.nc, self.scope = nc, scope

    def sb(self, name, shape, dt=F32):
        return self.scope.enter_context(self.nc.sbuf_tensor(name, shape, dt))

    def ps(self, name, shape, dt=F32):
        return self.scope.enter_context(self.nc.psum_tensor(name, shape, dt))

    def sem(self, name):
        return self.scope.enter_context(self.nc.semaphore(name))


def make_identity(pool, ident, zeroed, made):
    pool.memset(ident[:, :], 0.0).then_inc(zeroed, 1)
    pool.wait_ge(zeroed, 1)
    pool.affine_select(out=ident[:, :], in_=ident[:, :], compare_op=ALU.not_equal, fill=1.0, base=0,
                       pattern=[[-1, P]], channel_multiplier=1).then_inc(made, 1)


def project(nc, a, keep, x_tok, q_parts_dram, k_parts_dram):
    with ExitStack() as scope:
        m = Memory(nc, scope)
        ctxT = m.sb("ctxT", [P, DC, S])
        wq, wk, wv = (m.sb(f"w{c}_0", [P, DC, D]) for c in "qkv")
        bq, bk = m.sb("bq_col", [P, DC]), m.sb("bk_col", [P, DC])
        bv = m.sb("bv_rows", [P, D])
        mask_i = m.sb("mask_int", [1, S], I32)
        mask_raw = mask_i[:, :].bitcast(F32)
        mask_hi = m.sb("mask_hi", [1, S], BF16)
        mask_lo = m.sb("mask_lo", [1, S], BF16)
        projT = m.sb("projT", [P, DC, N])
        normed = projT[:, :, :].rearrange("p c n -> p (c n)").rearrange("p (t d) -> p t d", t=NT)
        norm = Norm(m, "ln1", normed)
        normedT = m.sb("normedT", [P, DC, N])
        halves = normedT[:, :, :].rearrange("p c n -> p (c n)").bitcast(BF16).rearrange("p (i c n) -> p i c n", i=2, c=DC)
        third = [halves[:, 0], halves[:, 1], m.sb("third2", [P, DC, N], BF16)[:, :, :]]
        bank = [m.ps(f"proj_bank{i}", [P, BANK]) for i in range(4)]

        x_in = [m.sem(f"x_in{g}") for g in range(NORM_GROUPS)]
        ctx_in, mask_in = m.sem("ctx_in"), m.sem("mask_in")
        wq_in, wk_in, wv_in, b_in, bv_in = (m.sem(s) for s in ("wq_in", "wk_in", "wv_in", "b_in", "bv_in"))
        ident_zero, ident_made = m.sem("ident_zero"), m.sem("ident_made")
        bank_full, bank_free_act, bank_free_dve = m.sem("bank_full"), m.sem("bank_free_act"), m.sem("bank_free_dve")
        split, mask_split, q_out, k_out = m.sem("split"), m.sem("mask_split"), m.sem("q_out"), m.sem("k_out")
        steps, aug_set, aug_in, values_set = m.sem("own_steps"), m.sem("aug_set"), m.sem("aug_in"), m.sem("values_set")

        FILLS_T = DC * (NT // 4)
        FILLS_P = DC * QB
        FILLS_QK = 2 * FILLS_P
        FILLS_V = KT

        n_act = FILLS_T + FILLS_QK

        block = scope.enter_context(nc.Block())

        @block.sync
        def _(sp):
            for g in range(NORM_GROUPS):
                part = slice(NORM_GROUP * g, NORM_GROUP * (g + 1))
                sp.dma_start(x_tok[:, part, :], a["x"].rearrange("b (t p) d -> p (b t) d", p=P)[:, part, :]
                             ).then_inc(x_in[g], 16)
            sp.dma_start(wq[:, :, :], a["wqT"].rearrange("(c p) n -> p c n", p=P)).then_inc(wq_in, 16)
            sp.dma_start(bq[:, :], a["bq"].rearrange("(c p) -> p c", p=P), allow_slow_non_contiguous=True).then_inc(b_in, 16)
            sp.dma_start(bk[:, :], a["bk"].rearrange("(c p) -> p c", p=P), allow_slow_non_contiguous=True).then_inc(b_in, 16)
            sp.dma_start(mask_i[:, :], a["mask"]).then_inc(mask_in, 16)
            sp.dma_start(wk[:, :, :], a["wkT"].rearrange("(c p) n -> p c n", p=P)).then_inc(wk_in, 16)
            sp.dma_start(ctxT[:, :, :], a["ctxT"].rearrange("(c p) n -> p c n", p=P)).then_inc(ctx_in, 16)
            sp.dma_start(wv[:, :, :], a["wvT"].rearrange("(c p) n -> p c n", p=P)).then_inc(wv_in, 16)
            sp.dma_start(bv[:, :], a["bv"].partition_broadcast(P)).then_inc(bv_in, 16)
            for i in range(3):
                sp.wait_ge(split, i + 1)
                sp.dma_start(q_parts_dram[i].rearrange("(c p) n -> p c n", p=P), third[i][:, :, :]).then_inc(q_out, 16)
            for i in range(3):
                sp.wait_ge(split, 3 + i + 1)
                sp.dma_start(k_parts_dram[i].rearrange("(c p) n -> p c n", p=P), third[i][:, :, 0:S]).then_inc(k_out, 16)
            sp.wait_ge(k_out, 16 * 3)
            sp.wait_ge(q_out, 16 * 3)
            sp.wait_ge(aug_set, 2)
            for r, i in enumerate(THIRDS_K):
                sp.dma_start(keep["k_aug"][W * r:W * (r + 1), :, :],
                             k_parts_dram[i].rearrange("(h w) n -> w h n", w=W)).then_inc(aug_in, 16)
            sp.wait_ge(mask_split, 3)
            for h in range(H):
                sp.dma_start(keep["k_aug"][ROWS_PROD:ROWS_PROD + 1, h, :], mask_hi[:, :]).then_inc(aug_in, 16)
                sp.dma_start(keep["k_aug"][ROWS_PROD + 1:ROWS_PROD + 2, h, :], mask_lo[:, :]).then_inc(aug_in, 16)
            sp.wait_ge(aug_in, 16 * (len(THIRDS_K) + 2 * H))

        @block.gpsimd
        def _(pool):
            make_identity(pool, keep["ident"], ident_zero, ident_made)
            pool.wait_ge(ident_made, 1)
            pool.tensor_copy(keep["ident_bf"][:, :], keep["ident"][:, :]).then_inc(ident_made, 1)
            pool.wait_ge(ident_made, 2)
            pool.memset(keep["q_aug"][ROWS_PROD:P, :, :], 1.0).then_inc(aug_set, 1)
            pool.wait_ge(aug_set, 1)
            pool.memset(keep["k_aug"][ROWS_PROD:P, :, :], 1.0).then_inc(aug_set, 1)
            pool.wait_ge(aug_set, 2)
            pool.memset(keep["values_flat"][:, :], 0.0).then_inc(values_set, 1)
            pool.wait_ge(values_set, 1)
            pool.memset(keep["values"][:, :, :, :, W:W + 1], 1.0).then_inc(values_set, 1)

        @block.tensor
        def _(pe):
            fills = 0

            def take_bank():
                if fills >= 4:
                    seen = fills - 3
                    if seen <= n_act:
                        pe.wait_ge(bank_free_act, seen)
                    else:
                        pe.wait_ge(bank_free_act, n_act)
                        pe.wait_ge(bank_free_dve, seen - n_act)
                return bank[fills % 4]

            pe.wait_ge(ident_made, 1)
            for g in range(NT // 4):
                pe.wait_ge(norm.norm_done, 4 * (g + 1))
                for c in range(DC):
                    b = take_bank()
                    for j in range(4):
                        last = pe.transpose(b[:, j * P:(j + 1) * P], normed[:, 4 * g + j, c * P:(c + 1) * P],
                                            keep["ident"][:, :])
                    last.then_inc(bank_full, 1)
                    fills += 1
            pe.wait_ge(wq_in, 16)
            for which, src, w in (("q", normedT, wq), ("k", ctxT, wk)):
                if which == "q":
                    pe.wait_ge(bank_free_act, FILLS_T)
                else:
                    pe.wait_ge(ctx_in, 16)
                    pe.wait_ge(wk_in, 16)
                width = N if which == "q" else S
                for mm in range(DC):
                    for n0 in range(0, width, BANK):
                        n1 = min(width, n0 + BANK)
                        b = take_bank()
                        for c in range(DC):
                            last = pe.matmul(b[:, 0:n1 - n0], w[:, c, mm * P:(mm + 1) * P], src[:, c, n0:n1],
                                             start=(c == 0), stop=(c == DC - 1))
                        last.then_inc(bank_full, 1)
                        fills += 1
            pe.wait_ge(wv_in, 16)
            for t in range(KT):
                b = take_bank()
                for c in range(DC):
                    last = pe.matmul(b[0:key_rows(t), 0:D], ctxT[:, c, t * P:t * P + key_rows(t)], wv[:, c, :],
                                     start=(c == 0), stop=(c == DC - 1))
                last.then_inc(bank_full, 1)
                fills += 1

        @block.scalar
        def _(act):
            norm.on_scalar(act, 0)
            fills = 0
            for g in range(NT // 4):
                if g + 1 < NORM_GROUPS:
                    norm.on_scalar(act, g + 1)
                for c in range(DC):
                    act.wait_ge(bank_full, fills + 1)
                    act.activation(normedT[:, c, g * BANK:(g + 1) * BANK], bank[fills % 4][:, :], ACT.Copy
                                   ).then_inc(bank_free_act, 1)
                    fills += 1
            act.wait_ge(b_in, 32)
            for which, bias, width in (("q", bq, N), ("k", bk, S)):
                if which == "k":
                    act.wait_ge(split, 3)
                for mm in range(DC):
                    for n0 in range(0, width, BANK):
                        n1 = min(width, n0 + BANK)
                        act.wait_ge(bank_full, fills + 1)
                        act.activation(projT[:, mm, n0:n1], bank[fills % 4][:, 0:n1 - n0], ACT.Identity,
                                       bias=bias[:, mm:mm + 1]).then_inc(bank_free_act, 1)
                        fills += 1

        @block.vector
        def _(dve):
            norm.on_vector(dve, x_tok, lambda g: dve.wait_ge(x_in[g], 16))
            dve.wait_ge(mask_in, 16)
            dve.tensor_scalar(mask_raw, mask_i[:, :], MASK_RAW, -MASK_RAW, ALU.mult, ALU.add).then_inc(mask_split, 1)
            dve.wait_ge(mask_split, 1)
            dve.tensor_copy(mask_hi[:, :], mask_raw).then_inc(mask_split, 1)
            dve.wait_ge(mask_split, 2)
            dve.tensor_tensor(mask_lo[:, :], mask_raw, mask_hi[:, :], ALU.subtract).then_inc(mask_split, 1)

            for which, width in (("q", N), ("k", S)):
                base = FILLS_T + (FILLS_P if which == "q" else FILLS_QK)
                dve.wait_ge(bank_free_act, base)
                if which == "k":
                    dve.wait_ge(q_out, 16 * 3)
                s0 = 0 if which == "q" else 3
                full = projT[:, :, 0:width]
                dve.tensor_copy(third[0][:, :, 0:width], full).then_inc(split, 1)
                dve.wait_ge(split, s0 + 1)
                dve.tensor_tensor(full, full, third[0][:, :, 0:width], ALU.subtract).then_inc(steps, 1)
                dve.wait_ge(steps, s0 // 3 + 1)
                dve.tensor_copy(third[1][:, :, 0:width], full).then_inc(split, 1)
                dve.wait_ge(split, s0 + 2)
                dve.tensor_tensor(third[2][:, :, 0:width], full, third[1][:, :, 0:width], ALU.subtract
                                  ).then_inc(split, 1)
            dve.wait_ge(bv_in, 16)
            dve.wait_ge(values_set, 1)
            for t in range(KT):
                rows = key_rows(t)
                f = n_act + t
                dve.wait_ge(bank_full, f + 1)
                dve.tensor_tensor(keep["values"][0:rows, :, t, :, 0:W],
                                  bank[f % 4][0:rows, 0:D].rearrange("p (g h w) -> p g h w", g=GROUPS, h=HG),
                                  bv[0:rows, :].rearrange("p (g h w) -> p g h w", g=GROUPS, h=HG),
                                  ALU.add).then_inc(bank_free_dve, 1)


def attend(nc, keep, x_tok, q_parts_dram):
    with ExitStack() as scope:
        m = Memory(nc, scope)
        q_aug = keep["q_aug"][:, :, :].rearrange("p s n -> p (s n)")
        k_flat = keep["k_aug"][:, :, :].rearrange("p h n -> p (h n)")
        values = keep["values_flat"]
        ident, ident_bf = keep["ident"], keep["ident_bf"]
        vals = m.sb("group_values", [P, KT, HG, HEAD_PE])
        probs = [m.sb(f"probs{i}", [P, HG, BANK]) for i in range(3)]
        acc_sb = m.sb("acc_sb", [P, BANK])
        max_part = m.sb("max_part", [P, QT, HG, WHOLE + 1])
        max_raw = m.sb("max_raw", [P, QT, HG])
        max_rest = m.sb("max_rest", [P, QT, HG])
        max_thirds = m.sb("max_thirds", [P, QT, 3, HG], BF16)
        max_rows = m.sb("max_rows", [3 * HG, BANK], BF16)
        recip = m.sb("recip", [P, QT, HG])
        head_out = m.sb("head_out", [P, QT, HG, W])
        scores = [m.ps(f"scores{i}", [P, 2, BANK]) for i in range(2)]
        ring = [m.ps(f"ring{i}", [P, BANK]) for i in range(BANKS)]
        acc = m.ps("acc", [P, BANK])

        score_free = m.sem("score_free")
        q_in = m.sem("q_in")
        score_ready = m.sem("score_ready")
        probs_free = m.sem("probs_free")
        ring_free = m.sem("ring_free")
        ring_ready = m.sem("ring_ready")
        acc_free = m.sem("acc_free")
        thirds_ready = m.sem("thirds_ready")
        added = m.sem("added")
        max_placed = m.sem("max_placed")
        vals_ready = m.sem("vals_ready")
        max_chain = m.sem("max_chain")
        out_chain = m.sem("out_chain")

        CHAIN_MAX = 4
        Q_LOAD = 16 * len(THIRDS_Q)
        HALF = KT // 2 + 1
        SUMS_AT = 2 * HG + 2
        ROWS_LATER = 6

        def is_first(it):
            return isinstance(it, int) and it == 0

        def is_last(it):
            return isinstance(it, int) and it == STEPS - 1

        def entries_of(it, ahead):
            taken = 0 if is_first(it) else LEAD
            plan = [(1, c) for c in range(taken, CHUNKS)] if ahead >= 1 else []
            complete = len(plan)
            plan += [(2, c) for c in range(LEAD)] if ahead >= 2 else []
            if ahead >= 1:
                plan.insert(min(complete + ROWS_LATER, len(plan)), "rows")
            if not is_first(it):
                plan.insert(min(SUMS_AT, len(plan)), "sums")
            return plan

        BEFORE_FIRST = CHUNKS + 1
        IN_FIRST = len(entries_of(0, 2))
        IN_STEP = CHUNKS + 2
        assert IN_STEP % BANKS == 0

        def entries_before(it):
            if is_first(it):
                return BEFORE_FIRST
            if is_last(it):
                return entries_before(STEPS - 2) + len(entries_of(STEPS - 2, 1))
            return IN_STEP * it + BEFORE_FIRST + IN_FIRST - IN_STEP

        def bank_of(it, n):
            return ring[(entries_before(it if isinstance(it, int) else 1) + n) % BANKS]

        def sums_turned(it):
            return 1 if is_last(it) else SUMS_AT + 1

        ENTRIES = entries_before(STEPS - 1) + len(entries_of(STEPS - 1, 0)) + 1

        def chunk_products(c):
            qt, part = divmod(c, CHUNKS_QT)
            if part < CHUNKS_QT - 1:
                return [(qt, part // WHOLE, part % WHOLE * BANK, BANK, 0)]
            return [(qt, h, WHOLE * BANK, REST, h * REST) for h in range(HG)]

        block = scope.enter_context(nc.Block())

        @block.tensor
        def _(pe):
            pe.sem_inc(probs_free, 3)
            pe.sem_inc(score_ready, 1)

            def max_chunk(bank, it, c):
                for qt, h, k0, n, at in chunk_products(c):
                    last = pe.matmul(bank[:, at:at + n],
                                     q_aug[0:ROWS_MASKED, bass.ds(it % RING * (HG * BANK) + h * BANK + qt * P, P)],
                                     k_flat[0:ROWS_MASKED, bass.ds(it // QB * (HG * S) + h * S + k0, n)],
                                     start=True, stop=True)
                last.then_inc(ring_ready, 1)

            def turn_rows(bank, count):
                pe.wait_ge(thirds_ready, count + 1)
                rows = bank[:, :].bitcast(BF16)
                for qt in range(QT):
                    last = pe.transpose(rows[0:3 * HG, qt * P:(qt + 1) * P],
                                        max_thirds[:, qt, :, :].rearrange("p a b -> p (a b)"), ident_bf[:, :])
                last.then_inc(ring_ready, 1)

            def turn_sums(bank, count):
                pe.wait_ge(acc_free, count + 2)
                for qt in range(QT):
                    last = pe.transpose(bank[:, qt * P:(qt + 1) * P], acc_sb[:, qt * P:(qt + 1) * P], ident[:, :])
                last.then_inc(ring_ready, 1)

            def score(it, t, h):
                pair, j = divmod(h, 2)
                rows = key_rows(t % KT)
                if j == 0:
                    pe.wait_ge(score_free, 2 * KT * it + 2 * t + pair + 1)
                at = it + t // KT
                last = pe.matmul(scores[pair][0:rows, j, :],
                                 k_flat[0:ROWS_ALL, bass.ds(at // QB * (HG * S) + h * S + t % KT * P, rows)],
                                 q_aug[0:ROWS_ALL, bass.ds(at % RING * (HG * BANK) + h * BANK, BANK)],
                                 start=True, stop=True)
                if j == 1:
                    last.then_inc(score_ready, 1)

            def weigh(it, t):
                rows = key_rows(t)
                pe.wait_ge(score_free, 2 * KT * it + 2 * t + 4)
                if t == 0:
                    pe.wait_ge(vals_ready, 2 * it + 1)
                    pe.wait_ge(acc_free, it + 1)
                if t == HALF:
                    pe.wait_ge(vals_ready, 2 * it + 2)
                slot = 2 if t == KT - 1 else t % 2
                for h in range(HG):
                    last = pe.matmul(acc[HEAD_PE * h:HEAD_PE * (h + 1), :], vals[0:rows, t, h, :],
                                     probs[slot][0:rows, h, :], start=(t == 0), stop=(t == KT - 1),
                                     tile_position=(0, HEAD_PE * h))
                last.then_inc(probs_free, 1)

            def fill(it, entry, n):
                pe.wait_ge(ring_free, entries_before(it) + n + 1)
                bank = bank_of(it, n)
                if entry == "sums":
                    turn_sums(bank, it - 1)
                elif entry == "rows":
                    turn_rows(bank, it + 1)
                else:
                    ahead, c = entry
                    if entry == (2, 0):
                        pe.wait_ge(q_in, Q_LOAD * (it + 3))
                    max_chunk(bank, it + ahead, c)

            def step(it, ahead):
                entries = entries_of(it, ahead)
                rate = max(len(entries), IN_STEP)
                done = 0
                for t in range(KT):
                    if t == KT - 1 and ahead >= 1:
                        pe.wait_ge(max_placed, 16 * it + 32)
                    for h in range(HG):
                        if t < KT - 1 or ahead >= 1:
                            score(it, t + 1, h)
                        due = min(len(entries), -(-(HG * t + h + 1) * rate // PLACES))
                        for n in range(done, due):
                            fill(it, entries[n], n)
                        done = due
                        if h == 1:
                            weigh(it, t)

            pe.wait_ge(q_in, Q_LOAD)
            for c in range(CHUNKS):
                pe.wait_ge(ring_free, c + 1)
                max_chunk(ring[c % BANKS], 0, c)
            pe.wait_ge(q_in, 2 * Q_LOAD)
            pe.wait_ge(ring_free, CHUNKS + 1)
            turn_rows(ring[CHUNKS % BANKS], 0)
            pe.wait_ge(max_placed, 16)
            for h in range(HG):
                score(0, 0, h)
            step(0, 2)
            with pe.Fori(1, STEPS - 2) as it:
                step(it, 2)
            step(STEPS - 2, 1)
            step(STEPS - 1, 0)
            pe.wait_ge(ring_free, ENTRIES)
            turn_sums(ring[(ENTRIES - 1) % BANKS], STEPS - 1)

        @block.scalar
        def _(act):
            act.sem_inc(score_free, 2)
            act.sem_inc(acc_free, 1)

            def copy_sums(count):
                act.wait_ge(probs_free, KT * count + KT + 3)
                if not is_first(count):
                    act.wait_ge(ring_ready, entries_before(count) + sums_turned(count))
                act.activation(acc_sb[:, :], acc[:, :], ACT.Copy).then_inc(acc_free, 1)

            def step(it, ahead):
                for t in range(KT):
                    rows = key_rows(t)
                    slot = 2 if t == KT - 1 else t % 2
                    back = {0: 1, 1: 2, KT - 1: 3}.get(t, t + 2)
                    act.wait_ge(probs_free, KT * it + back)
                    for pair in range(2):
                        act.wait_ge(score_ready, 2 * KT * it + 2 * t + pair + 2)
                        act.activation(probs[slot][0:rows, 2 * pair:2 * pair + 2, :], scores[pair][0:rows, :, :],
                                       ACT.Exp, scale=SCORE_SCALE).then_inc(score_free, 1)
                    if t == 0 and not is_first(it):
                        copy_sums(it - 1)

            step(0, 2)
            with act.Fori(1, STEPS - 2) as it:
                step(it, 2)
            step(STEPS - 2, 1)
            step(STEPS - 1, 0)
            copy_sums(STEPS - 1)

        @block.gpsimd
        def _(pool):
            def place_values(count, half):
                lo, hi = (0, HALF) if half == 0 else (HALF, KT)
                if not is_first(count):
                    pool.wait_ge(probs_free, KT * (count - 1) + hi + 3)
                pool.tensor_copy(vals[:, lo:hi, :, :].rearrange("p t h w -> p (t h w)"),
                                 values[:, bass.ds(count // QB * (KT * HG * HEAD_PE) + lo * (HG * HEAD_PE),
                                                   (hi - lo) * HG * HEAD_PE)]).then_inc(vals_ready, 1)

            place_values(0, 0)
            place_values(0, 1)
            with pool.Fori(1, STEPS) as it:
                place_values(it, 0)
                place_values(it, 1)

        @block.vector
        def _(dve):
            dve.sem_inc(ring_free, BANKS)

            def reduce_chunk(bank, c):
                qt, part = divmod(c, CHUNKS_QT)
                if part < CHUNKS_QT - 1:
                    h, k = divmod(part, WHOLE)
                    dve.tensor_reduce(max_part[:, qt, h, k:k + 1], bank[:, :], AX.X, ALU.max).then_inc(ring_free, 1)
                else:
                    dve.tensor_reduce(max_part[:, qt, :, WHOLE],
                                      bank[:, 0:HG * REST].rearrange("p (h n) -> p h n", h=HG), AX.X, ALU.max
                                      ).then_inc(ring_free, 1)

            def copy_rows(bank, count):
                if not is_first(count):
                    dve.wait_ge(max_placed, 16 * count)
                dve.tensor_copy(max_rows[:, :], bank[:, :].bitcast(BF16)[0:3 * HG, 0:BANK]).then_inc(ring_free, 1)

            th = [max_thirds[:, :, i, :] for i in range(3)]
            raw, rest = max_raw[:, :, :], max_rest[:, :, :]

            def split_maxima(count, reduced, part):
                if part == 0:
                    dve.wait_ge(ring_free, reduced + BANKS)
                    dve.tensor_reduce(raw, max_part[:, :, :, :], AX.X, ALU.max).then_inc(max_chain, 1)
                    dve.wait_ge(max_chain, CHAIN_MAX * count + 1)
                    return
                if part == 1:
                    dve.tensor_scalar(th[0], raw, -1.0, None, ALU.mult).then_inc(max_chain, 1)
                    return
                dve.wait_ge(max_chain, CHAIN_MAX * count + part)
                if part == 2:
                    dve.scalar_tensor_tensor(rest, raw, -1.0, th[0], ALU.mult, ALU.subtract).then_inc(max_chain, 1)
                if part == 3:
                    dve.tensor_copy(th[1], rest).then_inc(max_chain, 1)
                if part == 4:
                    dve.tensor_tensor(th[2], rest, th[1], ALU.subtract).then_inc(thirds_ready, 1)

            def divide_sums(bank, count):
                sums = bank[:, :].rearrange("p (q h w) -> p q h w", q=QT, h=HG)
                dve.reciprocal(recip[:, :, :], sums[:, :, :, W]).then_inc(out_chain, 1)
                dve.wait_ge(out_chain, count + 1)
                dve.tensor_tensor(head_out[:, :, :, :], sums[:, :, :, 0:W],
                                  recip[:, :, :].rearrange("p q (h o) -> p q h o", o=1).broadcast_to([P, QT, HG, W]),
                                  ALU.mult).then_inc(ring_free, 1)

            def add_sums(count, used):
                dve.wait_ge(ring_free, used + BANKS)
                xv = x_tok[:, bass.ds(count % QB * QT, QT), bass.ds(count // QB * (HG * W), HG * W)]
                dve.tensor_tensor(xv, xv, head_out[:, :, :, :].rearrange("p q h w -> p q (h w)"), ALU.add
                                  ).then_inc(added, 1)

            def step(it, ahead):
                entries = entries_of(it, ahead)
                base = entries_before(it)
                split_from = max([n for n, e in enumerate(entries) if isinstance(e, tuple) and e[0] == 1], default=None)
                for n, entry in enumerate(entries):
                    dve.wait_ge(ring_ready, base + n + 1)
                    bank = bank_of(it, n)
                    if entry == "sums":
                        divide_sums(bank, it - 1)
                    elif entry == "rows":
                        copy_rows(bank, it + 1)
                    else:
                        reduce_chunk(bank, entry[1])
                    if n > 0 and entries[n - 1] == "sums" or entry == "sums" and n == len(entries) - 1:
                        add_sums(it - 1, base + (n if entry != "sums" else n + 1))
                    if ahead >= 1 and n >= split_from:
                        parts = [n - split_from] if ahead == 2 else range(5) if n == split_from else []
                        for part in parts:
                            if part < 5:
                                split_maxima(it + 1, base + split_from + 1, part)

            for c in range(CHUNKS):
                dve.wait_ge(ring_ready, c + 1)
                reduce_chunk(ring[c % BANKS], c)
            for part in range(5):
                split_maxima(0, CHUNKS, part)
            dve.wait_ge(ring_ready, CHUNKS + 1)
            copy_rows(ring[CHUNKS % BANKS], 0)
            step(0, 2)
            with dve.Fori(1, STEPS - 2) as it:
                step(it, 2)
            step(STEPS - 2, 1)
            step(STEPS - 1, 0)
            dve.wait_ge(ring_ready, ENTRIES)
            divide_sums(ring[(ENTRIES - 1) % BANKS], STEPS - 1)
            add_sums(STEPS - 1, ENTRIES)

        @block.sync
        def _(sp):
            def load_queries(count):
                if not is_first(count):
                    sp.wait_ge(q_in, Q_LOAD * count)
                for r, i in enumerate(THIRDS_Q):
                    sp.dma_start(
                        q_aug[W * r:W * (r + 1), bass.ds(count % RING * (HG * BANK), HG * BANK)].rearrange("p (h n) -> p h n", h=HG),
                        q_parts_dram[i, bass.ds(count // QB * (HG * W), HG * W), bass.ds(count % QB * BANK, BANK)].rearrange("(h w) n -> w h n", h=HG)
                    ).then_inc(q_in, 16)

            def place(count):
                at = entries_of(count - 1, 1 if is_last(count) else 2).index("rows") if not is_first(count) else 0
                sp.wait_ge(ring_free, (entries_before(count - 1) + at if not is_first(count) else CHUNKS) + 1 + BANKS)
                sp.dma_start(
                    q_aug[ROWS_MASKED:ROWS_ALL, bass.ds(count % RING * (HG * BANK), HG * BANK)],
                    max_rows[:, :]).then_inc(max_placed, 16)

            for count in range(RING - 1):
                load_queries(count)
            place(0)
            load_queries(RING - 1)
            place(1)
            with sp.Fori(1, STEPS - RING + 1) as it:
                sp.wait_ge(score_ready, 2 * KT * it + 1)
                load_queries(it + RING - 1)
                place(it + 1)
            for count in range(STEPS - RING + 2, STEPS):
                place(count)
            sp.wait_ge(max_placed, 16 * STEPS)


E = 16
F = 512
FC = F // P
SHARED = 2
TOP = 2
CAP = -(-N * TOP * 5 // (E * 4))
CAP_TILES = -(-CAP // P)
SLOTS = E * CAP
CHUNK_TOK = N // (P // E)
NCH = N // CHUNK_TOK
KEY_BITS = 16
KEY_ABOVE = 131072.0

C_SUM, C_BEFORE = 0, P
C_BASE = 2 * P
C_EXPERT = C_BASE + 1
C_DUMMY = C_EXPERT + E
C_ALL = C_DUMMY + TOP * NT


def shape_constants(np):
    c = np.zeros((P, C_ALL), np.float32)
    e, chunk = np.arange(P) // NCH, np.arange(P) % NCH
    same = e[:, None] == e[None, :]
    c[:, C_SUM:C_SUM + P] = same
    c[:, C_BEFORE:C_BEFORE + P] = same & (chunk[:, None] < chunk[None, :])
    c[:, C_BASE] = e * CAP + 1
    c[:, C_EXPERT:C_EXPERT + E] = np.arange(E)
    t = np.arange(NT)[None, :] * P + np.arange(P)[:, None]
    for k in range(TOP):
        c[:, C_DUMMY + k * NT:C_DUMMY + (k + 1) * NT] = SLOTS + k * N + t
    return c


NORM_GROUP = 4
NORM_GROUPS = NT // NORM_GROUP


class Norm:

    def __init__(self, m, tag, normed):
        self.stats = m.sb(f"{tag}_stats", [P, NT, 6])
        self.meanvar = m.sb(f"{tag}_meanvar", [P, NT, 2])
        self.std, self.rstd = m.sb(f"{tag}_std", [P, NT]), m.sb(f"{tag}_rstd", [P, NT])
        self.eps = m.sb(f"{tag}_eps", [P, 1])
        self.normed = normed
        self.stats_done = m.sem(f"{tag}_stats_done")
        self.std_done = m.sem(f"{tag}_std_done")
        self.rstd_done = m.sem(f"{tag}_rstd_done")
        self.norm_done = m.sem(f"{tag}_norm_done")

    def _measure(self, dve, x_tok, g):
        tiles = range(NORM_GROUP * g, NORM_GROUP * (g + 1))
        for t in tiles:
            dve.bn_stats(self.stats[:, t, :], x_tok[:, t, :]).then_inc(self.stats_done, 1)
        for i, t in enumerate(tiles):
            dve.wait_ge(self.stats_done, self._measured(g) - 2 * NORM_GROUP + i + 1)
            dve.bn_aggr(self.meanvar[:, t, :], self.stats[:, t, :]).then_inc(self.stats_done, 1)

    def _measured(self, g):
        return 1 + 2 * NORM_GROUP * (g + 1)

    def _apply(self, dve, x_tok, g):
        part = slice(NORM_GROUP * g, NORM_GROUP * (g + 1))
        dve.wait_ge(self.std_done, g + 1)
        dve.reciprocal(self.rstd[:, part], self.std[:, part]).then_inc(self.rstd_done, 1)
        dve.wait_ge(self.rstd_done, g + 1)
        for t in range(NORM_GROUP * g, NORM_GROUP * (g + 1)):
            dve.tensor_scalar(self.normed[:, t, :], x_tok[:, t, :], self.meanvar[:, t, 0:1], self.rstd[:, t:t + 1],
                              ALU.subtract, ALU.mult).then_inc(self.norm_done, 1)

    def on_vector(self, dve, x_tok, before=lambda g: None):
        dve.memset(self.eps[:, :], EPS_LN).then_inc(self.stats_done, 1)
        for g in range(NORM_GROUPS + 1):
            if g < NORM_GROUPS:
                before(g)
                self._measure(dve, x_tok, g)
            if g > 0:
                self._apply(dve, x_tok, g - 1)

    def on_scalar(self, act, g):
        part = slice(NORM_GROUP * g, NORM_GROUP * (g + 1))
        act.wait_ge(self.stats_done, self._measured(g))
        act.activation(self.std[:, part], self.meanvar[:, part, 1], ACT.Sqrt, bias=self.eps[:, 0:1]
                       ).then_inc(self.std_done, 1)


def route_and_share(nc, a, keep, x_tok, normed, slots_in_dram, route):
    with ExitStack() as scope:
        m = Memory(nc, scope)
        ident = keep["ident"]
        norm = Norm(m, "ln2", normed)
        tokT = m.sb("tokT", [P, DC, N])
        sw1, sw3 = (m.sb(n, [P, SHARED, DC, F]) for n in ("sw1_sb", "sw3_sb"))
        sw2 = m.sb("sw2_sb", [P, SHARED, FC, D])
        gate_w, gate_b = m.sb("gate_w_sb", [P, DC, E]), m.sb("gate_b_rows", [P, E])
        const = m.sb("const", [P, C_ALL])
        zeros = m.sb("zeros", [P, 2560])
        silu = [m.sb(f"silu{i}", [P, BANK]) for i in range(2)]
        hidden = [m.sb(f"hidden{i}", [P, SHARED * FC, BANK]) for i in range(2)]
        gu = [m.ps(f"gu{i}", [P, 2, BANK]) for i in range(2)]
        y_bank = [m.ps(f"y_bank{i}", [P, BANK]) for i in range(2)]
        small = m.ps("small", [P, BANK])
        wide = m.ps("wide", [P, BANK])

        logits, gates, onehot1, onehot2, work, key = (m.sb(n, [P, NT, E]) for n in
                                                      ("logits", "gates", "onehot1", "onehot2", "work", "rkey"))
        col = m.sb("col", [P, NT])
        col2 = m.sb("col2", [P, NT])
        chosen_logit = [m.sb(f"chosen_logit{k}", [P, NT]) for k in range(TOP)]
        bits, sign = m.sb("bits", [P, NT, E], I32), m.sb("sign", [P, NT, E], I32)
        hi_tok, lo_tok = m.sb("hi_tok", [P, 2, E, NCH]), m.sb("lo_tok", [P, 2, E, NCH])
        slot_tok = m.sb("slot_tok", [P, NT, E])
        hi, lo = m.sb("hi", [P, CHUNK_TOK]), m.sb("lo", [P, CHUNK_TOK])
        above, equal, r1, r2, r3 = (m.sb(n, [P, CHUNK_TOK]) for n in ("above", "equal", "r1", "r2", "r3"))
        ones = m.sb("ones_row", [P, CHUNK_TOK])
        cand, cnt, inc = (m.sb(n, [P, 1]) for n in ("cand", "cnt", "inc"))
        totals = m.sb("totals", [P, 2])
        offs = m.sb("offs", [P, 4])

        sh_in, gate_in, const_in = m.sem("sh_in"), m.sem("gate_in"), m.sem("const_in")
        zero_set, zero_out = m.sem("zero_set"), m.sem("zero_out")
        t_full, t_free = m.sem("t_full"), m.sem("t_free")
        logits_ready, shifted, expd = m.sem("logits_ready"), m.sem("shifted"), m.sem("expd")
        gu_ready, silu_done, h_done = m.sem("gu_ready"), m.sem("silu_done"), m.sem("h_done")
        y_ready, y_done = m.sem("y_ready"), m.sem("y_done")
        keys_ready, keys_turned = m.sem("keys_ready"), m.sem("keys_turned")
        counted, summed = m.sem("counted"), m.sem("summed")
        totals_ready, offs_ready = m.sem("totals_ready"), m.sem("offs_ready")
        slots_ready, slots_turned = m.sem("slots_ready"), m.sem("slots_turned")
        idx_ready, sent = m.sem("idx_ready"), m.sem("sent")
        chain = m.sem("route_chain")

        UB = SHARED * FC
        BLOCKS = N // BANK
        KEYS_AT = 6
        EVENTS = []
        for blk_ in range(BLOCKS):
            for u_ in range(UB):
                EVENTS.append(("up", UB * blk_ + u_))
                if u_ == 1 and blk_ > 0:
                    EVENTS.append(("down", blk_ - 1))
        EVENTS.append(("down", BLOCKS - 1))
        SEARCH_FROM = ("up", KEYS_AT + 1)
        ROUNDS = 2 * KEY_BITS

        def rounds_of(event):
            first = 0
            for e in EVENTS[EVENTS.index(SEARCH_FROM):]:
                if e == event:
                    return first
                first += 2 if e[0] == "up" else 2 * (BANK // P)
            return -ROUNDS

        SEARCH_END = next(e for e in EVENTS if rounds_of(e) >= 0 and
                          rounds_of(e) + (2 if e[0] == "up" else 2 * (BANK // P)) >= ROUNDS)
        OFFS_AT = SEARCH_END
        TURN_AT = EVENTS[EVENTS.index(SEARCH_END) + 2]

        block = scope.enter_context(nc.Block())

        @block.sync
        def _(sp):
            sp.dma_start(gate_w[:, :, :], a["gate_w"].rearrange("(c p) e -> p c e", p=P)).then_inc(gate_in, 16)
            sp.dma_start(gate_b[:, :], a["gate_b"].partition_broadcast(P)).then_inc(gate_in, 16)
            for s in range(SHARED):
                sp.dma_start(sw1[:, s], a["sw1"][s].rearrange("(c p) f -> p c f", p=P)).then_inc(sh_in, 16)
                sp.dma_start(sw3[:, s], a["sw3"][s].rearrange("(c p) f -> p c f", p=P)).then_inc(sh_in, 16)
                sp.dma_start(sw2[:, s], a["sw2"][s].rearrange("(c p) f -> p c f", p=P)).then_inc(sh_in, 16)
            sp.dma_start(const[:, :], a["const"]).then_inc(const_in, 16)
            sp.wait_ge(zero_set, 1)
            for i in range(SLOTS * D // (P * 2560)):
                r = P * 2560 // D
                sp.dma_start(slots_in_dram[i * r:(i + 1) * r, :].rearrange("(p k) d -> p (k d)", p=P), zeros[:, :]
                             ).then_inc(zero_out, 16)
            sp.wait_ge(zero_out, 16 * (SLOTS * D // (P * 2560)))

        @block.gpsimd
        def _(pool):
            pool.memset(zeros[:, :], 0.0).then_inc(zero_set, 1)
            pool.wait_ge(zero_out, 16 * (SLOTS * D // (P * 2560)))
            pool.wait_ge(idx_ready, TOP)
            pool.wait_ge(norm.norm_done, NT)
            for k in range(TOP):
                for t in range(NT):
                    pool.indirect_dma_start(
                        out=slots_in_dram[:, :], out_offset=bass.IndirectOffsetOnAxis(ap=route["send"][k][:, t:t + 1], axis=0),
                        in_=normed[:, t, :], in_offset=None).then_inc(sent, 16)
            pool.wait_ge(sent, 16 * TOP * NT)

        @block.tensor
        def _(pe):
            for f in range(DC * NT // 4):
                g, c = divmod(f, DC)
                pe.wait_ge(norm.norm_done, 4 * (g + 1))
                if f >= 4:
                    pe.wait_ge(t_free, f - 3)
                b = gu[f % 4 // 2][:, f % 2, :]
                for j in range(4):
                    last = pe.transpose(b[:, j * P:(j + 1) * P], normed[:, 4 * g + j, c * P:(c + 1) * P], ident[:, :])
                last.then_inc(t_full, 1)
            pe.wait_ge(t_free, DC * NT // 4)
            pe.wait_ge(gate_in, 32)
            for t in range(NT):
                for c in range(DC):
                    last = pe.matmul(small[:, t * E:(t + 1) * E], tokT[:, c, t * P:(t + 1) * P], gate_w[:, c, :],
                                     start=(c == 0), stop=(c == DC - 1))
            last.then_inc(logits_ready, 1)
            pe.wait_ge(sh_in, 16 * 3 * SHARED)
            pe.wait_ge(const_in, 16)

            def search_round(n):
                if 0 <= n < ROUNDS:
                    pe.wait_ge(counted, n + 1)
                    pe.matmul(small[:, 0:1], const[:, C_SUM:C_SUM + P], cnt[:, :], start=True, stop=True
                              ).then_inc(summed, 1)

            def unit(n, first_round):
                blk, u = divmod(n, UB)
                s, f = divmod(u, FC)
                if n >= 2:
                    pe.wait_ge(h_done, n - 1)
                for j, w in enumerate((sw1, sw3)):
                    for c in range(DC):
                        last = pe.matmul(gu[n % 2][:, j, :], w[:, s, c, f * P:(f + 1) * P],
                                         tokT[:, c, blk * BANK:(blk + 1) * BANK], start=(c == 0), stop=(c == DC - 1))
                    if j == 1:
                        last.then_inc(gu_ready, 1)
                    search_round(first_round + j)

            def down(blk, first_round):
                pe.wait_ge(h_done, UB * (blk + 1))
                for tt in range(BANK // P):
                    t = 4 * blk + tt
                    if t >= 2:
                        pe.wait_ge(y_done, t - 1)
                    for u in range(UB):
                        s, f = divmod(u, FC)
                        last = pe.matmul(y_bank[tt % 2][:, 0:D], hidden[blk % 2][:, u, tt * P:(tt + 1) * P],
                                         sw2[:, s, f, :], start=(u == 0), stop=(u == UB - 1))
                        if u == UB - 1:
                            last.then_inc(y_ready, 1)
                        if u % (UB // 2) == UB // 2 - 1:
                            search_round(first_round + 2 * tt + u // (UB // 2))

            for event in EVENTS:
                kind, n = event
                (unit if kind == "up" else down)(n, rounds_of(event))
                if event == ("up", KEYS_AT):
                    pe.wait_ge(keys_ready, 1)
                    for j, src in enumerate((hi_tok, lo_tok)):
                        for s in range(2):
                            last = pe.transpose(wide[:, j * CHUNK_TOK + s * P:j * CHUNK_TOK + (s + 1) * P],
                                                src[:, s].rearrange("p e c -> p (e c)"), ident[:, :])
                    last.then_inc(keys_turned, 1)
                if event == OFFS_AT:
                    pe.wait_ge(totals_ready, 1)
                    pe.matmul(small[:, 0:2], const[:, C_BEFORE:C_BEFORE + P], totals[:, :], start=True, stop=True)
                    pe.matmul(small[:, 2:4], const[:, C_SUM:C_SUM + P], totals[:, :], start=True, stop=True
                              ).then_inc(offs_ready, 1)
                if event == TURN_AT:
                    pe.wait_ge(slots_ready, 1)
                    for s in range(2):
                        last = pe.transpose(wide[:, s * P:(s + 1) * P], r1[:, s * P:(s + 1) * P], ident[:, :])
                    last.then_inc(slots_turned, 1)

        @block.scalar
        def _(act):
            norm.on_scalar(act, 0)
            for f in range(DC * NT // 4):
                g, c = divmod(f, DC)
                if c == 0 and g + 1 < NORM_GROUPS:
                    norm.on_scalar(act, g + 1)
                act.wait_ge(t_full, f + 1)
                act.activation(tokT[:, c, g * BANK:(g + 1) * BANK], gu[f % 4 // 2][:, f % 2, :], ACT.Copy
                               ).then_inc(t_free, 1)
            act.wait_ge(shifted, 1)
            act.activation(gates[:, :, :], work[:, :, :], ACT.Exp).then_inc(expd, 1)
            for n in range(UB * BLOCKS):
                act.wait_ge(gu_ready, n + 1)
                if n >= 2:
                    act.wait_ge(h_done, n - 1)
                act.activation(silu[n % 2][:, :], gu[n % 2][:, 0, :], ACT.Silu).then_inc(silu_done, 1)

        @block.vector
        def _(dve):
            made = 0

            def link(ins):
                nonlocal made
                made += 1
                ins.then_inc(chain, 1)
                dve.wait_ge(chain, made)

            def over_experts(x):
                return x[:, :].rearrange("p (t o) -> p t o", o=1).broadcast_to([P, NT, E])

            def over_tokens(x):
                return x.rearrange("p (o e) -> p o e", o=1).broadcast_to([P, NT, E])

            def unit(n):
                dve.wait_ge(silu_done, n + 1)
                if n >= 2 * UB:
                    dve.wait_ge(y_ready, 4 * (n // UB - 1))
                dve.tensor_tensor(hidden[n // UB % 2][:, n % UB, :], silu[n % 2][:, :], gu[n % 2][:, 1, :], ALU.mult
                                  ).then_inc(h_done, 1)

            def add_tile(t):
                dve.wait_ge(y_ready, t + 1)
                dve.scalar_tensor_tensor(x_tok[:, t, :], y_bank[t % 2][:, 0:D], 1.0 / SHARED, x_tok[:, t, :],
                                         ALU.mult, ALU.add).then_inc(y_done, 1)

            def shift_logits():
                dve.wait_ge(logits_ready, 1)
                link(dve.tensor_copy(logits[:, :, :], small[:, 0:NT * E].rearrange("p (t e) -> p t e", e=E)))
                link(dve.tensor_reduce(col[:, :], logits[:, :, :], AX.X, ALU.max))
                dve.tensor_tensor(work[:, :, :], logits[:, :, :], over_experts(col), ALU.subtract).then_inc(shifted, 1)

            def finish_gates():
                dve.wait_ge(expd, 1)
                link(dve.tensor_reduce(col[:, :], gates[:, :, :], AX.X, ALU.add))
                link(dve.reciprocal(col2[:, :], col[:, :]))
                link(dve.tensor_tensor(gates[:, :, :], gates[:, :, :], over_experts(col2), ALU.mult))
                link(dve.tensor_tensor(gates[:, :, :], gates[:, :, :], over_tokens(gate_b[:, :]), ALU.add))

            def best_gate(k, onehot):
                link(dve.tensor_reduce(col[:, :], gates[:, :, :], AX.X, ALU.max))
                link(dve.tensor_tensor(work[:, :, :], gates[:, :, :], over_experts(col), ALU.is_equal))
                link(dve.scalar_tensor_tensor(key[:, :, :], work[:, :, :], -float(2 * E),
                                              over_tokens(const[:, C_EXPERT:C_EXPERT + E]), ALU.mult, ALU.add))
                link(dve.tensor_reduce(col[:, :], key[:, :, :], AX.X, ALU.min))
                link(dve.tensor_tensor(onehot[:, :, :], key[:, :, :], over_experts(col), ALU.is_equal))
                link(dve.tensor_tensor(work[:, :, :], logits[:, :, :], onehot[:, :, :], ALU.mult))
                link(dve.tensor_reduce(chosen_logit[k][:, :], work[:, :, :], AX.X, ALU.add))
                if k == 0:
                    link(dve.scalar_tensor_tensor(gates[:, :, :], onehot[:, :, :], -1e30, gates[:, :, :],
                                                  ALU.mult, ALU.add))

            def order_keys():
                raw = logits[:, :, :].bitcast(I32)
                link(dve.tensor_scalar(sign[:, :, :], raw, 31, 0x7FFFFFFF, ALU.arith_shift_right, ALU.bitwise_and))
                link(dve.tensor_tensor(bits[:, :, :], raw, sign[:, :, :], ALU.bitwise_xor))
                link(dve.tensor_scalar(sign[:, :, :], bits[:, :, :], 16, None, ALU.arith_shift_right))
                link(dve.tensor_scalar(bits[:, :, :], bits[:, :, :], 0xFFFF, None, ALU.bitwise_and))
                link(dve.tensor_tensor(work[:, :, :], onehot1[:, :, :], onehot2[:, :, :], ALU.add))
                link(dve.scalar_tensor_tensor(key[:, :, :], sign[:, :, :], 32769.0, work[:, :, :], ALU.add, ALU.mult))

            def lay_keys():
                for s in range(2):
                    v = key[:, :, :].rearrange("p (c s) e -> p s e c", s=2)[:, s]
                    link(dve.tensor_copy(hi_tok[:, s], v))
                    v = bits[:, :, :].rearrange("p (c s) e -> p s e c", s=2)[:, s]
                    if s == 0:
                        link(dve.tensor_copy(lo_tok[:, s], v))
                    else:
                        dve.tensor_copy(lo_tok[:, s], v).then_inc(keys_ready, 1)

            def take_keys():
                dve.wait_ge(keys_turned, 1)
                link(dve.tensor_copy(hi[:, :], wide[:, 0:CHUNK_TOK]))
                link(dve.tensor_copy(lo[:, :], wide[:, CHUNK_TOK:2 * CHUNK_TOK]))
                count_keys(0)

            def count_keys(n):
                if n % KEY_BITS == 0:
                    link(dve.memset(cand[:, :], 2.0 ** (KEY_BITS - 1)))
                dve.tensor_scalar(r3[:, :], (hi, lo)[n // KEY_BITS][:, :], cand[:, 0:1], None, ALU.is_ge, ALU.add,
                                  accum_out=cnt[:, :]).then_inc(counted, 1)

            def end_round(n):
                if not 0 <= n < ROUNDS:
                    return
                step = 2.0 ** (KEY_BITS - 1 - n % KEY_BITS)
                dve.wait_ge(summed, n + 1)
                link(dve.tensor_scalar(inc[:, :], small[:, 0:1], float(CAP), step, ALU.is_ge, ALU.mult))
                link(dve.scalar_tensor_tensor(cand[:, :], inc[:, :], -0.5 * step, cand[:, :], ALU.add, ALU.add))
                if n == KEY_BITS - 1:
                    lower_keys()
                if n == ROUNDS - 1:
                    rank()
                else:
                    count_keys(n + 1)

            def lower_keys():
                link(dve.tensor_scalar(cand[:, :], cand[:, :], -0.5, None, ALU.add))
                link(dve.tensor_scalar(above[:, :], hi[:, :], cand[:, 0:1], None, ALU.is_gt))
                link(dve.tensor_scalar(equal[:, :], hi[:, :], cand[:, 0:1], None, ALU.is_equal))
                link(dve.scalar_tensor_tensor(r1[:, :], lo[:, :], 1.0, equal[:, :], ALU.add, ALU.mult))
                link(dve.scalar_tensor_tensor(r2[:, :], above[:, :], KEY_ABOVE, r1[:, :], ALU.mult, ALU.add))
                link(dve.tensor_scalar(lo[:, :], r2[:, :], -1.0, None, ALU.add))

            def rank():
                link(dve.tensor_scalar(cand[:, :], cand[:, :], -0.5, None, ALU.add))
                link(dve.tensor_scalar(r3[:, :], hi[:, :], 0.0, None, ALU.is_gt))
                link(dve.scalar_tensor_tensor(above[:, :], lo[:, :], cand[:, 0:1], r3[:, :], ALU.is_gt, ALU.mult))
                link(dve.scalar_tensor_tensor(equal[:, :], lo[:, :], cand[:, 0:1], r3[:, :], ALU.is_equal, ALU.mult))
                link(dve.memset(ones[:, :], 1.0))
                link(dve.tensor_tensor_scan(r1[:, :], ones[:, :], above[:, :], 0.0, ALU.mult, ALU.add))
                link(dve.tensor_tensor_scan(r2[:, :], ones[:, :], equal[:, :], 0.0, ALU.mult, ALU.add))
                link(dve.tensor_copy(totals[:, 0:1], r1[:, CHUNK_TOK - 1:CHUNK_TOK]))
                dve.tensor_copy(totals[:, 1:2], r2[:, CHUNK_TOK - 1:CHUNK_TOK]).then_inc(totals_ready, 1)

            def place():
                dve.wait_ge(offs_ready, 1)
                base = const[:, C_BASE:C_BASE + 1]
                link(dve.tensor_copy(offs[:, :], small[:, 0:4]))
                link(dve.scalar_tensor_tensor(r1[:, :], r1[:, :], offs[:, 0:1], above[:, :], ALU.add, ALU.subtract))
                link(dve.scalar_tensor_tensor(r2[:, :], r2[:, :], offs[:, 1:2], equal[:, :], ALU.add, ALU.subtract))
                link(dve.tensor_scalar(r2[:, :], r2[:, :], offs[:, 2:3], None, ALU.add))
                link(dve.scalar_tensor_tensor(r3[:, :], r2[:, :], float(CAP), equal[:, :], ALU.is_lt, ALU.mult))
                link(dve.scalar_tensor_tensor(r2[:, :], r2[:, :], base, r3[:, :], ALU.add, ALU.mult))
                link(dve.scalar_tensor_tensor(r1[:, :], r1[:, :], base, above[:, :], ALU.add, ALU.mult))
                dve.tensor_tensor(r1[:, :], r1[:, :], r2[:, :], ALU.add).then_inc(slots_ready, 1)

            def address():
                dve.wait_ge(slots_turned, 1)
                for s in range(2):
                    link(dve.tensor_copy(slot_tok[:, :, :].rearrange("p (c s) e -> p s e c", s=2)[:, s],
                                         wide[:, s * P:(s + 1) * P].rearrange("p (e c) -> p e c", e=E)))
                for k, onehot in enumerate((onehot1, onehot2)):
                    dummy = const[:, C_DUMMY + k * NT:C_DUMMY + (k + 1) * NT]
                    link(dve.tensor_tensor(work[:, :, :], slot_tok[:, :, :], onehot[:, :, :], ALU.mult))
                    link(dve.tensor_reduce(col[:, :], work[:, :, :], AX.X, ALU.add))
                    link(dve.tensor_scalar(col2[:, :], col[:, :], 0.0, None, ALU.is_gt))
                    link(dve.tensor_tensor(route["weight"][k][:, :], chosen_logit[k][:, :], col2[:, :], ALU.mult))
                    link(dve.tensor_scalar(route["fetch"][k][:, :], col[:, :], -1.0, 0.0, ALU.add, ALU.max))
                    link(dve.scalar_tensor_tensor(col[:, :], col[:, :], -1.0, dummy, ALU.add, ALU.subtract))
                    link(dve.tensor_tensor(col[:, :], col[:, :], col2[:, :], ALU.mult))
                    dve.tensor_tensor(route["send"][k][:, :], col[:, :], dummy, ALU.add).then_inc(idx_ready, 1)
                    dve.wait_ge(idx_ready, k + 1)

            norm.on_vector(dve, x_tok)
            dve.wait_ge(gate_in, 32)
            dve.wait_ge(const_in, 16)
            shift_logits()
            ungated = None
            for event in EVENTS:
                kind, n = event
                if ungated is not None:
                    unit(ungated)
                    ungated = None
                if event == ("up", 0):
                    finish_gates()
                if event == ("up", 1):
                    best_gate(0, onehot1)
                if event == ("up", 2):
                    best_gate(1, onehot2)
                if event == ("up", 3):
                    order_keys()
                if event == ("up", 4):
                    lay_keys()
                first_round = rounds_of(event)
                if kind == "up":
                    for j in range(2):
                        end_round(first_round + j)
                    ungated = n
                else:
                    for tt in range(BANK // P):
                        for j in range(2):
                            end_round(first_round + 2 * tt + j)
                        add_tile(BANK // P * n + tt)
                if event == ("up", KEYS_AT):
                    take_keys()
                if event == OFFS_AT:
                    place()
                if event == TURN_AT:
                    address()


def run_experts(nc, a, keep, slots_in_dram, slots_out_dram):
    with ExitStack() as scope:
        m = Memory(nc, scope)
        ident = keep["ident"]
        w1, w3 = ([m.sb(f"{n}_{i}", [P, DC, F]) for i in range(2)] for n in ("ew1", "ew3"))
        w2 = [m.sb(f"ew2_{i}", [P, FC, D]) for i in range(2)]
        rows = [m.sb(f"slot_rows{i}", [P, CAP_TILES, D]) for i in range(2)]
        rowsT = [m.sb(f"slot_rowsT{i}", [P, DC, CAP]) for i in range(2)]
        silu = [m.sb(f"esilu{i}", [P, CAP]) for i in range(2)]
        hidden = [m.sb(f"ehidden{i}", [P, FC, CAP]) for i in range(2)]
        y_sb = [m.sb(f"y_sb{i}", [P, CAP_TILES, D]) for i in range(2)]
        gu = [m.ps(f"egu{i}", [P, 2, BANK]) for i in range(2)]
        turn = m.ps("eturn", [P, DC, BANK])
        y_bank = [m.ps(f"ey_bank{i}", [P, BANK]) for i in range(2)]

        w_in = [m.sem(f"expert_w_in{i}") for i in range(2)]
        rows_in = [m.sem(f"rows_in{i}") for i in range(2)]
        turned, rowsT_ready = m.sem("rows_turned"), m.sem("rowsT_ready")
        gu_ready, silu_done = m.sem("egu_ready"), m.sem("esilu_done")
        h_done = m.sem("eh_done")
        y_ready, y_copied = m.sem("ey_ready"), m.sem("ey_copied")
        y_out = [m.sem(f"y_out{i}") for i in range(2)]
        TAIL_CAP = CAP - (CAP_TILES - 1) * P
        full = CAP_TILES - 1
        sizes = [P] * full + [TAIL_CAP]

        block = scope.enter_context(nc.Block())

        def expert_slots(dram, e, t):
            return dram[bass.ds(e * CAP + t * P, sizes[t]), :]

        @block.sync
        def _(sp):
            def load(e, i):
                sp.dma_start(w1[i][:, :, :], a["ew1"][bass.ds(e, 1)].rearrange("o (c p) f -> p (o c) f", p=P)).then_inc(w_in[i], 16)
                sp.dma_start(w3[i][:, :, :], a["ew3"][bass.ds(e, 1)].rearrange("o (c p) f -> p (o c) f", p=P)).then_inc(w_in[i], 16)
                sp.dma_start(w2[i][:, :, :], a["ew2"][bass.ds(e, 1)].rearrange("o (c p) f -> p (o c) f", p=P)).then_inc(w_in[i], 16)

            def load_rows(e, i):
                for t in range(CAP_TILES):
                    sp.dma_start(rows[i][0:sizes[t], t, :], expert_slots(slots_in_dram, e, t)).then_inc(rows_in[i], 16)

            def store(e, i):
                sp.wait_ge(y_copied, CAP_TILES * (e + 1) + 2)
                for t in range(CAP_TILES):
                    sp.dma_start(expert_slots(slots_out_dram, e, t), y_sb[i][0:sizes[t], t, :]).then_inc(y_out[i], 16)

            for i in range(2):
                sp.sem_inc(y_out[i], 1)
                load_rows(i, i)
                load(i, i)
            with sp.Fori(0, E // 2 - 1) as r:
                for i in range(2):
                    e = 2 * r + i
                    sp.wait_ge(y_ready, CAP_TILES * (e + 1))
                    load(e + 2, i)
                    load_rows(e + 2, i)
                    store(e, i)
            for i in range(2):
                store(E - 2 + i, i)
            for i in range(2):
                sp.wait_ge(y_out[i], 16 * CAP_TILES * (E // 2) + 1)

        @block.tensor
        def _(pe):
            def turn_rows(e, i, r):
                pe.wait_ge(rows_in[i], 16 * CAP_TILES * (r + 1))
                if not isinstance(e, int) or e > 0:
                    pe.wait_ge(rowsT_ready, DC * e)
                for c in range(DC):
                    for t, n in enumerate(sizes):
                        last = pe.transpose(turn[:, c, t * P:t * P + n], rows[i][0:n, t, c * P:(c + 1) * P],
                                            ident[0:n, 0:n])
                    last.then_inc(turned, 1)

            def up(e, i, r):
                pe.wait_ge(rowsT_ready, DC * (e + 1))
                pe.wait_ge(w_in[i], 48 * (r + 1))
                for f in range(FC):
                    pe.wait_ge(h_done, FC * e + f + 1)
                    for j, w in enumerate((w1, w3)):
                        for c in range(DC):
                            last = pe.matmul(gu[f % 2][:, j, 0:CAP], w[i][:, c, f * P:(f + 1) * P], rowsT[i][:, c, :],
                                             start=(c == 0), stop=(c == DC - 1))
                    last.then_inc(gu_ready, 1)

            def down(e, i):
                pe.wait_ge(h_done, FC * (e + 1) + 2)
                for t, n in enumerate(sizes):
                    pe.wait_ge(y_copied, CAP_TILES * e + t + 1)
                    for f in range(FC):
                        last = pe.matmul(y_bank[(CAP_TILES * i + t) % 2][0:n, 0:D], hidden[i][:, f, t * P:t * P + n],
                                         w2[i][:, f, :], start=(f == 0), stop=(f == FC - 1))
                    last.then_inc(y_ready, 1)

            turn_rows(0, 0, 0)
            with pe.Fori(0, E // 2 - 1) as r:
                for i in range(2):
                    e = 2 * r + i
                    up(e, i, r)
                    turn_rows(e + 1, 1 - i, r + i)
                    down(e, i)
            r = E // 2 - 1
            up(E - 2, 0, r)
            turn_rows(E - 1, 1, r)
            down(E - 2, 0)
            up(E - 1, 1, r)
            down(E - 1, 1)

        @block.scalar
        def _(act):
            act.sem_inc(y_copied, 2)

            def copy_turned(e, i):
                for c in range(DC):
                    act.wait_ge(turned, DC * e + c + 1)
                    act.activation(rowsT[i][:, c, :], turn[:, c, 0:CAP], ACT.Copy).then_inc(rowsT_ready, 1)

            def activate(e, i):
                for f in range(FC):
                    act.wait_ge(gu_ready, FC * e + f + 1)
                    act.wait_ge(h_done, FC * e + f + 1)
                    act.activation(silu[f % 2][:, :], gu[f % 2][:, 0, 0:CAP], ACT.Silu).then_inc(silu_done, 1)

            def copy_out(e, i, r):
                act.wait_ge(y_out[i], 16 * CAP_TILES * r + 1)
                for t, n in enumerate(sizes):
                    act.wait_ge(y_ready, CAP_TILES * e + t + 1)
                    act.activation(y_sb[i][0:n, t, :], y_bank[(CAP_TILES * i + t) % 2][0:n, 0:D], ACT.Copy
                                   ).then_inc(y_copied, 1)

            copy_turned(0, 0)
            with act.Fori(0, E // 2 - 1) as r:
                for i in range(2):
                    e = 2 * r + i
                    activate(e, i)
                    copy_turned(e + 1, 1 - i)
                    copy_out(e, i, r)
            activate(E - 2, 0)
            copy_turned(E - 1, 1)
            copy_out(E - 2, 0, E // 2 - 1)
            activate(E - 1, 1)
            copy_out(E - 1, 1, E // 2 - 1)

        @block.vector
        def _(dve):
            dve.sem_inc(h_done, 2)

            def gate(e, i):
                for f in range(FC):
                    dve.wait_ge(silu_done, FC * e + f + 1)
                    dve.tensor_tensor(hidden[i][:, f, :], silu[f % 2][:, :], gu[f % 2][:, 1, 0:CAP], ALU.mult
                                      ).then_inc(h_done, 1)

            with dve.Fori(0, E // 2) as r:
                for i in range(2):
                    gate(2 * r + i, i)



QK = 64
ZQ = 256
ZB = N // ZQ
ZT = ZQ // P
HID = 1024
HC = HID // P
RMS_EPS, QUANT_EPS = 1e-6, 1e-5
ROUND = 12582912.0
LEVELS = 127.0


def combine_and_attend(nc, a, keep, x_tok, slots_out_dram, route):
    with ExitStack() as scope:
        m = Memory(nc, scope)
        ident = keep["ident"]
        got = [m.sb(f"got{k}", [P, NT, D]) for k in range(TOP)]
        ctxT = m.sb("ctxT_1", [P, DC, S])
        wq, wk = m.sb("wq_1", [P, DC, QK]), m.sb("wk_1", [P, DC, QK])
        wv = m.sb("wv_1", [P, DC, D])
        bq, bk, bv = m.sb("bq_1", [QK, 1]), m.sb("bk_1", [QK, 1]), m.sb("bv_1", [P, D])
        qT, kT = m.sb("qT_1", [P, N]), m.sb("kT_1", [P, S])
        v = m.sb("v_1", [P, KT, D])
        norm = Norm(m, "ln3", got[0])
        tokT = m.sb("tokT_1", [P, DC, N])
        z = [m.sb(f"z{i}", [P, KT, ZQ]) for i in range(2)]
        bank = [m.ps(f"l1_bank{i}", [P, BANK]) for i in range(4)]
        z_bank = [m.ps(f"z_bank{i}", [P, BANK]) for i in range(2)]
        o_bank = [m.ps(f"o_bank{i}", [P, BANK]) for i in range(2)]

        fetched = [m.sem(f"fetched{g}") for g in range(NORM_GROUPS)]
        added, padded = m.sem("expert_added"), m.sem("padded")
        kin, vin, qin = m.sem("k1_in"), m.sem("v1_in"), m.sem("q1_in")
        bank_full = m.sem("l1_bank_full")
        by_act, by_dve = m.sem("l1_bank_free_act"), m.sem("l1_bank_free_dve")
        z_ready, z_done = m.sem("z_ready"), m.sem("z_done")
        o_ready, o_done = m.sem("o_ready"), m.sem("o_done")

        FILLS_K = -(-S // BANK)
        FILLS_V = KT
        FILLS_T = DC * NT // 4
        FILLS_Q = N // BANK

        block = scope.enter_context(nc.Block())

        @block.gpsimd
        def _(pool):
            pool.memset(qT[QK:P, :], 0.0).then_inc(padded, 1)
            pool.wait_ge(padded, 1)
            pool.memset(kT[QK:P, :], 0.0).then_inc(padded, 1)
            for t in range(NT):
                for k in range(TOP):
                    pool.indirect_dma_start(
                        out=got[k][:, t, :], out_offset=None, in_=slots_out_dram[:, :],
                        in_offset=bass.IndirectOffsetOnAxis(ap=route["fetch"][k][:, t:t + 1], axis=0)
                    ).then_inc(fetched[t // NORM_GROUP], 16)

        @block.sync
        def _(sp):
            sp.dma_start(wk[:, :, :], a["wk1T"].rearrange("(c p) n -> p c n", p=P)).then_inc(kin, 16)
            sp.dma_start(bk[:, :], a["bk1"].rearrange("(p o) -> p o", o=1), allow_slow_non_contiguous=True).then_inc(kin, 16)
            sp.dma_start(ctxT[:, :, :], a["ctxT"].rearrange("(c p) n -> p c n", p=P)).then_inc(kin, 16)
            sp.dma_start(wv[:, :, :], a["wv1T"].rearrange("(c p) n -> p c n", p=P)).then_inc(vin, 16)
            sp.dma_start(bv[:, :], a["bv1"].partition_broadcast(P)).then_inc(vin, 16)
            sp.dma_start(wq[:, :, :], a["wq1T"].rearrange("(c p) n -> p c n", p=P)).then_inc(qin, 16)
            sp.dma_start(bq[:, :], a["bq1"].rearrange("(p o) -> p o", o=1), allow_slow_non_contiguous=True).then_inc(qin, 16)

        @block.tensor
        def _(pe):
            fills = 0

            def take_bank():
                if fills >= 4:
                    seen = fills - 3
                    pe.wait_ge(by_act, min(seen, FILLS_K) + max(0, seen - FILLS_K - FILLS_V))
                    if seen > FILLS_K:
                        pe.wait_ge(by_dve, min(seen - FILLS_K, FILLS_V))
                return bank[fills % 4]

            pe.wait_ge(kin, 48)
            for n0 in range(0, S, BANK):
                n1 = min(S, n0 + BANK)
                b = take_bank()
                for c in range(DC):
                    last = pe.matmul(b[0:QK, 0:n1 - n0], wk[:, c, :], ctxT[:, c, n0:n1], start=(c == 0), stop=(c == DC - 1))
                last.then_inc(bank_full, 1)
                fills += 1
            pe.wait_ge(vin, 32)
            for t in range(KT):
                b = take_bank()
                for c in range(DC):
                    last = pe.matmul(b[0:key_rows(t), 0:D], ctxT[:, c, t * P:t * P + key_rows(t)], wv[:, c, :],
                                     start=(c == 0), stop=(c == DC - 1))
                last.then_inc(bank_full, 1)
                fills += 1
            for g in range(NT // 4):
                pe.wait_ge(norm.norm_done, 4 * (g + 1))
                for c in range(DC):
                    b = take_bank()
                    for j in range(4):
                        last = pe.transpose(b[:, j * P:(j + 1) * P], norm.normed[:, 4 * g + j, c * P:(c + 1) * P], ident[:, :])
                    last.then_inc(bank_full, 1)
                    fills += 1
            pe.wait_ge(qin, 32)
            pe.wait_ge(by_act, FILLS_K + FILLS_T)
            for n0 in range(0, N, BANK):
                b = take_bank()
                for c in range(DC):
                    last = pe.matmul(b[0:QK, :], wq[:, c, :], tokT[:, c, n0:n0 + BANK], start=(c == 0), stop=(c == DC - 1))
                last.then_inc(bank_full, 1)
                fills += 1
            pe.wait_ge(by_act, FILLS_K + FILLS_T + FILLS_Q)
            pe.wait_ge(padded, 2)

            def score(b, i, t):
                rows = key_rows(t)
                pe.wait_ge(z_done, KT * b + t + 1)
                pe.matmul(z_bank[(KT * i + t) % 2][0:rows, 0:ZQ], kT[:, t * P:t * P + rows], qT[:, bass.ds(b * ZQ, ZQ)],
                          start=True, stop=True).then_inc(z_ready, 1)

            def weigh(b, i, k):
                tt, t = divmod(k, KT)
                rows = key_rows(t)
                if t == 0:
                    pe.wait_ge(o_done, ZT * b + tt + 1)
                if tt == 0:
                    pe.wait_ge(z_done, KT * b + t + 3)
                last = pe.matmul(o_bank[tt][:, 0:D], z[i][0:rows, t, tt * P:(tt + 1) * P], v[0:rows, t, :],
                                 start=(t == 0), stop=(t == KT - 1))
                if t == KT - 1:
                    last.then_inc(o_ready, 1)

            def block_step(b, i):
                for t in range(KT):
                    score(b, i, t)
                    for j in range(ZT):
                        weigh(b - 1, 1 - i, ZT * t + j)

            for t in range(KT):
                score(0, 0, t)
            with pe.Fori(0, ZB // 2 - 1) as r:
                block_step(2 * r + 1, 1)
                block_step(2 * r + 2, 0)
            block_step(ZB - 1, 1)
            for k in range(ZT * KT):
                weigh(ZB - 1, 1, k)

        @block.scalar
        def _(act):
            fills = 0
            act.sem_inc(z_done, 2)
            act.wait_ge(kin, 48)
            for n0 in range(0, S, BANK):
                n1 = min(S, n0 + BANK)
                act.wait_ge(bank_full, fills + 1)
                act.activation(kT[0:QK, n0:n1], bank[fills % 4][0:QK, 0:n1 - n0], ACT.Identity, bias=bk[:, 0:1]).then_inc(by_act, 1)
                fills += 1
            fills += FILLS_V
            norm.on_scalar(act, 0)
            for g in range(NT // 4):
                if g + 1 < NORM_GROUPS:
                    norm.on_scalar(act, g + 1)
                for c in range(DC):
                    act.wait_ge(bank_full, fills + 1)
                    act.activation(tokT[:, c, g * BANK:(g + 1) * BANK], bank[fills % 4][:, :], ACT.Copy).then_inc(by_act, 1)
                    fills += 1
            act.wait_ge(qin, 32)
            for n0 in range(0, N, BANK):
                act.wait_ge(bank_full, fills + 1)
                act.activation(qT[0:QK, n0:n0 + BANK], bank[fills % 4][0:QK, :], ACT.Identity, bias=bq[:, 0:1]).then_inc(by_act, 1)
                fills += 1

            def squash(b, i):
                for t in range(KT):
                    rows = key_rows(t)
                    act.wait_ge(z_ready, KT * b + t + 1)
                    act.activation(z[i][0:rows, t, :], z_bank[(KT * i + t) % 2][0:rows, 0:ZQ], ACT.Sigmoid, scale=QK ** -0.5
                                   ).then_inc(z_done, 1)

            squash(0, 0)
            squash(1, 1)
            with act.Fori(0, ZB // 2 - 1) as r:
                act.wait_ge(o_ready, ZT * (2 * r + 1))
                squash(2 * r + 2, 0)
                act.wait_ge(o_ready, ZT * (2 * r + 2))
                squash(2 * r + 3, 1)

        @block.vector
        def _(dve):
            dve.sem_inc(o_done, 2)
            dve.wait_ge(vin, 32)
            for t in range(KT):
                rows, f = key_rows(t), FILLS_K + t
                dve.wait_ge(bank_full, f + 1)
                dve.tensor_tensor(v[0:rows, t, :], bank[f % 4][0:rows, 0:D], bv[0:rows, :], ALU.add).then_inc(by_dve, 1)

            def add_fetched(g):
                dve.wait_ge(fetched[g], 16 * TOP * NORM_GROUP)
                first = TOP * NORM_GROUP * g
                for k in range(TOP):
                    for i in range(NORM_GROUP):
                        t = NORM_GROUP * g + i
                        if k:
                            dve.wait_ge(added, first + i + 1)
                        dve.scalar_tensor_tensor(x_tok[:, t, :], got[k][:, t, :], route["weight"][k][:, t:t + 1],
                                                 x_tok[:, t, :], ALU.mult, ALU.add).then_inc(added, 1)
                dve.wait_ge(added, first + TOP * NORM_GROUP)

            norm.on_vector(dve, x_tok, add_fetched)

            def add_out(b):
                for tt in range(ZT):
                    dve.wait_ge(o_ready, ZT * b + tt + 1)
                    xv = x_tok[:, bass.ds(b * ZT + tt, 1), :].rearrange("p o d -> p (o d)")
                    dve.tensor_tensor(xv, xv, o_bank[tt][:, 0:D], ALU.add).then_inc(o_done, 1)

            with dve.Fori(0, ZB) as b:
                add_out(b)


def feed_forward(nc, a, keep, x_tok, out):
    with ExitStack() as scope:
        m = Memory(nc, scope)
        ident_bf = keep["ident_bf"]
        w1, w2 = m.sb("ff_w1", [P, DC, HID]), m.sb("ff_w2", [P, HC, D])
        t1, t2 = m.sb("ternary1", [P, DC, HID], BF16), m.sb("ternary2", [P, HC, D], BF16)
        b1, b2 = m.sb("b1_rows", [P, HID]), m.sb("b2_rows", [P, D])
        ones = m.sb("ones_sq", [P, P])
        w_abs, w_mean, w_scale = m.sb("w_abs", [P, 2]), m.sb("w_mean", [P, 2]), m.sb("w_scale", [P, 2])
        q1 = m.sb("q1", [P, NT, D], BF16)
        q1T = m.sb("q1T", [P, DC, N], BF16)
        h = m.sb("h", [P, NT, HID])
        norm = Norm(m, "ln4", h[:, 0:NT * D // HID, :].rearrange("p t n -> p (t n)").rearrange("p (t d) -> p t d", t=NT))
        squares = m.sb("squares", [P, HID])
        q2f = [m.sb(f"q2f{i}", [P, HID]) for i in range(2)]
        q2 = [m.sb(f"q2_{i}", [P, HID], BF16) for i in range(2)]
        q2T = [m.sb(f"q2T_{i}", [P, HC, P], BF16) for i in range(2)]
        ssq, big, rstd, factor, back = ([m.sb(f"{n}{i}", [P, NT]) for i in range(2)] for n in
                                        ("ssq", "big", "rms", "factor", "back"))
        eps = m.sb("rms_eps", [P, 1])
        pre = [m.ps(f"pre{i}", [P, 2, BANK]) for i in range(2)]
        turn = [m.ps(f"fturn{i}", [P, 2 * BANK], BF16) for i in range(2)]
        y_bank = [m.ps(f"fy_bank{i}", [P, BANK]) for i in range(2)]

        w_in, b_in = m.sem("ff_w_in"), m.sem("ff_b_in")
        chain = m.sem("ff_chain")
        w_counted, w_summed = m.sem("w_counted"), m.sem("w_summed")
        squared, rooted = m.sem("squared"), m.sem("rooted")
        root_in = m.sem("root_in")
        quantized, tern_ready = m.sem("quantized"), m.sem("tern_ready")
        t_full, t_free = m.sem("ff_t_full"), m.sem("ff_t_free")
        b2_added = m.sem("b2_added")
        pre_ready, pre_read = m.sem("pre_ready"), m.sem("pre_read")
        gelu_done, h_seen = m.sem("gelu_done"), m.sem("h_seen")
        rounded, q2_ready = m.sem("rounded"), m.sem("q2_ready")
        turned2, q2T_ready = m.sem("turned2"), m.sem("q2T_ready")
        y_ready, y_done = m.sem("fy_ready"), m.sem("fy_done")
        stored = m.sem("stored")

        GT = 4

        block = scope.enter_context(nc.Block())

        @block.sync
        def _(sp):
            sp.dma_start(w1[:, :, :], a["w1T"].rearrange("(c p) n -> p c n", p=P)).then_inc(w_in, 16)
            sp.dma_start(w2[:, :, :], a["w2T"].rearrange("(c p) n -> p c n", p=P)).then_inc(w_in, 16)
            sp.dma_start(b1[:, :], a["b1"].partition_broadcast(P)).then_inc(b_in, 16)
            sp.dma_start(b2[:, :], a["b2"].partition_broadcast(P)).then_inc(b_in, 16)
            for g in range(NT // GT):
                sp.wait_ge(y_done, GT * (g + 1) + 2)
                sp.dma_start(out.rearrange("b (t p) d -> p (b t) d", p=P)[:, GT * g:GT * (g + 1), :],
                             x_tok[:, GT * g:GT * (g + 1), :]).then_inc(stored, 16)
            sp.wait_ge(stored, 16 * (NT // GT))

        @block.gpsimd
        def _(pool):
            pool.wait_ge(b_in, 32)
            pool.wait_ge(norm.norm_done, NT)
            for t in range(NT):
                if t:
                    pool.wait_ge(b2_added, t)
                pool.tensor_tensor(x_tok[:, t, :], x_tok[:, t, :], b2[:, :], ALU.add).then_inc(b2_added, 1)

        @block.tensor
        def _(pe):
            pe.wait_ge(w_counted, 3)
            pe.matmul(y_bank[0][:, 0:2], ones[:, :], w_abs[:, :], start=True, stop=True).then_inc(w_summed, 1)
            for f in range(DC * NT // GT):
                g, c = divmod(f, DC)
                pe.wait_ge(quantized, GT * (g + 1))
                if f >= 2:
                    pe.wait_ge(t_free, f - 1)
                for j in range(GT):
                    last = pe.transpose(turn[f % 2][:, j * P:(j + 1) * P], q1[:, GT * g + j, c * P:(c + 1) * P],
                                        ident_bf[:, :])
                last.then_inc(t_full, 1)
            pe.wait_ge(t_free, DC * NT // GT)
            pe.wait_ge(tern_ready, 2)
            with pe.Fori(0, NT // 2) as r:
                for i in range(2):
                    pe.wait_ge(pre_read, 2 * r + i + 1)
                    for half in range(2):
                        for c in range(DC):
                            last = pe.matmul(pre[i][:, half, :],
                                             q1T[:, c, bass.ds(r * (2 * P) + i * P, P)],
                                             t1[:, c, half * BANK:(half + 1) * BANK], start=(c == 0), stop=(c == DC - 1))
                    last.then_inc(pre_ready, 1)

            def turn_hidden(t, i):
                pe.wait_ge(q2_ready, t + 1)
                if not isinstance(t, int) or t >= 2:
                    pe.wait_ge(q2T_ready, t - 1)
                for c in range(HC):
                    last = pe.transpose(turn[i][:, c * P:(c + 1) * P], q2[i][:, c * P:(c + 1) * P], ident_bf[:, :])
                last.then_inc(turned2, 1)

            def down(t, i):
                pe.wait_ge(q2T_ready, t + 1)
                pe.wait_ge(y_done, t + 1)
                for c in range(HC):
                    last = pe.matmul(y_bank[i][:, 0:D], q2T[i][:, c, :], t2[:, c, :], start=(c == 0), stop=(c == HC - 1))
                last.then_inc(y_ready, 1)

            turn_hidden(0, 0)
            turn_hidden(1, 1)
            with pe.Fori(0, NT // 2 - 1) as r:
                for i in range(2):
                    down(2 * r + i, i)
                    turn_hidden(2 * r + i + 2, i)
            down(NT - 2, 0)
            down(NT - 1, 1)

        @block.scalar
        def _(act):
            norm.on_scalar(act, 0)
            for t in range(NT):
                if t % NORM_GROUP == 0 and t // NORM_GROUP + 1 < NORM_GROUPS:
                    norm.on_scalar(act, t // NORM_GROUP + 1)
                act.wait_ge(norm.norm_done, t + 1)
                if t:
                    act.wait_ge(squared, t)
                act.activation(squares[:, 0:D], norm.normed[:, t, :], ACT.Square, accum_out=ssq[0][:, t:t + 1]).then_inc(squared, 1)
            act.wait_ge(squared, NT)
            act.wait_ge(root_in, 1)
            act.activation(rstd[0][:, :], ssq[0][:, :], ACT.Sqrt, bias=eps[:, 0:1], scale=1.0 / D).then_inc(rooted, 1)
            for f in range(DC * NT // GT):
                g, c = divmod(f, DC)
                act.wait_ge(t_full, f + 1)
                act.activation(q1T[:, c, g * BANK:(g + 1) * BANK], turn[f % 2][:, 0:BANK], ACT.Copy).then_inc(t_free, 1)
            with act.Fori(0, NT) as t:
                act.wait_ge(pre_read, t + 3)
                hv = h[:, bass.ds(t, 1), :].rearrange("p o d -> p (o d)")
                act.activation(hv, hv, ACT.Gelu).then_inc(gelu_done, 1)
                act.wait_ge(gelu_done, t + 1)
                act.wait_ge(squared, t + NT)
                act.activation(squares[:, :], hv, ACT.Square, accum_out=ssq[1][:, bass.ds(t, 1)]).then_inc(squared, 1)
            act.wait_ge(squared, 2 * NT)
            act.activation(rstd[1][:, :], ssq[1][:, :], ACT.Sqrt, bias=eps[:, 0:1], scale=1.0 / HID).then_inc(rooted, 1)

            def to_bf16(t, i):
                act.wait_ge(rounded, t + 1)
                act.activation(q2[i][:, :], q2f[i][:, :], ACT.Copy, bias=-ROUND).then_inc(q2_ready, 1)

            def copy_turned(t, i):
                act.wait_ge(turned2, t + 1)
                act.activation(q2T[i][:, :, :].rearrange("p c n -> p (c n)"), turn[i][:, :], ACT.Copy).then_inc(q2T_ready, 1)

            to_bf16(0, 0)
            to_bf16(1, 1)
            copy_turned(0, 0)
            copy_turned(1, 1)
            with act.Fori(0, NT // 2 - 1) as r:
                for i in range(2):
                    to_bf16(2 * r + i + 2, i)
                    act.wait_ge(y_ready, 2 * r + i + 1)
                    copy_turned(2 * r + i + 2, i)

        @block.vector
        def _(dve):
            made = 0

            def link(ins):
                nonlocal made
                made += 1
                ins.then_inc(chain, 1)
                dve.wait_ge(chain, made)

            def scales(i):
                link(dve.reciprocal(rstd[i][:, :], rstd[i][:, :]))
                link(dve.tensor_tensor(back[i][:, :], big[i][:, :], rstd[i][:, :], ALU.mult))
                link(dve.tensor_scalar(back[i][:, :], back[i][:, :], QUANT_EPS, 1.0 / LEVELS, ALU.max, ALU.mult))
                link(dve.reciprocal(factor[i][:, :], back[i][:, :]))
                link(dve.tensor_tensor(factor[i][:, :], factor[i][:, :], rstd[i][:, :], ALU.mult))
                link(dve.tensor_scalar(back[i][:, :], back[i][:, :], w_mean[:, i:i + 1], None, ALU.mult))

            link(dve.memset(eps[:, :], RMS_EPS))
            norm.on_vector(dve, x_tok)
            for t in range(NT):
                dve.wait_ge(norm.norm_done, t + 1)
                dve.tensor_reduce(big[0][:, t:t + 1], norm.normed[:, t, :], AX.X, ALU.max, apply_absolute_value=True
                                  ).then_inc(root_in, 1)
            dve.memset(ones[:, :], 1.0).then_inc(w_counted, 1)
            dve.wait_ge(w_in, 32)
            for i, w in enumerate((w1, w2)):
                dve.tensor_reduce(w_abs[:, i:i + 1], w[:, :, :].rearrange("p c n -> p (c n)"), AX.X, ALU.add,
                                  apply_absolute_value=True).then_inc(w_counted, 1)
            dve.wait_ge(w_summed, 1)
            link(dve.tensor_scalar(w_mean[:, :], y_bank[0][:, 0:2], 1.0 / (D * HID), QUANT_EPS, ALU.mult, ALU.max))
            link(dve.reciprocal(w_scale[:, :], w_mean[:, :]))
            dve.wait_ge(rooted, 1)
            dve.wait_ge(root_in, NT)
            scales(0)
            for t in range(NT):
                if t >= 2:
                    dve.wait_ge(quantized, t - 1)
                link(dve.tensor_scalar(q2f[t % 2][:, 0:D], norm.normed[:, t, :], factor[0][:, t:t + 1], ROUND, ALU.mult, ALU.add))
                link(dve.tensor_scalar(q2f[t % 2][:, 0:D], q2f[t % 2][:, 0:D], ROUND + LEVELS, ROUND - LEVELS - 1,
                                       ALU.min, ALU.max))
                dve.tensor_scalar(q1[:, t, :], q2f[t % 2][:, 0:D], -ROUND, None, ALU.add).then_inc(quantized, 1)
            for i, (w, tern) in enumerate(((w1, t1), (w2, t2))):
                flat = w[:, :, :].rearrange("p c n -> p (c n)")
                link(dve.tensor_scalar(flat, flat, w_scale[:, i:i + 1], ROUND, ALU.mult, ALU.add))
                link(dve.tensor_scalar(flat, flat, ROUND + 1.0, ROUND - 1.0, ALU.min, ALU.max))
                dve.tensor_scalar(tern[:, :, :].rearrange("p c n -> p (c n)"), flat, -ROUND, None, ALU.add
                                  ).then_inc(tern_ready, 1)
            dve.wait_ge(b_in, 32)
            dve.sem_inc(pre_read, 2)
            dve.sem_inc(y_done, 2)

            def bias(t, i):
                dve.wait_ge(pre_ready, t + 1)
                dve.scalar_tensor_tensor(h[:, bass.ds(t, 1), :].rearrange("p o (a n) -> p (o a) n", a=2), pre[i][:, :, :],
                                         back[0][:, bass.ds(t, 1)], b1[:, :].rearrange("p (a n) -> p a n", a=2),
                                         ALU.mult, ALU.add).then_inc(pre_read, 1)

            def largest(t):
                dve.wait_ge(gelu_done, t + 1)
                dve.tensor_reduce(big[1][:, bass.ds(t, 1)], h[:, bass.ds(t, 1), :].rearrange("p o d -> p (o d)"), AX.X,
                                  ALU.max, apply_absolute_value=True).then_inc(h_seen, 1)

            dve.wait_ge(quantized, NT)
            dve.wait_ge(squared, NT)
            bias(0, 0)
            bias(1, 1)
            with dve.Fori(0, NT // 2 - 1) as r:
                for i in range(2):
                    largest(2 * r + i)
                    bias(2 * r + i + 2, i)
            largest(NT - 2)
            largest(NT - 1)
            dve.wait_ge(rooted, 2)
            dve.wait_ge(h_seen, NT)
            scales(1)

            def quantize(t, i):
                if not isinstance(t, int) or t >= 2:
                    dve.wait_ge(q2_ready, t - 1)
                hv = h[:, bass.ds(t, 1), :].rearrange("p o d -> p (o d)")
                dve.tensor_scalar(hv, hv, factor[1][:, bass.ds(t, 1)], ROUND, ALU.mult, ALU.add).then_inc(h_seen, 1)
                dve.wait_ge(h_seen, t + NT + 1)
                dve.tensor_scalar(q2f[i][:, :], hv, ROUND + LEVELS, ROUND - LEVELS - 1, ALU.min, ALU.max
                                  ).then_inc(rounded, 1)

            def finish(t, i):
                dve.wait_ge(y_ready, t + 1)
                xv = x_tok[:, bass.ds(t, 1), :].rearrange("p o d -> p (o d)")
                dve.scalar_tensor_tensor(xv, y_bank[i][:, 0:D], back[1][:, bass.ds(t, 1)], xv, ALU.mult, ALU.add
                                         ).then_inc(y_done, 1)

            dve.wait_ge(b2_added, NT)
            for t in range(2):
                quantize(t, t)
            with dve.Fori(0, NT // 2 - 1) as r:
                for i in range(2):
                    quantize(2 * r + i + 2, i)
                    finish(2 * r + i, i)
            finish(NT - 2, 0)
            finish(NT - 1, 1)


def build(nc, a, out):
    q_parts_dram = nc.dram_tensor("q_parts", (3, D, N), BF16, kind="Internal").ap()
    k_parts_dram = nc.dram_tensor("k_parts", (3, D, S), BF16, kind="Internal").ap()
    with ExitStack() as scope:
        m = Memory(nc, scope)
        x_tok = m.sb("x_tok", [P, NT, D])
        ident, ident_bf = m.sb("ident", [P, P]), m.sb("ident_bf", [P, P], BF16)
        with ExitStack() as inner:
            mi = Memory(nc, inner)
            values = mi.sb("values", [P, GROUPS * KT * HG * HEAD_PE])
            keep = {
                "ident": ident, "ident_bf": ident_bf,
                "q_aug": mi.sb("q_aug", [P, RING, HG * BANK], BF16),
                "k_aug": mi.sb("k_aug", [P, H, S], BF16),
                "values_flat": values,
                "values": values[:, :].rearrange("p (g t h w) -> p g t h w", g=GROUPS, t=KT, h=HG),
            }
            project(nc, a, keep, x_tok, q_parts_dram, k_parts_dram)
            attend(nc, keep, x_tok, q_parts_dram)
        slots_in = nc.dram_tensor("slots_in", (SLOTS + TOP * N, D), F32, kind="Internal").ap()
        slots_out = nc.dram_tensor("slots_out", (SLOTS, D), F32, kind="Internal").ap()
        route = {
            "send": [m.sb(f"send{k}", [P, NT], U32) for k in range(TOP)],
            "fetch": [m.sb(f"fetch{k}", [P, NT], U32) for k in range(TOP)],
            "weight": [m.sb(f"weight{k}", [P, NT]) for k in range(TOP)],
        }
        keep = {"ident": ident, "ident_bf": ident_bf}
        with ExitStack() as inner:
            normed = Memory(nc, inner).sb("ln2_normed", [P, NT, D])
            route_and_share(nc, a, keep, x_tok, normed, slots_in, route)
        run_experts(nc, a, keep, slots_in, slots_out)
        combine_and_attend(nc, a, keep, x_tok, slots_out, route)
        feed_forward(nc, a, keep, x_tok, out)


def kernel(**inputs):
    import numpy as _np
    import concourse.bacc as _bacc
    from concourse import mybir as _mybir
    from concourse.bass_utils import run_bass_kernel_spmd as _run

    given = {k: _np.asarray(v) for k, v in inputs.items()}
    laid = {
        "x": given["x"],
        "ctxT": given["ctx_1024"][0].T,
        "mask": given["mask_BxS2_ik0"],
        "wqT": given["L0_xattn_Wq"].T,
        "wkT": given["L0_xattn_Wk"].T,
        "wvT": given["L0_xattn_Wv"].T,
        "bq": given["L0_xattn_bq"],
        "bk": given["L0_xattn_bk"],
        "bv": given["L0_xattn_bv"],
        "gate_w": given["L0_ffn_gate_w"],
        "gate_b": given["L0_ffn_gate_b"],
        "ew1": given["L0_ffn_ew1"],
        "ew3": given["L0_ffn_ew3"],
        "ew2": given["L0_ffn_ew2"],
        "sw1": given["L0_ffn_sw1"],
        "sw3": given["L0_ffn_sw3"],
        "sw2": given["L0_ffn_sw2"],
        "wq1T": given["L1_xattn_Wq"].T,
        "wk1T": given["L1_xattn_Wk"].T,
        "wv1T": given["L1_xattn_Wv"].T,
        "bq1": given["L1_xattn_bq"],
        "bk1": given["L1_xattn_bk"],
        "bv1": given["L1_xattn_bv"],
        "w1T": given["L1_ffn_w1"].T,
        "b1": given["L1_ffn_b1"],
        "w2T": given["L1_ffn_w2"].T,
        "b2": given["L1_ffn_b2"],
        "const": shape_constants(_np),
    }
    nc = _bacc.Bacc("TRN2", target_bir_lowering=False, num_devices=1)
    arrays, aps = {}, {}
    for name, a in laid.items():
        a = _np.ascontiguousarray(a)
        arrays[f"in_{name}"] = a
        aps[name] = nc.dram_tensor(f"in_{name}", a.shape, _mybir.dt.from_np(a.dtype), kind="ExternalInput").ap()
    out = nc.dram_tensor("out_x", (1, N, D), F32, kind="ExternalOutput").ap()
    build(nc, aps, out)
    r = _run(nc, [arrays], core_ids=[0])
    return r.results[0]["out_x"]
```

```python
from contextlib import ExitStack

import concourse.bass as bass
from concourse import mybir

F32 = mybir.dt.float32
BF16 = mybir.dt.bfloat16
I32 = mybir.dt.int32
U32 = mybir.dt.uint32
ALU = mybir.AluOpType
ACT = mybir.ActivationFunctionType
AX = mybir.AxisListType

P = 128
BANK = 512

N = 2048
D = 256
DC = D // P
NT = N // P
S = 1601
KT = -(-S // P)
TAIL = S - (KT - 1) * P
EPS_LN = 1e-5

H = 16
W = D // H
GROUPS = 4
HG = H // GROUPS
QB = N // BANK
STEPS = GROUPS * QB
QT = BANK // P
HEAD_PE = 32

THIRDS_K = (0, 1, 0, 2, 0, 1)
THIRDS_Q = (0, 0, 1, 0, 2, 1)
ROWS_PROD = W * len(THIRDS_K)
ROWS_MASKED = ROWS_PROD + 2
ROWS_ALL = ROWS_MASKED + 3
Q_LOAD = 16 * len(THIRDS_Q)
MASK_RAW = 10000.0 * W ** 0.5
SCORE_SCALE = W ** -0.5

WHOLE = S // BANK
REST = S - WHOLE * BANK
RING = 4
CHUNKS_QT = HG * WHOLE + 1
CHUNKS = QT * CHUNKS_QT
BANKS = 3
SLOT_LAST = 3
PLACES = KT * HG
LEAD = 18


def key_rows(t):
    return P if t < KT - 1 else TAIL


def sub(flat, start, count):
    return flat[:, bass.ds(start, count)]


class Memory:

    def __init__(self, nc, scope):
        self.nc, self.scope = nc, scope

    def sb(self, name, shape, dt=F32):
        return self.scope.enter_context(self.nc.sbuf_tensor(name, shape, dt))

    def ps(self, name, shape, dt=F32):
        return self.scope.enter_context(self.nc.psum_tensor(name, shape, dt))

    def sem(self, name):
        return self.scope.enter_context(self.nc.semaphore(name))


def make_identity(pool, ident, zeroed, made):
    pool.memset(ident[:, :], 0.0).then_inc(zeroed, 1)
    pool.wait_ge(zeroed, 1)
    pool.affine_select(out=ident[:, :], in_=ident[:, :], compare_op=ALU.not_equal, fill=1.0, base=0,
                       pattern=[[-1, P]], channel_multiplier=1).then_inc(made, 1)


def load_step_queries(sp, q_aug, q_parts_dram, count, done):
    for r, i in enumerate(THIRDS_Q):
        sp.dma_start(
            q_aug[W * r:W * (r + 1), bass.ds(count % RING * (HG * BANK), HG * BANK)].rearrange("p (h n) -> p h n", h=HG),
            q_parts_dram[i, bass.ds(count // QB * (HG * W), HG * W), bass.ds(count % QB * BANK, BANK)
                         ].rearrange("(h w) n -> w h n", h=HG)
        ).then_inc(done, 16)


def project(nc, a, keep, x_tok, q_parts_dram, k_parts_dram):
    with ExitStack() as scope:
        m = Memory(nc, scope)
        ctxT = m.sb("ctxT", [P, DC, S])
        wq, wk, wv = (m.sb(f"w{c}_0", [P, DC, D]) for c in "qkv")
        bq, bk = m.sb("bq_col", [P, DC]), m.sb("bk_col", [P, DC])
        bv = m.sb("bv_rows", [P, D])
        mask_i = m.sb("mask_int", [1, S], I32)
        mask_raw = mask_i[:, :].bitcast(F32)
        mask_hi = m.sb("mask_hi", [1, S], BF16)
        mask_lo = m.sb("mask_lo", [1, S], BF16)
        normed = m.sb("normed", [P, NT, D])
        norm = Norm(m, "ln1", normed)
        normedT = m.sb("normedT", [P, DC, N])
        full = [m.sb(f"full{i}", [P, BANK]) for i in range(2)]
        thirds = [m.sb(f"thirds{i}", [P, 3, BANK], BF16) for i in range(4)]
        bank = [m.ps(f"proj_bank{i}", [P, BANK]) for i in range(4)]

        x_in = [m.sem(f"x_in{g}") for g in range(NORM_GROUPS)]
        ctx_in, mask_in = m.sem("ctx_in"), m.sem("mask_in")
        wq_in, wk_in, wv_in, b_in, bv_in = (m.sem(s) for s in ("wq_in", "wk_in", "wv_in", "b_in", "bv_in"))
        ident_zero, ident_made = m.sem("ident_zero"), m.sem("ident_made")
        bank_full, bank_free_act, bank_free_dve = m.sem("bank_full"), m.sem("bank_free_act"), m.sem("bank_free_dve")
        split, mask_split = m.sem("split"), m.sem("mask_split")
        thirds_out = [m.sem(f"thirds_out{i}") for i in range(4)]
        steps, aug_set, values_set = m.sem("own_steps"), m.sem("aug_set"), m.sem("values_set")
        aug_in, rest_in, q_in = keep["aug_in"], keep["rest_in"], keep["q_in"]

        FILLS_T = DC * (NT // 4)
        PIECES = [(which, mm, n0, min(width, n0 + BANK)) for which, width in (("k", S), ("q", N))
                  for mm in range(DC) for n0 in range(0, width, BANK)]
        PIECES_K = sum(piece[0] == "k" for piece in PIECES)
        FIRST_K = PIECES_K // DC

        n_act = FILLS_T + len(PIECES)

        block = scope.enter_context(nc.Block())

        @block.sync
        def _(sp):
            for g in range(NORM_GROUPS):
                part = slice(NORM_GROUP * g, NORM_GROUP * (g + 1))
                sp.dma_start(x_tok[:, part, :], a["x"].rearrange("b (t p) d -> p (b t) d", p=P)[:, part, :]
                             ).then_inc(x_in[g], 16)
            sp.dma_start(wk[:, :, :], a["wkT"].rearrange("(c p) n -> p c n", p=P)).then_inc(wk_in, 16)
            sp.dma_start(ctxT[:, :, :], a["ctxT"].rearrange("(c p) n -> p c n", p=P)).then_inc(ctx_in, 16)
            sp.dma_start(bk[:, :], a["bk"].rearrange("(c p) -> p c", p=P), allow_slow_non_contiguous=True).then_inc(b_in, 16)
            sp.dma_start(bq[:, :], a["bq"].rearrange("(c p) -> p c", p=P), allow_slow_non_contiguous=True).then_inc(b_in, 16)
            sp.dma_start(mask_i[:, :], a["mask"]).then_inc(mask_in, 16)
            sp.dma_start(wq[:, :, :], a["wqT"].rearrange("(c p) n -> p c n", p=P)).then_inc(wq_in, 16)
            sp.dma_start(wv[:, :, :], a["wvT"].rearrange("(c p) n -> p c n", p=P)).then_inc(wv_in, 16)
            sp.dma_start(bv[:, :], a["bv"].partition_broadcast(P)).then_inc(bv_in, 16)

            def load_keys(g, done):
                for r, i in enumerate(THIRDS_K):
                    sp.dma_start(keep["k_aug"][W * r:W * (r + 1), HG * g:HG * (g + 1), :],
                                 k_parts_dram[i, HG * W * g:HG * W * (g + 1), :].rearrange("(h w) n -> w h n", w=W)
                                 ).then_inc(done, 16)

            for j, (which, mm, n0, n1) in enumerate(PIECES):
                sp.wait_ge(split, j + 1)
                dram = k_parts_dram if which == "k" else q_parts_dram
                sp.dma_start(dram[:, mm * P:(mm + 1) * P, n0:n1].rearrange("i p n -> p i n"), thirds[j % 4][:, :, 0:n1 - n0]
                             ).then_inc(thirds_out[j % 4], 16)
                if j == FIRST_K - 1:
                    for i in range(4):
                        sp.wait_ge(thirds_out[i], 16 * ((j - i) // 4 + 1))
                    load_keys(0, aug_in)
                    sp.wait_ge(aug_set, 2)
                    sp.wait_ge(mask_split, 3)
                    for row, part in enumerate((mask_hi, mask_lo)):
                        sp.dma_start(keep["k_aug"][ROWS_PROD + row:ROWS_PROD + row + 1, :, :],
                                     part[:, :].rearrange("p (o n) -> p o n", o=1).broadcast_to([1, H, S])).then_inc(aug_in, 16)
                if j == PIECES_K:
                    sp.wait_ge(thirds_out[j % 4], 16 * (j // 4 + 1))
                    load_step_queries(sp, keep["q_aug_flat"], q_parts_dram, 0, q_in)
            for i in range(4):
                sp.wait_ge(thirds_out[i], 16 * (len(PIECES) // 4))
            for g in range(1, GROUPS):
                load_keys(g, rest_in)
            sp.wait_ge(aug_in, 16 * (len(THIRDS_K) + 2))
            sp.wait_ge(q_in, Q_LOAD)

        @block.gpsimd
        def _(pool):
            make_identity(pool, keep["ident"], ident_zero, ident_made)
            pool.wait_ge(ident_made, 1)
            pool.tensor_copy(keep["ident_bf"][:, :], keep["ident"][:, :]).then_inc(ident_made, 1)
            pool.wait_ge(ident_made, 2)
            pool.memset(keep["q_aug"][ROWS_PROD:P, :, :], 1.0).then_inc(aug_set, 1)
            pool.wait_ge(aug_set, 1)
            pool.memset(keep["k_aug"][ROWS_PROD:P, :, :], 1.0).then_inc(aug_set, 1)
            pool.wait_ge(aug_set, 2)
            pool.memset(keep["values_flat"][:, :], 0.0).then_inc(values_set, 1)
            pool.wait_ge(values_set, 1)
            pool.memset(keep["values"][:, :, :, :, W:W + 1], 1.0).then_inc(values_set, 1)

        @block.tensor
        def _(pe):
            fills = 0

            def take_bank():
                if fills >= 4:
                    seen = fills - 3
                    if seen <= n_act:
                        pe.wait_ge(bank_free_act, seen)
                    else:
                        pe.wait_ge(bank_free_act, n_act)
                        pe.wait_ge(bank_free_dve, seen - n_act)
                return bank[fills % 4]

            pe.wait_ge(ident_made, 1)
            for g in range(NT // 4):
                pe.wait_ge(norm.norm_done, 4 * (g + 1))
                for c in range(DC):
                    b = take_bank()
                    for j in range(4):
                        last = pe.transpose(b[:, j * P:(j + 1) * P], normed[:, 4 * g + j, c * P:(c + 1) * P],
                                            keep["ident"][:, :])
                    last.then_inc(bank_full, 1)
                    fills += 1
            for j, (which, mm, n0, n1) in enumerate(PIECES):
                src, w = (normedT, wq) if which == "q" else (ctxT, wk)
                if j == 0:
                    pe.wait_ge(ctx_in, 16)
                    pe.wait_ge(wk_in, 16)
                if j == PIECES_K:
                    pe.wait_ge(wq_in, 16)
                    pe.wait_ge(bank_free_act, FILLS_T)
                b = take_bank()
                for c in range(DC):
                    last = pe.matmul(b[:, 0:n1 - n0], w[:, c, mm * P:(mm + 1) * P], src[:, c, n0:n1],
                                     start=(c == 0), stop=(c == DC - 1))
                last.then_inc(bank_full, 1)
                fills += 1
            pe.wait_ge(wv_in, 16)
            for t in range(KT):
                b = take_bank()
                for c in range(DC):
                    last = pe.matmul(b[0:key_rows(t), 0:D], ctxT[:, c, t * P:t * P + key_rows(t)], wv[:, c, :],
                                     start=(c == 0), stop=(c == DC - 1))
                last.then_inc(bank_full, 1)
                fills += 1

        @block.scalar
        def _(act):
            norm.on_scalar(act, 0)
            fills = 0
            for g in range(NT // 4):
                if g + 1 < NORM_GROUPS:
                    norm.on_scalar(act, g + 1)
                for c in range(DC):
                    act.wait_ge(bank_full, fills + 1)
                    act.activation(normedT[:, c, g * BANK:(g + 1) * BANK], bank[fills % 4][:, :], ACT.Copy
                                   ).then_inc(bank_free_act, 1)
                    fills += 1
            act.wait_ge(b_in, 32)
            for j, (which, mm, n0, n1) in enumerate(PIECES):
                bias = bq if which == "q" else bk
                act.wait_ge(bank_full, fills + 1)
                if j >= 2:
                    act.wait_ge(split, j - 1)
                if j >= 4:
                    act.wait_ge(thirds_out[j % 4], 16 * (j // 4))
                act.activation(full[j % 2][:, 0:n1 - n0], bank[fills % 4][:, 0:n1 - n0], ACT.Identity,
                               bias=bias[:, mm:mm + 1])
                act.activation(thirds[j % 4][:, 0, 0:n1 - n0], bank[fills % 4][:, 0:n1 - n0], ACT.Identity,
                               bias=bias[:, mm:mm + 1]).then_inc(bank_free_act, 1)
                fills += 1

        @block.vector
        def _(dve):
            norm.on_vector(dve, x_tok, lambda g: dve.wait_ge(x_in[g], 16))
            dve.wait_ge(mask_in, 16)
            dve.tensor_scalar(mask_raw, mask_i[:, :], MASK_RAW, -MASK_RAW, ALU.mult, ALU.add).then_inc(mask_split, 1)
            dve.wait_ge(mask_split, 1)
            dve.tensor_copy(mask_hi[:, :], mask_raw).then_inc(mask_split, 1)
            dve.wait_ge(mask_split, 2)
            dve.tensor_tensor(mask_lo[:, :], mask_raw, mask_hi[:, :], ALU.subtract).then_inc(mask_split, 1)

            for j, (_, _, n0, n1) in enumerate(PIECES):
                whole = full[j % 2][:, 0:n1 - n0]
                t0, t1, t2 = (thirds[j % 4][:, i, 0:n1 - n0] for i in range(3))
                dve.wait_ge(bank_free_act, FILLS_T + j + 1)
                dve.tensor_tensor(whole, whole, t0, ALU.subtract).then_inc(steps, 1)
                dve.wait_ge(steps, 2 * j + 1)
                dve.tensor_copy(t1, whole).then_inc(steps, 1)
                dve.wait_ge(steps, 2 * j + 2)
                dve.tensor_tensor(t2, whole, t1, ALU.subtract).then_inc(split, 1)
            dve.wait_ge(bv_in, 16)
            dve.wait_ge(values_set, 1)
            for t in range(KT):
                rows = key_rows(t)
                f = n_act + t
                dve.wait_ge(bank_full, f + 1)
                dve.tensor_tensor(keep["values"][0:rows, :, t, :, 0:W],
                                  bank[f % 4][0:rows, 0:D].rearrange("p (g h w) -> p g h w", g=GROUPS, h=HG),
                                  bv[0:rows, :].rearrange("p (g h w) -> p g h w", g=GROUPS, h=HG),
                                  ALU.add).then_inc(bank_free_dve, 1)


def attend(nc, keep, x_tok, q_parts_dram):
    with ExitStack() as scope:
        m = Memory(nc, scope)
        q_aug = keep["q_aug_flat"]
        k_flat = keep["k_aug"][:, :, :].rearrange("p h n -> p (h n)")
        values = keep["values_flat"]
        ident, ident_bf = keep["ident"], keep["ident_bf"]
        vals = m.sb("group_values", [P, KT, HG, HEAD_PE])
        probs = [m.sb(f"probs{i}", [P, HG, BANK]) for i in range(SLOT_LAST + 1)]
        acc_sb = m.sb("acc_sb", [P, BANK])
        max_part = m.sb("max_part", [P, QT, HG, WHOLE + 1])
        max_raw = m.sb("max_raw", [P, QT, HG])
        max_rest = m.sb("max_rest", [P, QT, HG])
        max_thirds = m.sb("max_thirds", [P, QT, 3, HG], BF16)
        max_rows = m.sb("max_rows", [3 * HG, BANK], BF16)
        recip = m.sb("recip", [P, QT, HG])
        head_out = m.sb("head_out", [P, QT, HG, W])
        scores = [m.ps(f"scores{i}", [P, 2, BANK]) for i in range(2)]
        ring = [m.ps(f"ring{i}", [P, BANK]) for i in range(BANKS)]
        acc = m.ps("acc", [P, BANK])

        score_free = m.sem("score_free")
        q_in = keep["q_in"]
        score_ready = m.sem("score_ready")
        probs_free = m.sem("probs_free")
        ring_free = m.sem("ring_free")
        ring_ready = m.sem("ring_ready")
        acc_free = m.sem("acc_free")
        thirds_ready = m.sem("thirds_ready")
        added = m.sem("added")
        max_placed = m.sem("max_placed")
        vals_ready = m.sem("vals_ready")
        max_chain = m.sem("max_chain")
        out_chain = m.sem("out_chain")

        CHAIN_MAX = 4
        HALF = KT // 2 + 1
        SUMS_AT = 2 * HG + 2
        ROWS_LATER = 6

        def is_first(it):
            return isinstance(it, int) and it == 0

        def is_last(it):
            return isinstance(it, int) and it == STEPS - 1

        def entries_of(it, ahead):
            taken = 0 if is_first(it) else LEAD
            plan = [(1, c) for c in range(taken, CHUNKS)] if ahead >= 1 else []
            complete = len(plan)
            plan += [(2, c) for c in range(LEAD)] if ahead >= 2 else []
            if ahead >= 1:
                plan.insert(min(complete + ROWS_LATER, len(plan)), "rows")
            if not is_first(it):
                plan.insert(min(SUMS_AT, len(plan)), "sums")
            return plan

        BEFORE_FIRST = CHUNKS + 1
        IN_FIRST = len(entries_of(0, 2))
        IN_STEP = CHUNKS + 2
        assert IN_STEP % BANKS == 0

        def entries_before(it):
            if is_first(it):
                return BEFORE_FIRST
            if is_last(it):
                return entries_before(STEPS - 2) + len(entries_of(STEPS - 2, 1))
            return IN_STEP * it + BEFORE_FIRST + IN_FIRST - IN_STEP

        def bank_of(it, n):
            return ring[(entries_before(it if isinstance(it, int) else 1) + n) % BANKS]

        def sums_turned(it):
            return 1 if is_last(it) else SUMS_AT + 1

        ENTRIES = entries_before(STEPS - 1) + len(entries_of(STEPS - 1, 0)) + 1

        def slot_of(t):
            return SLOT_LAST if t == KT - 1 else t % SLOT_LAST

        def chunk_products(c):
            qt, part = divmod(c, CHUNKS_QT)
            if part < CHUNKS_QT - 1:
                return [(qt, part // WHOLE, part % WHOLE * BANK, BANK, 0)]
            return [(qt, h, WHOLE * BANK, REST, h * REST) for h in range(HG)]

        block = scope.enter_context(nc.Block())

        @block.tensor
        def _(pe):
            pe.sem_inc(probs_free, 3)
            pe.sem_inc(score_ready, 1)

            def max_chunk(bank, it, c):
                for qt, h, k0, n, at in chunk_products(c):
                    last = pe.matmul(bank[:, at:at + n],
                                     q_aug[0:ROWS_MASKED, bass.ds(it % RING * (HG * BANK) + h * BANK + qt * P, P)],
                                     k_flat[0:ROWS_MASKED, bass.ds(it // QB * (HG * S) + h * S + k0, n)],
                                     start=True, stop=True)
                last.then_inc(ring_ready, 1)

            def turn_rows(bank, count):
                pe.wait_ge(thirds_ready, count + 1)
                rows = bank[:, :].bitcast(BF16)
                for qt in range(QT):
                    last = pe.transpose(rows[0:3 * HG, qt * P:(qt + 1) * P],
                                        max_thirds[:, qt, :, :].rearrange("p a b -> p (a b)"), ident_bf[:, :])
                last.then_inc(ring_ready, 1)

            def turn_sums(bank, count):
                pe.wait_ge(acc_free, count + 2)
                for qt in range(QT):
                    last = pe.transpose(bank[:, qt * P:(qt + 1) * P], acc_sb[:, qt * P:(qt + 1) * P], ident[:, :])
                last.then_inc(ring_ready, 1)

            def score(it, t, h):
                pair, j = divmod(h, 2)
                rows = key_rows(t % KT)
                if j == 0:
                    pe.wait_ge(score_free, 2 * KT * it + 2 * t + pair + 1)
                at = it + t // KT
                last = pe.matmul(scores[pair][0:rows, j, :],
                                 k_flat[0:ROWS_ALL, bass.ds(at // QB * (HG * S) + h * S + t % KT * P, rows)],
                                 q_aug[0:ROWS_ALL, bass.ds(at % RING * (HG * BANK) + h * BANK, BANK)],
                                 start=True, stop=True)
                if j == 1:
                    last.then_inc(score_ready, 1)

            def weigh(it, t):
                rows = key_rows(t)
                pe.wait_ge(score_free, 2 * KT * it + 2 * t + 4)
                if t == 0:
                    pe.wait_ge(vals_ready, 2 * it + 1)
                    pe.wait_ge(acc_free, it + 1)
                if t == HALF:
                    pe.wait_ge(vals_ready, 2 * it + 2)
                slot = slot_of(t)
                for h in range(HG):
                    last = pe.matmul(acc[HEAD_PE * h:HEAD_PE * (h + 1), :], vals[0:rows, t, h, :],
                                     probs[slot][0:rows, h, :], start=(t == 0), stop=(t == KT - 1),
                                     tile_position=(0, HEAD_PE * h))
                last.then_inc(probs_free, 1)

            def fill(it, entry, n):
                pe.wait_ge(ring_free, entries_before(it) + n + 1)
                bank = bank_of(it, n)
                if entry == "sums":
                    turn_sums(bank, it - 1)
                elif entry == "rows":
                    turn_rows(bank, it + 1)
                else:
                    ahead, c = entry
                    if entry == (2, 0):
                        pe.wait_ge(q_in, Q_LOAD * (it + 3))
                    max_chunk(bank, it + ahead, c)

            def step(it, ahead):
                entries = entries_of(it, ahead)
                rate = max(len(entries), IN_STEP)
                done = 0
                for t in range(KT):
                    if t == KT - 1 and ahead >= 1:
                        pe.wait_ge(max_placed, 16 * it + 32)
                    for h in range(HG):
                        if t < KT - 1 or ahead >= 1:
                            score(it, t + 1, h)
                        due = min(len(entries), -(-(HG * t + h + 1) * rate // PLACES))
                        if ahead == 0 and HG * t + h < SUMS_AT:
                            due = 0
                        for n in range(done, due):
                            fill(it, entries[n], n)
                        done = due
                        if h == (1 if ahead == 2 else HG - 1):
                            if t > 0:
                                weigh(it, t - 1)
                            elif not is_first(it):
                                weigh(it - 1, KT - 1)

            pe.wait_ge(q_in, Q_LOAD)
            for c in range(CHUNKS):
                pe.wait_ge(ring_free, c + 1)
                max_chunk(ring[c % BANKS], 0, c)
            pe.wait_ge(q_in, 2 * Q_LOAD)
            pe.wait_ge(ring_free, CHUNKS + 1)
            turn_rows(ring[CHUNKS % BANKS], 0)
            pe.wait_ge(max_placed, 16)
            for h in range(HG):
                score(0, 0, h)
            pe.wait_ge(keep["rest_in"], 16 * len(THIRDS_K) * (GROUPS - 1))
            step(0, 2)
            with pe.Fori(1, STEPS - 2) as it:
                step(it, 2)
            step(STEPS - 2, 1)
            step(STEPS - 1, 0)
            weigh(STEPS - 1, KT - 1)
            pe.wait_ge(ring_free, ENTRIES)
            turn_sums(ring[(ENTRIES - 1) % BANKS], STEPS - 1)

        @block.scalar
        def _(act):
            act.sem_inc(score_free, 2)
            act.sem_inc(acc_free, 1)

            def copy_sums(count):
                act.wait_ge(probs_free, KT * count + KT + 3)
                if not is_first(count):
                    act.wait_ge(ring_ready, entries_before(count) + sums_turned(count))
                act.activation(acc_sb[:, :], acc[:, :], ACT.Copy).then_inc(acc_free, 1)

            def step(it, ahead):
                for t in range(KT):
                    rows = key_rows(t)
                    slot = slot_of(t)
                    back = {0: 1, 1: 1, 2: 2, KT - 1: 3}.get(t, t + 1)
                    act.wait_ge(probs_free, KT * it + back)
                    for pair in range(2):
                        if (t, pair) == (1, 1) and not is_first(it):
                            copy_sums(it - 1)
                        act.wait_ge(score_ready, 2 * KT * it + 2 * t + pair + 2)
                        act.activation(probs[slot][0:rows, 2 * pair:2 * pair + 2, :], scores[pair][0:rows, :, :],
                                       ACT.Exp, scale=SCORE_SCALE).then_inc(score_free, 1)

            step(0, 2)
            with act.Fori(1, STEPS - 2) as it:
                step(it, 2)
            step(STEPS - 2, 1)
            step(STEPS - 1, 0)
            copy_sums(STEPS - 1)

        @block.gpsimd
        def _(pool):
            def place_values(count, half):
                lo, hi = (0, HALF) if half == 0 else (HALF, KT)
                if not is_first(count):
                    pool.wait_ge(probs_free, KT * (count - 1) + hi + 3)
                pool.tensor_copy(vals[:, lo:hi, :, :].rearrange("p t h w -> p (t h w)"),
                                 values[:, bass.ds(count // QB * (KT * HG * HEAD_PE) + lo * (HG * HEAD_PE),
                                                   (hi - lo) * HG * HEAD_PE)]).then_inc(vals_ready, 1)

            place_values(0, 0)
            place_values(0, 1)
            with pool.Fori(1, STEPS) as it:
                place_values(it, 0)
                place_values(it, 1)

        @block.vector
        def _(dve):
            dve.sem_inc(ring_free, BANKS)

            def reduce_chunk(bank, c):
                qt, part = divmod(c, CHUNKS_QT)
                if part < CHUNKS_QT - 1:
                    h, k = divmod(part, WHOLE)
                    dve.tensor_reduce(max_part[:, qt, h, k:k + 1], bank[:, :], AX.X, ALU.max).then_inc(ring_free, 1)
                else:
                    dve.tensor_reduce(max_part[:, qt, :, WHOLE],
                                      bank[:, 0:HG * REST].rearrange("p (h n) -> p h n", h=HG), AX.X, ALU.max
                                      ).then_inc(ring_free, 1)

            def copy_rows(bank, count):
                if not is_first(count):
                    dve.wait_ge(max_placed, 16 * count)
                dve.tensor_copy(max_rows[:, :], bank[:, :].bitcast(BF16)[0:3 * HG, 0:BANK]).then_inc(ring_free, 1)

            th = [max_thirds[:, :, i, :] for i in range(3)]
            raw, rest = max_raw[:, :, :], max_rest[:, :, :]

            def split_maxima(count, reduced, part):
                if part == 0:
                    dve.wait_ge(ring_free, reduced + BANKS)
                    dve.tensor_reduce(raw, max_part[:, :, :, :], AX.X, ALU.max).then_inc(max_chain, 1)
                    dve.wait_ge(max_chain, CHAIN_MAX * count + 1)
                    return
                if part == 1:
                    dve.tensor_scalar(th[0], raw, -1.0, None, ALU.mult).then_inc(max_chain, 1)
                    return
                dve.wait_ge(max_chain, CHAIN_MAX * count + part)
                if part == 2:
                    dve.scalar_tensor_tensor(rest, raw, -1.0, th[0], ALU.mult, ALU.subtract).then_inc(max_chain, 1)
                if part == 3:
                    dve.tensor_copy(th[1], rest).then_inc(max_chain, 1)
                if part == 4:
                    dve.tensor_tensor(th[2], rest, th[1], ALU.subtract).then_inc(thirds_ready, 1)

            def divide_sums(bank, count):
                sums = bank[:, :].rearrange("p (q h w) -> p q h w", q=QT, h=HG)
                dve.reciprocal(recip[:, :, :], sums[:, :, :, W]).then_inc(out_chain, 1)
                dve.wait_ge(out_chain, count + 1)
                dve.tensor_tensor(head_out[:, :, :, :], sums[:, :, :, 0:W],
                                  recip[:, :, :].rearrange("p q (h o) -> p q h o", o=1).broadcast_to([P, QT, HG, W]),
                                  ALU.mult).then_inc(ring_free, 1)

            def add_sums(count, used):
                dve.wait_ge(ring_free, used + BANKS)
                xv = x_tok[:, bass.ds(count % QB * QT, QT), bass.ds(count // QB * (HG * W), HG * W)]
                dve.tensor_tensor(xv, xv, head_out[:, :, :, :].rearrange("p q h w -> p q (h w)"), ALU.add
                                  ).then_inc(added, 1)

            def step(it, ahead):
                entries = entries_of(it, ahead)
                base = entries_before(it)
                split_from = max([n for n, e in enumerate(entries) if isinstance(e, tuple) and e[0] == 1], default=None)
                for n, entry in enumerate(entries):
                    dve.wait_ge(ring_ready, base + n + 1)
                    bank = bank_of(it, n)
                    if entry == "sums":
                        divide_sums(bank, it - 1)
                    elif entry == "rows":
                        copy_rows(bank, it + 1)
                    else:
                        reduce_chunk(bank, entry[1])
                    if n > 0 and entries[n - 1] == "sums" or entry == "sums" and n == len(entries) - 1:
                        add_sums(it - 1, base + (n if entry != "sums" else n + 1))
                    if ahead >= 1 and n >= split_from:
                        parts = [n - split_from] if ahead == 2 else range(5) if n == split_from else []
                        for part in parts:
                            if part < 5:
                                split_maxima(it + 1, base + split_from + 1, part)

            for c in range(CHUNKS):
                dve.wait_ge(ring_ready, c + 1)
                reduce_chunk(ring[c % BANKS], c)
            for part in range(5):
                split_maxima(0, CHUNKS, part)
            dve.wait_ge(ring_ready, CHUNKS + 1)
            copy_rows(ring[CHUNKS % BANKS], 0)
            step(0, 2)
            with dve.Fori(1, STEPS - 2) as it:
                step(it, 2)
            step(STEPS - 2, 1)
            step(STEPS - 1, 0)
            dve.wait_ge(ring_ready, ENTRIES)
            divide_sums(ring[(ENTRIES - 1) % BANKS], STEPS - 1)
            add_sums(STEPS - 1, ENTRIES)

        @block.sync
        def _(sp):
            def load_queries(count):
                sp.wait_ge(q_in, Q_LOAD * count)
                load_step_queries(sp, q_aug, q_parts_dram, count, q_in)

            def place(count):
                at = entries_of(count - 1, 1 if is_last(count) else 2).index("rows") if not is_first(count) else 0
                sp.wait_ge(ring_free, (entries_before(count - 1) + at if not is_first(count) else CHUNKS) + 1 + BANKS)
                sp.dma_start(
                    q_aug[ROWS_MASKED:ROWS_ALL, bass.ds(count % RING * (HG * BANK), HG * BANK)],
                    max_rows[:, :]).then_inc(max_placed, 16)

            for count in range(1, RING - 1):
                load_queries(count)
            place(0)
            load_queries(RING - 1)
            place(1)
            with sp.Fori(1, STEPS - RING + 1) as it:
                sp.wait_ge(score_ready, 2 * KT * it + 1)
                load_queries(it + RING - 1)
                place(it + 1)
            for count in range(STEPS - RING + 2, STEPS):
                place(count)
            sp.wait_ge(max_placed, 16 * STEPS)


E = 16
F = 512
FC = F // P
GATE_PE = P // (N // BANK)
SHARED = 2
TOP = 2
CAP = -(-N * TOP * 5 // (E * 4))
CAP_TILES = -(-CAP // P)
SLOTS = E * CAP
CHUNK_TOK = N // (P // E)
NCH = N // CHUNK_TOK
KEY_BITS = 16
KEY_ABOVE = 131072.0

C_SUM, C_BEFORE = 0, P
C_BASE = 2 * P
C_EXPERT = C_BASE + 1
C_DUMMY = C_EXPERT + E
C_ALL = C_DUMMY + TOP * NT


def shape_constants(np):
    c = np.zeros((P, C_ALL), np.float32)
    e, chunk = np.arange(P) // NCH, np.arange(P) % NCH
    same = e[:, None] == e[None, :]
    c[:, C_SUM:C_SUM + P] = same
    c[:, C_BEFORE:C_BEFORE + P] = same & (chunk[:, None] < chunk[None, :])
    c[:, C_BASE] = e * CAP + 1
    c[:, C_EXPERT:C_EXPERT + E] = np.arange(E)
    t = np.arange(NT)[None, :] * P + np.arange(P)[:, None]
    for k in range(TOP):
        c[:, C_DUMMY + k * NT:C_DUMMY + (k + 1) * NT] = SLOTS + k * N + t
    return c


NORM_GROUP = 4
NORM_GROUPS = NT // NORM_GROUP


class Norm:

    def __init__(self, m, tag, normed):
        self.stats = m.sb(f"{tag}_stats", [P, NT, 6])
        self.meanvar = m.sb(f"{tag}_meanvar", [P, NT, 2])
        self.std, self.rstd = m.sb(f"{tag}_std", [P, NT]), m.sb(f"{tag}_rstd", [P, NT])
        self.eps = m.sb(f"{tag}_eps", [P, 1])
        self.normed = normed
        self.stats_done = m.sem(f"{tag}_stats_done")
        self.std_done = m.sem(f"{tag}_std_done")
        self.rstd_done = m.sem(f"{tag}_rstd_done")
        self.norm_done = m.sem(f"{tag}_norm_done")

    def take_stats(self, dve, x_tok, g):
        tiles = range(NORM_GROUP * g, NORM_GROUP * (g + 1))
        for t in tiles:
            dve.bn_stats(self.stats[:, t, :], x_tok[:, t, :]).then_inc(self.stats_done, 1)
        for i, t in enumerate(tiles):
            dve.wait_ge(self.stats_done, self._stats_of(g) - 2 * NORM_GROUP + i + 1)
            dve.bn_aggr(self.meanvar[:, t, :], self.stats[:, t, :]).then_inc(self.stats_done, 1)

    def _stats_of(self, g):
        return 1 + 2 * NORM_GROUP * (g + 1)

    def normalize(self, dve, x_tok, g):
        part = slice(NORM_GROUP * g, NORM_GROUP * (g + 1))
        dve.wait_ge(self.std_done, g + 1)
        dve.reciprocal(self.rstd[:, part], self.std[:, part]).then_inc(self.rstd_done, 1)
        dve.wait_ge(self.rstd_done, g + 1)
        for t in range(NORM_GROUP * g, NORM_GROUP * (g + 1)):
            dve.tensor_scalar(self.normed[:, t, :], x_tok[:, t, :], self.meanvar[:, t, 0:1], self.rstd[:, t:t + 1],
                              ALU.subtract, ALU.mult).then_inc(self.norm_done, 1)

    def on_vector(self, dve, x_tok, before=lambda g: None):
        dve.memset(self.eps[:, :], EPS_LN).then_inc(self.stats_done, 1)
        for g in range(NORM_GROUPS + 1):
            if g < NORM_GROUPS:
                before(g)
                self.take_stats(dve, x_tok, g)
            if g > 0:
                self.normalize(dve, x_tok, g - 1)

    def on_scalar(self, act, g):
        part = bass.ds(NORM_GROUP * g, NORM_GROUP)
        act.wait_ge(self.stats_done, self._stats_of(g))
        act.activation(self.std[:, part], self.meanvar[:, part, 1], ACT.Sqrt, bias=self.eps[:, 0:1]
                       ).then_inc(self.std_done, 1)


def route_and_share(nc, a, keep, x_tok, normed, slots_in_dram, route, layer):
    with ExitStack() as scope:
        m = Memory(nc, scope)
        ident = keep["ident"]
        norm = Norm(m, "ln2", normed)
        tokT = m.sb("tokT", [P, DC, N])
        sw1, sw3 = (m.sb(n, [P, SHARED, DC, F]) for n in ("sw1_sb", "sw3_sb"))
        sw2 = m.sb("sw2_sb", [P, SHARED, FC, D])
        gate_w, gate_b = m.sb("gate_w_sb", [P, DC, GATE_PE]), m.sb("gate_b_rows", [P, E])
        logitsT = m.sb("logitsT", [P, BANK])
        const = m.sb("const", [P, C_ALL])
        zeros = m.sb("zeros", [P, 2560])
        silu = [m.sb(f"silu{i}", [P, BANK]) for i in range(2)]
        hidden = [m.sb(f"hidden{i}", [P, SHARED * FC, BANK]) for i in range(2)]
        gu = [m.ps(f"gu{i}", [P, 2, BANK]) for i in range(2)]
        y_bank = [m.ps(f"y_bank{i}", [P, BANK]) for i in range(2)]
        small = m.ps("small", [P, BANK])
        wide = m.ps("wide", [P, BANK])

        logits, gates, onehot1, onehot2, work, key = (m.sb(n, [P, NT, E]) for n in
                                                      ("logits", "gates", "onehot1", "onehot2", "work", "rkey"))
        col = m.sb("col", [P, NT])
        col2 = m.sb("col2", [P, NT])
        chosen_logit = [m.sb(f"chosen_logit{k}", [P, NT]) for k in range(TOP)]
        bits, sign = m.sb("bits", [P, NT, E], I32), m.sb("sign", [P, NT, E], I32)
        hi_tok, lo_tok = m.sb("hi_tok", [P, 2, E, NCH]), m.sb("lo_tok", [P, 2, E, NCH])
        slot_tok = m.sb("slot_tok", [P, NT, E])
        hi, lo = m.sb("hi", [P, CHUNK_TOK]), m.sb("lo", [P, CHUNK_TOK])
        above, equal, r1, r2, r3 = (m.sb(n, [P, CHUNK_TOK]) for n in ("above", "equal", "r1", "r2", "r3"))
        ones = m.sb("ones_row", [P, CHUNK_TOK])
        cand, cnt, inc = (m.sb(n, [P, 1]) for n in ("cand", "cnt", "inc"))
        totals = m.sb("totals", [P, 2])
        offs = m.sb("offs", [P, 4])

        sh_in, gate_in, const_in = m.sem("sh_in"), m.sem("gate_in"), m.sem("const_in")
        zero_set, zero_out = m.sem("zero_set"), m.sem("zero_out")
        t_full, t_free = m.sem("t_full"), m.sem("t_free")
        gate_zero, gated, gated_copied = m.sem("gate_zero"), m.sem("gated"), m.sem("gated_copied")
        logits_ready, shifted, expd = m.sem("logits_ready"), m.sem("shifted"), m.sem("expd")
        gu_ready, silu_done, h_done = m.sem("gu_ready"), m.sem("silu_done"), m.sem("h_done")
        y_ready, y_done = m.sem("y_ready"), m.sem("y_done")
        keys_ready, keys_turned = m.sem("keys_ready"), m.sem("keys_turned")
        counted, summed = m.sem("counted"), m.sem("summed")
        totals_ready, offs_ready = m.sem("totals_ready"), m.sem("offs_ready")
        slots_ready, slots_turned = m.sem("slots_ready"), m.sem("slots_turned")
        idx_ready, sent = m.sem("idx_ready"), m.sem("sent")
        chain = m.sem("route_chain")

        UB = SHARED * FC
        BLOCKS = N // BANK
        KEYS_AT = 6
        EVENTS = []
        for blk_ in range(BLOCKS):
            for u_ in range(UB):
                EVENTS.append(("up", UB * blk_ + u_))
                if u_ == 1 and blk_ > 0:
                    EVENTS.append(("down", blk_ - 1))
        EVENTS.append(("down", BLOCKS - 1))
        SEARCH_FROM = ("up", KEYS_AT + 1)
        ROUNDS = 2 * KEY_BITS

        def rounds_of(event):
            first = 0
            for e in EVENTS[EVENTS.index(SEARCH_FROM):]:
                if e == event:
                    return first
                first += 2 if e[0] == "up" else 2 * (BANK // P)
            return -ROUNDS

        SEARCH_END = next(e for e in EVENTS if rounds_of(e) >= 0 and
                          rounds_of(e) + (2 if e[0] == "up" else 2 * (BANK // P)) >= ROUNDS)
        OFFS_AT = SEARCH_END
        TURN_AT = EVENTS[EVENTS.index(SEARCH_END) + 2]
        TERNARY_AT = EVENTS[EVENTS.index(TURN_AT) + 1:][:layer.STEPS]
        assert len(TERNARY_AT) == layer.STEPS

        block = scope.enter_context(nc.Block())

        @block.sync
        def _(sp):
            sp.wait_ge(gate_zero, 1)
            sp.dma_start(gate_w[:, :, 0:E], a["gate_w"].rearrange("(c p) e -> p c e", p=P)).then_inc(gate_in, 16)
            sp.dma_start(gate_b[:, :], a["gate_b"].partition_broadcast(P)).then_inc(gate_in, 16)
            for s in range(SHARED):
                sp.dma_start(sw1[:, s], a["sw1"][s].rearrange("(c p) f -> p c f", p=P)).then_inc(sh_in, 16)
                sp.dma_start(sw3[:, s], a["sw3"][s].rearrange("(c p) f -> p c f", p=P)).then_inc(sh_in, 16)
                sp.dma_start(sw2[:, s], a["sw2"][s].rearrange("(c p) f -> p c f", p=P)).then_inc(sh_in, 16)
            sp.dma_start(const[:, :], a["const"]).then_inc(const_in, 16)
            sp.wait_ge(zero_set, 1)
            for i in range(SLOTS * D // (P * 2560)):
                r = P * 2560 // D
                sp.dma_start(slots_in_dram[i * r:(i + 1) * r, :].rearrange("(p k) d -> p (k d)", p=P), zeros[:, :]
                             ).then_inc(zero_out, 16)
            layer.load(sp, a)
            sp.wait_ge(zero_out, 16 * (SLOTS * D // (P * 2560)))

        @block.gpsimd
        def _(pool):
            pool.memset(gate_w[:, :, :], 0.0).then_inc(gate_zero, 1)
            pool.wait_ge(gate_zero, 1)
            pool.memset(zeros[:, :], 0.0).then_inc(zero_set, 1)
            pool.wait_ge(zero_out, 16 * (SLOTS * D // (P * 2560)))
            pool.wait_ge(idx_ready, TOP)
            pool.wait_ge(norm.norm_done, NT)
            for k in range(TOP):
                for t in range(NT):
                    pool.indirect_dma_start(
                        out=slots_in_dram[:, :], out_offset=bass.IndirectOffsetOnAxis(ap=route["send"][k][:, t:t + 1], axis=0),
                        in_=normed[:, t, :], in_offset=None).then_inc(sent, 16)
            pool.wait_ge(sent, 16 * TOP * NT)

        @block.tensor
        def _(pe):
            for f in range(DC * NT // 4):
                g, c = divmod(f, DC)
                pe.wait_ge(norm.norm_done, 4 * (g + 1))
                if f >= 4:
                    pe.wait_ge(t_free, f - 3)
                b = gu[f % 4 // 2][:, f % 2, :]
                for j in range(4):
                    last = pe.transpose(b[:, j * P:(j + 1) * P], normed[:, 4 * g + j, c * P:(c + 1) * P], ident[:, :])
                last.then_inc(t_full, 1)
            pe.wait_ge(t_free, DC * NT // 4)
            pe.wait_ge(gate_in, 32)
            for c in range(DC):
                for j in range(BLOCKS):
                    last = pe.matmul(small[GATE_PE * j:GATE_PE * (j + 1), :], gate_w[:, c, :], tokT[:, c, j * BANK:(j + 1) * BANK],
                                     start=(c == 0), stop=(c == DC - 1), tile_position=(0, GATE_PE * j))
            last.then_inc(gated, 1)
            pe.wait_ge(sh_in, 16 * 3 * SHARED)
            pe.wait_ge(const_in, 16)

            def search_round(n):
                if 0 <= n < ROUNDS:
                    pe.wait_ge(counted, n + 1)
                    pe.matmul(small[:, 0:1], const[:, C_SUM:C_SUM + P], cnt[:, :], start=True, stop=True
                              ).then_inc(summed, 1)

            def unit(n, first_round):
                blk, u = divmod(n, UB)
                s, f = divmod(u, FC)
                if n >= 2:
                    pe.wait_ge(h_done, n - 1)
                for j, w in enumerate((sw1, sw3)):
                    for c in range(DC):
                        last = pe.matmul(gu[n % 2][:, j, :], w[:, s, c, f * P:(f + 1) * P],
                                         tokT[:, c, blk * BANK:(blk + 1) * BANK], start=(c == 0), stop=(c == DC - 1))
                    if j == 1:
                        last.then_inc(gu_ready, 1)
                    search_round(first_round + j)

            def down(blk, first_round):
                pe.wait_ge(h_done, UB * (blk + 1))
                for tt in range(BANK // P):
                    t = 4 * blk + tt
                    if t >= 2:
                        pe.wait_ge(y_done, t - 1)
                    for u in range(UB):
                        s, f = divmod(u, FC)
                        last = pe.matmul(y_bank[tt % 2][:, 0:D], hidden[blk % 2][:, u, tt * P:(tt + 1) * P],
                                         sw2[:, s, f, :], start=(u == 0), stop=(u == UB - 1))
                        if u == UB - 1:
                            last.then_inc(y_ready, 1)
                        if u % (UB // 2) == UB // 2 - 1:
                            search_round(first_round + 2 * tt + u // (UB // 2))

            for event in EVENTS:
                kind, n = event
                (unit if kind == "up" else down)(n, rounds_of(event))
                if event == ("up", 0):
                    pe.wait_ge(gated_copied, 1)
                    for q in range(BANK // P):
                        last = pe.transpose(small[:, q * P:(q + 1) * P], logitsT[:, q * P:(q + 1) * P], ident[:, :])
                    last.then_inc(logits_ready, 1)
                if event == ("up", KEYS_AT):
                    pe.wait_ge(keys_ready, 1)
                    for j, src in enumerate((hi_tok, lo_tok)):
                        for s in range(2):
                            last = pe.transpose(wide[:, j * CHUNK_TOK + s * P:j * CHUNK_TOK + (s + 1) * P],
                                                src[:, s].rearrange("p e c -> p (e c)"), ident[:, :])
                    last.then_inc(keys_turned, 1)
                if event == OFFS_AT:
                    pe.wait_ge(totals_ready, 1)
                    pe.matmul(small[:, 0:2], const[:, C_BEFORE:C_BEFORE + P], totals[:, :], start=True, stop=True)
                    pe.matmul(small[:, 2:4], const[:, C_SUM:C_SUM + P], totals[:, :], start=True, stop=True
                              ).then_inc(offs_ready, 1)
                if event == TURN_AT:
                    pe.wait_ge(slots_ready, 1)
                    for s in range(2):
                        last = pe.transpose(wide[:, s * P:(s + 1) * P], r1[:, s * P:(s + 1) * P], ident[:, :])
                    last.then_inc(slots_turned, 1)
                if event == TERNARY_AT[1]:
                    layer.sum_sizes(pe, small)

        @block.scalar
        def _(act):
            norm.on_scalar(act, 0)
            for f in range(DC * NT // 4):
                g, c = divmod(f, DC)
                if c == 0 and g + 1 < NORM_GROUPS:
                    norm.on_scalar(act, g + 1)
                act.wait_ge(t_full, f + 1)
                act.activation(tokT[:, c, g * BANK:(g + 1) * BANK], gu[f % 4 // 2][:, f % 2, :], ACT.Copy
                               ).then_inc(t_free, 1)
            act.wait_ge(gated, 1)
            act.activation(logitsT[:, :], small[:, :], ACT.Copy).then_inc(gated_copied, 1)
            act.wait_ge(shifted, 1)
            act.activation(gates[:, :, :], work[:, :, :], ACT.Exp).then_inc(expd, 1)
            for n in range(UB * BLOCKS):
                act.wait_ge(gu_ready, n + 1)
                if n >= 2:
                    act.wait_ge(h_done, n - 1)
                act.activation(silu[n % 2][:, :], gu[n % 2][:, 0, :], ACT.Silu).then_inc(silu_done, 1)

        @block.vector
        def _(dve):
            made = 0

            def link(ins):
                nonlocal made
                made += 1
                ins.then_inc(chain, 1)
                dve.wait_ge(chain, made)

            def over_experts(x):
                return x[:, :].rearrange("p (t o) -> p t o", o=1).broadcast_to([P, NT, E])

            def over_tokens(x):
                return x.rearrange("p (o e) -> p o e", o=1).broadcast_to([P, NT, E])

            def unit(n):
                dve.wait_ge(silu_done, n + 1)
                if n >= 2 * UB:
                    dve.wait_ge(y_ready, 4 * (n // UB - 1))
                dve.tensor_tensor(hidden[n // UB % 2][:, n % UB, :], silu[n % 2][:, :], gu[n % 2][:, 1, :], ALU.mult
                                  ).then_inc(h_done, 1)

            def add_tile(t):
                dve.wait_ge(y_ready, t + 1)
                dve.scalar_tensor_tensor(x_tok[:, t, :], y_bank[t % 2][:, 0:D], 1.0 / SHARED, x_tok[:, t, :],
                                         ALU.mult, ALU.add).then_inc(y_done, 1)

            def shift_logits():
                dve.wait_ge(logits_ready, 1)
                link(dve.tensor_copy(logits[:, :, :].rearrange("p (j q) e -> p q j e", j=BLOCKS),
                                     small[:, :].rearrange("p (q j e) -> p q j e", j=BLOCKS, e=GATE_PE)[:, :, :, 0:E]))
                link(dve.tensor_reduce(col[:, :], logits[:, :, :], AX.X, ALU.max))
                dve.tensor_tensor(work[:, :, :], logits[:, :, :], over_experts(col), ALU.subtract).then_inc(shifted, 1)

            def finish_gates():
                dve.wait_ge(expd, 1)
                link(dve.tensor_reduce(col[:, :], gates[:, :, :], AX.X, ALU.add))
                link(dve.reciprocal(col2[:, :], col[:, :]))
                link(dve.tensor_tensor(gates[:, :, :], gates[:, :, :], over_experts(col2), ALU.mult))
                link(dve.tensor_tensor(gates[:, :, :], gates[:, :, :], over_tokens(gate_b[:, :]), ALU.add))

            def best_gate(k, onehot):
                link(dve.tensor_reduce(col[:, :], gates[:, :, :], AX.X, ALU.max))
                link(dve.tensor_tensor(work[:, :, :], gates[:, :, :], over_experts(col), ALU.is_equal))
                link(dve.scalar_tensor_tensor(key[:, :, :], work[:, :, :], -float(2 * E),
                                              over_tokens(const[:, C_EXPERT:C_EXPERT + E]), ALU.mult, ALU.add))
                link(dve.tensor_reduce(col[:, :], key[:, :, :], AX.X, ALU.min))
                link(dve.tensor_tensor(onehot[:, :, :], key[:, :, :], over_experts(col), ALU.is_equal))
                link(dve.tensor_tensor(work[:, :, :], logits[:, :, :], onehot[:, :, :], ALU.mult))
                link(dve.tensor_reduce(chosen_logit[k][:, :], work[:, :, :], AX.X, ALU.add))
                if k == 0:
                    link(dve.scalar_tensor_tensor(gates[:, :, :], onehot[:, :, :], -1e30, gates[:, :, :],
                                                  ALU.mult, ALU.add))

            def order_keys():
                raw = logits[:, :, :].bitcast(I32)
                link(dve.tensor_scalar(sign[:, :, :], raw, 31, 0x7FFFFFFF, ALU.arith_shift_right, ALU.bitwise_and))
                link(dve.tensor_tensor(bits[:, :, :], raw, sign[:, :, :], ALU.bitwise_xor))
                link(dve.tensor_scalar(sign[:, :, :], bits[:, :, :], 16, None, ALU.arith_shift_right))
                link(dve.tensor_scalar(bits[:, :, :], bits[:, :, :], 0xFFFF, None, ALU.bitwise_and))
                link(dve.tensor_tensor(work[:, :, :], onehot1[:, :, :], onehot2[:, :, :], ALU.add))
                link(dve.scalar_tensor_tensor(key[:, :, :], sign[:, :, :], 32769.0, work[:, :, :], ALU.add, ALU.mult))

            def lay_keys():
                for s in range(2):
                    v = key[:, :, :].rearrange("p (c s) e -> p s e c", s=2)[:, s]
                    link(dve.tensor_copy(hi_tok[:, s], v))
                    v = bits[:, :, :].rearrange("p (c s) e -> p s e c", s=2)[:, s]
                    if s == 0:
                        link(dve.tensor_copy(lo_tok[:, s], v))
                    else:
                        dve.tensor_copy(lo_tok[:, s], v).then_inc(keys_ready, 1)

            def take_keys():
                dve.wait_ge(keys_turned, 1)
                link(dve.tensor_copy(hi[:, :], wide[:, 0:CHUNK_TOK]))
                link(dve.tensor_copy(lo[:, :], wide[:, CHUNK_TOK:2 * CHUNK_TOK]))
                count_keys(0)

            def count_keys(n):
                if n % KEY_BITS == 0:
                    link(dve.memset(cand[:, :], 2.0 ** (KEY_BITS - 1)))
                dve.tensor_scalar(r3[:, :], (hi, lo)[n // KEY_BITS][:, :], cand[:, 0:1], None, ALU.is_ge, ALU.add,
                                  accum_out=cnt[:, :]).then_inc(counted, 1)

            def end_round(n):
                if not 0 <= n < ROUNDS:
                    return
                step = 2.0 ** (KEY_BITS - 1 - n % KEY_BITS)
                dve.wait_ge(summed, n + 1)
                link(dve.tensor_scalar(inc[:, :], small[:, 0:1], float(CAP), step, ALU.is_ge, ALU.mult))
                link(dve.scalar_tensor_tensor(cand[:, :], inc[:, :], -0.5 * step, cand[:, :], ALU.add, ALU.add))
                if n == KEY_BITS - 1:
                    lower_keys()
                if n == ROUNDS - 1:
                    rank()
                else:
                    count_keys(n + 1)

            def lower_keys():
                link(dve.tensor_scalar(cand[:, :], cand[:, :], -0.5, None, ALU.add))
                link(dve.tensor_scalar(above[:, :], hi[:, :], cand[:, 0:1], None, ALU.is_gt))
                link(dve.tensor_scalar(equal[:, :], hi[:, :], cand[:, 0:1], None, ALU.is_equal))
                link(dve.scalar_tensor_tensor(r1[:, :], lo[:, :], 1.0, equal[:, :], ALU.add, ALU.mult))
                link(dve.scalar_tensor_tensor(r2[:, :], above[:, :], KEY_ABOVE, r1[:, :], ALU.mult, ALU.add))
                link(dve.tensor_scalar(lo[:, :], r2[:, :], -1.0, None, ALU.add))

            def rank():
                link(dve.tensor_scalar(cand[:, :], cand[:, :], -0.5, None, ALU.add))
                link(dve.tensor_scalar(r3[:, :], hi[:, :], 0.0, None, ALU.is_gt))
                link(dve.scalar_tensor_tensor(above[:, :], lo[:, :], cand[:, 0:1], r3[:, :], ALU.is_gt, ALU.mult))
                link(dve.scalar_tensor_tensor(equal[:, :], lo[:, :], cand[:, 0:1], r3[:, :], ALU.is_equal, ALU.mult))
                link(dve.memset(ones[:, :], 1.0))
                link(dve.tensor_tensor_scan(r1[:, :], ones[:, :], above[:, :], 0.0, ALU.mult, ALU.add))
                link(dve.tensor_tensor_scan(r2[:, :], ones[:, :], equal[:, :], 0.0, ALU.mult, ALU.add))
                link(dve.tensor_copy(totals[:, 0:1], r1[:, CHUNK_TOK - 1:CHUNK_TOK]))
                dve.tensor_copy(totals[:, 1:2], r2[:, CHUNK_TOK - 1:CHUNK_TOK]).then_inc(totals_ready, 1)

            def place():
                dve.wait_ge(offs_ready, 1)
                base = const[:, C_BASE:C_BASE + 1]
                link(dve.tensor_copy(offs[:, :], small[:, 0:4]))
                link(dve.scalar_tensor_tensor(r1[:, :], r1[:, :], offs[:, 0:1], above[:, :], ALU.add, ALU.subtract))
                link(dve.scalar_tensor_tensor(r2[:, :], r2[:, :], offs[:, 1:2], equal[:, :], ALU.add, ALU.subtract))
                link(dve.tensor_scalar(r2[:, :], r2[:, :], offs[:, 2:3], None, ALU.add))
                link(dve.scalar_tensor_tensor(r3[:, :], r2[:, :], float(CAP), equal[:, :], ALU.is_lt, ALU.mult))
                link(dve.scalar_tensor_tensor(r2[:, :], r2[:, :], base, r3[:, :], ALU.add, ALU.mult))
                link(dve.scalar_tensor_tensor(r1[:, :], r1[:, :], base, above[:, :], ALU.add, ALU.mult))
                dve.tensor_tensor(r1[:, :], r1[:, :], r2[:, :], ALU.add).then_inc(slots_ready, 1)

            def address():
                dve.wait_ge(slots_turned, 1)
                for s in range(2):
                    link(dve.tensor_copy(slot_tok[:, :, :].rearrange("p (c s) e -> p s e c", s=2)[:, s],
                                         wide[:, s * P:(s + 1) * P].rearrange("p (e c) -> p e c", e=E)))
                for k, onehot in enumerate((onehot1, onehot2)):
                    dummy = const[:, C_DUMMY + k * NT:C_DUMMY + (k + 1) * NT]
                    link(dve.tensor_tensor(work[:, :, :], slot_tok[:, :, :], onehot[:, :, :], ALU.mult))
                    link(dve.tensor_reduce(col[:, :], work[:, :, :], AX.X, ALU.add))
                    link(dve.tensor_scalar(col2[:, :], col[:, :], 0.0, None, ALU.is_gt))
                    link(dve.tensor_tensor(route["weight"][k][:, :], chosen_logit[k][:, :], col2[:, :], ALU.mult))
                    link(dve.tensor_scalar(route["fetch"][k][:, :], col[:, :], -1.0, 0.0, ALU.add, ALU.max))
                    link(dve.scalar_tensor_tensor(col[:, :], col[:, :], -1.0, dummy, ALU.add, ALU.subtract))
                    link(dve.tensor_tensor(col[:, :], col[:, :], col2[:, :], ALU.mult))
                    dve.tensor_tensor(route["send"][k][:, :], col[:, :], dummy, ALU.add).then_inc(idx_ready, 1)
                    dve.wait_ge(idx_ready, k + 1)

            norm.on_vector(dve, x_tok)
            dve.wait_ge(gate_in, 32)
            dve.wait_ge(const_in, 16)
            shift_logits()
            ungated = None
            for event in EVENTS:
                kind, n = event
                if ungated is not None:
                    unit(ungated)
                    ungated = None
                if event == ("up", 0):
                    finish_gates()
                if event == ("up", 1):
                    best_gate(0, onehot1)
                if event == ("up", 2):
                    best_gate(1, onehot2)
                if event == ("up", 3):
                    order_keys()
                if event == ("up", 4):
                    lay_keys()
                first_round = rounds_of(event)
                if kind == "up":
                    for j in range(2):
                        end_round(first_round + j)
                    ungated = n
                else:
                    for tt in range(BANK // P):
                        for j in range(2):
                            end_round(first_round + 2 * tt + j)
                        add_tile(BANK // P * n + tt)
                if event == ("up", KEYS_AT):
                    take_keys()
                if event == OFFS_AT:
                    place()
                if event == TURN_AT:
                    address()
                if event in TERNARY_AT:
                    layer.on_vector(dve, link, small, TERNARY_AT.index(event))


def run_experts(nc, a, keep, slots_in_dram, slots_out_dram):
    FULL = CAP // P
    HALF_TILE = CAP - FULL * P
    assert 2 * HALF_TILE == P and FULL == 2
    with ExitStack() as scope:
        m = Memory(nc, scope)
        ident = keep["ident"]
        w1, w3 = ([m.sb(f"{n}_{i}", [P, DC, F]) for i in range(2)] for n in ("ew1", "ew3"))
        w2 = [m.sb(f"ew2_{i}", [P, FC, D]) for i in range(2)]
        rows = [m.sb(f"slot_rows{i}", [P, CAP_TILES, D]) for i in range(2)]
        rowsT = [m.sb(f"slot_rowsT{i}", [P, DC, CAP]) for i in range(2)]
        silu = [m.sb(f"esilu{i}", [P, CAP]) for i in range(2)]
        hidden = [m.sb(f"ehidden{i}", [P, FC, CAP]) for i in range(2)]
        y_sb = [m.sb(f"y_sb{i}", [P, FULL, D]) for i in range(2)]
        y_halves = m.sb("y_halves", [P, D])
        gu = [m.ps(f"egu{i}", [P, 2, BANK]) for i in range(2)]
        turn = m.ps("eturn", [P, DC, BANK])
        y_bank = [m.ps(f"ey_bank{i}", [P, BANK]) for i in range(2)]

        up_in = [m.sem(f"expert_up_in{i}") for i in range(2)]
        down_in = [m.sem(f"expert_down_in{i}") for i in range(2)]
        rows_in = [m.sem(f"rows_in{i}") for i in range(2)]
        turned, rowsT_ready = m.sem("rows_turned"), m.sem("rowsT_ready")
        gu_ready, silu_done = m.sem("egu_ready"), m.sem("esilu_done")
        h_done = m.sem("eh_done")
        y_ready, y_copied = m.sem("ey_ready"), m.sem("ey_copied")
        y_out = [m.sem(f"y_out{i}") for i in range(2)]
        halves_ready, halves_copied = m.sem("halves_ready"), m.sem("halves_copied")
        halves_out = m.sem("halves_out")
        sizes = [P] * FULL + [HALF_TILE]

        block = scope.enter_context(nc.Block())

        def expert_slots(dram, e, t):
            return dram[bass.ds(e * CAP + t * P, sizes[t]), :]

        @block.sync
        def _(sp):
            def load_up(e, i):
                sp.dma_start(w1[i][:, :, :], a["ew1"][bass.ds(e, 1)].rearrange("o (c p) f -> p (o c) f", p=P)).then_inc(up_in[i], 16)
                sp.dma_start(w3[i][:, :, :], a["ew3"][bass.ds(e, 1)].rearrange("o (c p) f -> p (o c) f", p=P)).then_inc(up_in[i], 16)

            def load_down(e, i):
                sp.dma_start(w2[i][:, :, :], a["ew2"][bass.ds(e, 1)].rearrange("o (c p) f -> p (o c) f", p=P)).then_inc(down_in[i], 16)

            def load_rows(e, i):
                for t in range(CAP_TILES):
                    sp.dma_start(rows[i][0:sizes[t], t, :], expert_slots(slots_in_dram, e, t)).then_inc(rows_in[i], 16)

            def store(e, i):
                sp.wait_ge(y_copied, FULL * (e + 1) + 2)
                for t in range(FULL):
                    sp.dma_start(expert_slots(slots_out_dram, e, t), y_sb[i][:, t, :]).then_inc(y_out[i], 16)

            def store_halves(r):
                sp.wait_ge(halves_copied, r + 2)
                for i in range(2):
                    sp.dma_start(expert_slots(slots_out_dram, 2 * r + i, FULL), y_halves[HALF_TILE * i:HALF_TILE * (i + 1), :]
                                 ).then_inc(halves_out, 16)

            sp.sem_inc(halves_out, 1)
            for i in range(2):
                sp.sem_inc(y_out[i], 1)
                load_rows(i, i)
                load_up(i, i)
                load_down(i, i)
            with sp.Fori(0, E // 2 - 1) as r:
                for i in range(2):
                    e = 2 * r + i
                    sp.wait_ge(gu_ready, FC * (e + 1))
                    load_up(e + 2, i)
                    load_rows(e + 2, i)
                    store(e, i)
                sp.wait_ge(halves_ready, r + 1)
                for i in range(2):
                    load_down(2 * r + i + 2, i)
                store_halves(r)
            for i in range(2):
                store(E - 2 + i, i)
            store_halves(E // 2 - 1)
            for i in range(2):
                sp.wait_ge(y_out[i], 16 * FULL * (E // 2) + 1)
            sp.wait_ge(halves_out, 32 * (E // 2) + 1)

        @block.tensor
        def _(pe):
            def turn_rows(e, i, r):
                pe.wait_ge(rows_in[i], 16 * CAP_TILES * (r + 1))
                if not isinstance(e, int) or e > 0:
                    pe.wait_ge(rowsT_ready, DC * e)
                for c in range(DC):
                    for t, n in enumerate(sizes):
                        last = pe.transpose(turn[:, c, t * P:t * P + n], rows[i][0:n, t, c * P:(c + 1) * P],
                                            ident[0:n, 0:n])
                    last.then_inc(turned, 1)

            def up(e, i, r):
                pe.wait_ge(rowsT_ready, DC * (e + 1))
                pe.wait_ge(up_in[i], 32 * (r + 1))
                for f in range(FC):
                    pe.wait_ge(h_done, FC * e + f + 1)
                    for j, w in enumerate((w1, w3)):
                        for c in range(DC):
                            last = pe.matmul(gu[f % 2][:, j, 0:CAP], w[i][:, c, f * P:(f + 1) * P], rowsT[i][:, c, :],
                                             start=(c == 0), stop=(c == DC - 1))
                    last.then_inc(gu_ready, 1)

            def down(e, i, r):
                pe.wait_ge(h_done, FC * (e + 1) + 2)
                pe.wait_ge(down_in[i], 16 * (r + 1))
                for t in range(FULL):
                    pe.wait_ge(y_copied, FULL * e + t + 1)
                    for f in range(FC):
                        last = pe.matmul(y_bank[t][:, 0:D], hidden[i][:, f, t * P:(t + 1) * P],
                                         w2[i][:, f, :], start=(f == 0), stop=(f == FC - 1))
                    last.then_inc(y_ready, 1)

            def down_halves(turned_experts):
                pe.wait_ge(rowsT_ready, DC * turned_experts)
                for f in range(FC):
                    for i in range(2):
                        last = pe.matmul(turn[HALF_TILE * i:HALF_TILE * (i + 1), 0, 0:D], hidden[i][:, f, FULL * P:CAP],
                                         w2[i][:, f, :], start=(f == 0), stop=(f == FC - 1),
                                         tile_position=(0, HALF_TILE * i))
                last.then_inc(halves_ready, 1)

            pe.sem_inc(halves_copied, 1)
            turn_rows(0, 0, 0)
            with pe.Fori(0, E // 2 - 1) as r:
                up(2 * r, 0, r)
                pe.wait_ge(halves_copied, r + 1)
                turn_rows(2 * r + 1, 1, r)
                down(2 * r, 0, r)
                up(2 * r + 1, 1, r)
                turn_rows(2 * r + 2, 0, r + 1)
                down(2 * r + 1, 1, r)
                down_halves(2 * r + 3)
            r = E // 2 - 1
            up(E - 2, 0, r)
            pe.wait_ge(halves_copied, r + 1)
            turn_rows(E - 1, 1, r)
            down(E - 2, 0, r)
            up(E - 1, 1, r)
            down(E - 1, 1, r)
            down_halves(E)

        @block.scalar
        def _(act):
            act.sem_inc(y_copied, 2)

            def copy_turned(e, i):
                for c in range(DC):
                    act.wait_ge(turned, DC * e + c + 1)
                    act.activation(rowsT[i][:, c, :], turn[:, c, 0:CAP], ACT.Copy).then_inc(rowsT_ready, 1)

            def activate(e, i):
                for f in range(FC):
                    act.wait_ge(gu_ready, FC * e + f + 1)
                    act.wait_ge(h_done, FC * e + f + 1)
                    act.activation(silu[f % 2][:, :], gu[f % 2][:, 0, 0:CAP], ACT.Silu).then_inc(silu_done, 1)

            def copy_out(e, i, r):
                act.wait_ge(y_out[i], 16 * FULL * r + 1)
                for t in range(FULL):
                    act.wait_ge(y_ready, FULL * e + t + 1)
                    act.activation(y_sb[i][:, t, :], y_bank[t][:, 0:D], ACT.Copy).then_inc(y_copied, 1)

            def copy_halves(r):
                act.wait_ge(halves_out, 32 * r + 1)
                act.wait_ge(halves_ready, r + 1)
                act.activation(y_halves[:, :], turn[:, 0, 0:D], ACT.Copy).then_inc(halves_copied, 1)

            copy_turned(0, 0)
            with act.Fori(0, E // 2 - 1) as r:
                for i in range(2):
                    e = 2 * r + i
                    activate(e, i)
                    copy_turned(e + 1, 1 - i)
                    copy_out(e, i, r)
                copy_halves(r)
            r = E // 2 - 1
            activate(E - 2, 0)
            copy_turned(E - 1, 1)
            copy_out(E - 2, 0, r)
            activate(E - 1, 1)
            copy_out(E - 1, 1, r)
            copy_halves(r)

        @block.vector
        def _(dve):
            dve.sem_inc(h_done, 2)

            def gate(e, i):
                for f in range(FC):
                    dve.wait_ge(silu_done, FC * e + f + 1)
                    dve.tensor_tensor(hidden[i][:, f, :], silu[f % 2][:, :], gu[f % 2][:, 1, 0:CAP], ALU.mult
                                      ).then_inc(h_done, 1)

            with dve.Fori(0, E // 2) as r:
                for i in range(2):
                    gate(2 * r + i, i)



QK = 64
ZQ = 256
ZB = N // ZQ
ZT = ZQ // P
HID = 1024
HC = HID // P
RMS_EPS, QUANT_EPS = 1e-6, 1e-5
ROUND = 12582912.0
LEVELS = 127.0


class Quantization:

    def __init__(self, m):
        self.norm = Norm(m, "ln4", m.sb("ln4_normed", [P, NT, D]))
        self.squares = m.sb("normed_squares", [P, NORM_GROUP * D])
        self.ints = m.sb("quant_ints", [P, NT, D], BF16)
        self.eps = m.sb("rms_eps", [P, 1])
        self.ssq, self.big, self.root, self.factor, self.back = (
            m.sb(f"quant_{n}", [P, NT]) for n in ("ssq", "big", "root", "factor", "back"))
        self.eps_set, self.big_done = m.sem("rms_eps_set"), m.sem("big_done")
        self.squared, self.rooted = m.sem("normed_squared"), m.sem("normed_rooted")
        self.chain, self.held, self.quantized = m.sem("quant_chain"), m.sem("held"), m.sem("quantized")
        self.made = 0

    def start(self, dve):
        dve.memset(self.eps[:, :], RMS_EPS).then_inc(self.eps_set, 1)
        dve.memset(self.norm.eps[:, :], EPS_LN).then_inc(self.norm.stats_done, 1)

    def squares_on_scalar(self, act, g):
        for i in range(NORM_GROUP):
            t = NORM_GROUP * g + i
            act.wait_ge(self.norm.norm_done, t + 1)
            act.activation(self.squares[:, i * D:(i + 1) * D],
                           self.norm.normed[:, bass.ds(t, 1), :].rearrange("p o d -> p (o d)"), ACT.Square,
                           accum_out=self.ssq[:, bass.ds(t, 1)]).then_inc(self.squared, 1)
        act.wait_ge(self.squared, NORM_GROUP * (g + 1))
        act.wait_ge(self.eps_set, 1)
        part = bass.ds(NORM_GROUP * g, NORM_GROUP)
        act.activation(self.root[:, part], self.ssq[:, part], ACT.Sqrt, bias=self.eps[:, 0:1], scale=1.0 / D
                       ).then_inc(self.rooted, 1)

    def integers(self, act, g):
        act.wait_ge(self.held, g + 1)
        part = bass.ds(NORM_GROUP * g, NORM_GROUP)
        act.activation(self.ints[:, part, :].rearrange("p t d -> p (t d)"),
                       self.norm.normed[:, part, :].rearrange("p t d -> p (t d)"), ACT.Copy, bias=-ROUND
                       ).then_inc(self.quantized, 1)

    def stats_and_norm(self, dve, x_tok, g):
        self.norm.take_stats(dve, x_tok, g)
        self.norm.normalize(dve, x_tok, g)
        part = slice(NORM_GROUP * g, NORM_GROUP * (g + 1))
        dve.wait_ge(self.norm.norm_done, NORM_GROUP * (g + 1))
        dve.tensor_reduce(self.big[:, part], self.norm.normed[:, part, :], AX.X, ALU.max, apply_absolute_value=True
                          ).then_inc(self.big_done, 1)

    def link(self, dve, ins):
        self.made += 1
        ins.then_inc(self.chain, 1)
        dve.wait_ge(self.chain, self.made)

    def hold(self, dve, w_mean, g):
        dve.wait_ge(self.rooted, g + 1)
        dve.wait_ge(self.big_done, g + 1)
        part = slice(NORM_GROUP * g, NORM_GROUP * (g + 1))
        scales(dve, lambda ins: self.link(dve, ins), self.root[:, part], self.big[:, part], self.back[:, part],
               self.factor[:, part], w_mean[:, 0:1])
        for t in range(NORM_GROUP * g, NORM_GROUP * (g + 1)):
            tile = self.norm.normed[:, t, :]
            self.made += 1
            dve.tensor_scalar(tile, tile, self.factor[:, t:t + 1], ROUND, ALU.mult, ALU.add).then_inc(self.chain, 1)
        dve.wait_ge(self.chain, self.made)
        tiles = self.norm.normed[:, part, :].rearrange("p t d -> p (t d)")
        dve.tensor_scalar(tiles, tiles, ROUND + LEVELS, ROUND - LEVELS - 1, ALU.min, ALU.max).then_inc(self.held, 1)


def scales(dve, link, root, big, back, factor, w_mean):
    link(dve.reciprocal(root, root))
    link(dve.tensor_tensor(back, big, root, ALU.mult))
    link(dve.tensor_scalar(back, back, QUANT_EPS, 1.0 / LEVELS, ALU.max, ALU.mult))
    link(dve.reciprocal(factor, back))
    link(dve.tensor_tensor(factor, factor, root, ALU.mult))
    link(dve.tensor_scalar(back, back, w_mean, None, ALU.mult))


class NextLayer:

    def __init__(self, m):
        self.ctxT = m.sb("ctxT_1", [P, DC, S])
        self.wq, self.wk = m.sb("wq_1", [P, DC, QK]), m.sb("wk_1", [P, DC, QK])
        self.wv = m.sb("wv_1", [P, DC, D])
        self.bq, self.bk, self.bv = m.sb("bq_1", [QK, 1]), m.sb("bk_1", [QK, 1]), m.sb("bv_1", [P, D])
        self.w = [m.sb("ff_w1", [P, DC, HID]), m.sb("ff_w2", [P, HC, D])]
        self.ternary = [m.sb("ternary1", [P, DC, HID], BF16), m.sb("ternary2", [P, HC, D], BF16)]
        self.ones = m.sb("ones_sq", [P, P])
        self.w_abs, self.w_mean, self.w_scale = (m.sb(n, [P, 2]) for n in ("w_abs", "w_mean", "w_scale"))
        self.kin, self.vin, self.qin = m.sem("k1_in"), m.sem("v1_in"), m.sem("q1_in")
        self.w_in, self.counted, self.summed = m.sem("ff_w_in"), m.sem("w_counted"), m.sem("w_summed")

    def load(self, sp, a):
        sp.dma_start(self.w[0][:, :, :], a["w1T"].rearrange("(c p) n -> p c n", p=P)).then_inc(self.w_in, 16)
        sp.dma_start(self.w[1][:, :, :], a["w2T"].rearrange("(c p) n -> p c n", p=P)).then_inc(self.w_in, 16)
        sp.dma_start(self.wk[:, :, :], a["wk1T"].rearrange("(c p) n -> p c n", p=P)).then_inc(self.kin, 16)
        sp.dma_start(self.bk[:, :], a["bk1"].rearrange("(p o) -> p o", o=1), allow_slow_non_contiguous=True).then_inc(self.kin, 16)
        sp.dma_start(self.ctxT[:, :, :], a["ctxT"].rearrange("(c p) n -> p c n", p=P)).then_inc(self.kin, 16)
        sp.dma_start(self.wv[:, :, :], a["wv1T"].rearrange("(c p) n -> p c n", p=P)).then_inc(self.vin, 16)
        sp.dma_start(self.bv[:, :], a["bv1"].partition_broadcast(P)).then_inc(self.vin, 16)
        sp.dma_start(self.wq[:, :, :], a["wq1T"].rearrange("(c p) n -> p c n", p=P)).then_inc(self.qin, 16)
        sp.dma_start(self.bq[:, :], a["bq1"].rearrange("(p o) -> p o", o=1), allow_slow_non_contiguous=True).then_inc(self.qin, 16)

    def sum_sizes(self, pe, bank):
        pe.wait_ge(self.counted, 3)
        pe.matmul(bank[:, 0:2], self.ones[:, :], self.w_abs[:, :], start=True, stop=True).then_inc(self.summed, 1)

    def on_vector(self, dve, link, bank, step):
        flat = [w[:, :, :].rearrange("p c n -> p (c n)") for w in self.w]
        if step < 2:
            if step == 0:
                dve.memset(self.ones[:, :], 1.0).then_inc(self.counted, 1)
                dve.wait_ge(self.w_in, 32)
            dve.tensor_reduce(self.w_abs[:, step:step + 1], flat[step], AX.X, ALU.add, apply_absolute_value=True
                              ).then_inc(self.counted, 1)
            return
        if step == 2:
            dve.wait_ge(self.summed, 1)
            link(dve.tensor_scalar(self.w_mean[:, :], bank[:, 0:2], 1.0 / (D * HID), QUANT_EPS, ALU.mult, ALU.max))
            link(dve.reciprocal(self.w_scale[:, :], self.w_mean[:, :]))
            return
        i, part = divmod(step - 3, 3)
        if part == 0:
            link(dve.tensor_scalar(flat[i], flat[i], self.w_scale[:, i:i + 1], ROUND, ALU.mult, ALU.add))
        if part == 1:
            link(dve.tensor_scalar(flat[i], flat[i], ROUND + 1.0, ROUND - 1.0, ALU.min, ALU.max))
        if part == 2:
            link(dve.tensor_scalar(self.ternary[i][:, :, :].rearrange("p c n -> p (c n)"), flat[i], -ROUND, None, ALU.add))

    STEPS = 9


def combine_and_attend(nc, a, keep, x_tok, slots_out_dram, route, layer, quant):
    with ExitStack() as scope:
        m = Memory(nc, scope)
        ident = keep["ident"]
        got = [m.sb(f"got{k}", [P, NT, D]) for k in range(TOP)]
        ctxT, wq, wk, wv, bq, bk, bv = layer.ctxT, layer.wq, layer.wk, layer.wv, layer.bq, layer.bk, layer.bv
        qT, kT = m.sb("qT_1", [P, N]), m.sb("kT_1", [P, S])
        v = m.sb("v_1", [P, KT, D])
        norm = Norm(m, "ln3", got[0])
        tokT = m.sb("tokT_1", [P, DC, N])
        z = [m.sb(f"z{i}", [P, KT, ZQ]) for i in range(2)]
        bank = [m.ps(f"l1_bank{i}", [P, BANK]) for i in range(4)]
        z_bank = bank + [m.ps("z_bank", [P, BANK])]
        q_bank = m.ps("q_bank", [P, BANK])
        o_bank = [m.ps(f"o_bank{i}", [P, BANK]) for i in range(2)]

        fetched = [m.sem(f"fetched{g}") for g in range(NORM_GROUPS)]
        added, padded = m.sem("expert_added"), m.sem("padded")
        kin, vin, qin = layer.kin, layer.vin, layer.qin
        bank_full = m.sem("l1_bank_full")
        q_full, q_copied = m.sem("q_bank_full"), m.sem("q_bank_copied")
        by_act, by_dve = m.sem("l1_bank_free_act"), m.sem("l1_bank_free_dve")
        z_ready, z_done = m.sem("z_ready"), m.sem("z_done")
        o_ready, o_done = m.sem("o_ready"), m.sem("o_done")

        Z_AHEAD = len(z_bank) - 1

        def z_bank_of(i, t):
            n = KT * i + t
            through_all = 2 * KT % Z_AHEAD * len(z_bank)
            return z_bank[n % len(z_bank) if n < through_all else (n - through_all) % Z_AHEAD]

        FILLS_K = -(-S // BANK)
        FILLS_V = KT
        FILLS_G = DC + 1
        LATER = {(1, 2): 1, (2, 0): 2, (2, 6): 3}
        APART = 2
        ROOTS_AT = (1, 8)

        def fills_after(b, t):
            return [(g, i) for (b0, t0), g in LATER.items() for i in range(FILLS_G) if (b, t) == (b0, t0 + APART * i)]

        block = scope.enter_context(nc.Block())

        @block.gpsimd
        def _(pool):
            for t in range(NT):
                for k in range(TOP):
                    pool.indirect_dma_start(
                        out=got[k][:, t, :], out_offset=None, in_=slots_out_dram[:, :],
                        in_offset=bass.IndirectOffsetOnAxis(ap=route["fetch"][k][:, t:t + 1], axis=0)
                    ).then_inc(fetched[t // NORM_GROUP], 16)

        @block.tensor
        def _(pe):
            fills = 0

            def take_bank():
                if fills >= 4:
                    seen = fills - 3
                    pe.wait_ge(by_act, min(seen, FILLS_K))
                    if seen > FILLS_K:
                        pe.wait_ge(by_dve, seen - FILLS_K)
                return bank[fills % 4]

            pe.wait_ge(kin, 48)
            for n0 in range(0, S, BANK):
                n1 = min(S, n0 + BANK)
                b = take_bank()
                for c in range(DC):
                    last = pe.matmul(b[0:QK, 0:n1 - n0], wk[:, c, :], ctxT[:, c, n0:n1], start=(c == 0), stop=(c == DC - 1))
                last.then_inc(bank_full, 1)
                fills += 1
            pe.wait_ge(vin, 32)
            for t in range(KT):
                b = take_bank()
                for c in range(DC):
                    last = pe.matmul(b[0:key_rows(t), 0:D], ctxT[:, c, t * P:t * P + key_rows(t)], wv[:, c, :],
                                     start=(c == 0), stop=(c == DC - 1))
                last.then_inc(bank_full, 1)
                fills += 1

            def fill_queries(g, i):
                if g or i:
                    pe.wait_ge(q_copied, FILLS_G * g + i)
                if i < DC:
                    pe.wait_ge(norm.norm_done, 4 * (g + 1))
                    for j in range(4):
                        last = pe.transpose(q_bank[:, j * P:(j + 1) * P], norm.normed[:, 4 * g + j, i * P:(i + 1) * P], ident[:, :])
                else:
                    pe.wait_ge(qin, 32)
                    for c in range(DC):
                        last = pe.matmul(q_bank[0:QK, :], wq[:, c, :], tokT[:, c, g * BANK:(g + 1) * BANK],
                                         start=(c == 0), stop=(c == DC - 1))
                last.then_inc(q_full, 1)

            for i in range(FILLS_G):
                fill_queries(0, i)
            pe.wait_ge(by_act, FILLS_K)
            pe.wait_ge(by_dve, FILLS_V)
            pe.wait_ge(padded, 2)
            pe.wait_ge(q_copied, FILLS_G)

            def score(b, i, t):
                rows = key_rows(t)
                pe.wait_ge(z_done, KT * b + t + 1)
                pe.matmul(z_bank_of(i, t)[0:rows, 0:ZQ], kT[:, t * P:t * P + rows], qT[:, bass.ds(b * ZQ, ZQ)],
                          start=True, stop=True).then_inc(z_ready, 1)

            def weigh(b, i, k):
                tt, t = divmod(k, KT)
                rows = key_rows(t)
                if t == 0:
                    pe.wait_ge(o_done, ZT * b + tt + 1)
                if tt == 0:
                    pe.wait_ge(z_done, KT * b + t + 1 + Z_AHEAD)
                last = pe.matmul(o_bank[tt][:, 0:D], z[i][0:rows, t, tt * P:(tt + 1) * P], v[0:rows, t, :],
                                 start=(t == 0), stop=(t == KT - 1))
                if t == KT - 1:
                    last.then_inc(o_ready, 1)

            def block_step(b, i):
                for t in range(KT):
                    score(b, i, t)
                    for j in range(ZT):
                        weigh(b - 1, 1 - i, ZT * t + j)
                    if isinstance(b, int):
                        for fill in fills_after(b, t):
                            fill_queries(*fill)

            for t in range(KT):
                score(0, 0, t)
            block_step(1, 1)
            pe.wait_ge(q_copied, 2 * FILLS_G)
            block_step(2, 0)
            pe.wait_ge(q_copied, NORM_GROUPS * FILLS_G)
            with pe.Fori(1, ZB // 2 - 1) as r:
                block_step(2 * r + 1, 1)
                block_step(2 * r + 2, 0)
            block_step(ZB - 1, 1)
            for k in range(ZT * KT):
                weigh(ZB - 1, 1, k)

        @block.scalar
        def _(act):
            fills = 0
            act.sem_inc(z_done, Z_AHEAD)
            act.wait_ge(kin, 48)
            for n0 in range(0, S, BANK):
                n1 = min(S, n0 + BANK)
                act.wait_ge(bank_full, fills + 1)
                act.activation(kT[0:QK, n0:n1], bank[fills % 4][0:QK, 0:n1 - n0], ACT.Identity, bias=bk[:, 0:1]).then_inc(by_act, 1)
                fills += 1
            fills += FILLS_V
            norm.on_scalar(act, 0)

            def copy_queries(g, i):
                act.wait_ge(q_full, FILLS_G * g + i + 1)
                if i < DC:
                    act.activation(tokT[:, i, g * BANK:(g + 1) * BANK], q_bank[:, :], ACT.Copy).then_inc(q_copied, 1)
                else:
                    act.activation(qT[0:QK, g * BANK:(g + 1) * BANK], q_bank[0:QK, :], ACT.Identity, bias=bq[:, 0:1]
                                   ).then_inc(q_copied, 1)

            act.wait_ge(qin, 32)
            for i in range(FILLS_G):
                copy_queries(0, i)

            def squash(b, i):
                for t in range(KT):
                    rows = key_rows(t)
                    act.wait_ge(z_ready, KT * b + t + 1)
                    act.activation(z[i][0:rows, t, :], z_bank_of(i, t)[0:rows, 0:ZQ], ACT.Sigmoid, scale=QK ** -0.5
                                   ).then_inc(z_done, 1)
                    if isinstance(b, int):
                        for fill in fills_after(b, t):
                            copy_queries(*fill)
                        if (b, t) == ROOTS_AT:
                            norm.on_scalar(act, 3)

            def squash_two(r):
                act.wait_ge(o_ready, ZT * (2 * r + 1))
                squash(2 * r + 2, 0)
                act.wait_ge(o_ready, ZT * (2 * r + 2))
                quant.norm.on_scalar(act, r)
                squash(2 * r + 3, 1)
                quant.squares_on_scalar(act, r)

            norm.on_scalar(act, 1)
            squash(0, 0)
            norm.on_scalar(act, 2)
            squash(1, 1)
            squash_two(0)
            with act.Fori(1, ZB // 2 - 1) as r:
                squash_two(r)
                quant.integers(act, r - 1)
            quant.norm.on_scalar(act, NORM_GROUPS - 1)
            quant.squares_on_scalar(act, NORM_GROUPS - 1)
            quant.integers(act, NORM_GROUPS - 2)

        @block.vector
        def _(dve):
            dve.sem_inc(o_done, 2)
            dve.memset(qT[QK:P, :], 0.0).then_inc(padded, 1)
            dve.memset(kT[QK:P, :], 0.0).then_inc(padded, 1)

            def add_fetched(g):
                dve.wait_ge(fetched[g], 16 * TOP * NORM_GROUP)
                first = TOP * NORM_GROUP * g
                for k in range(TOP):
                    for i in range(NORM_GROUP):
                        t = NORM_GROUP * g + i
                        if k:
                            dve.wait_ge(added, first + i + 1)
                        dve.scalar_tensor_tensor(x_tok[:, t, :], got[k][:, t, :], route["weight"][k][:, t:t + 1],
                                                 x_tok[:, t, :], ALU.mult, ALU.add).then_inc(added, 1)
                dve.wait_ge(added, first + TOP * NORM_GROUP)

            dve.memset(norm.eps[:, :], EPS_LN).then_inc(norm.stats_done, 1)
            dve.wait_ge(vin, 32)
            for t in range(KT):
                rows, f = key_rows(t), FILLS_K + t
                dve.wait_ge(bank_full, f + 1)
                dve.tensor_tensor(v[0:rows, t, :], bank[f % 4][0:rows, 0:D], bv[0:rows, :], ALU.add).then_inc(by_dve, 1)
                if t == KT - 6:
                    add_fetched(0)
                if t == KT - 4:
                    norm.take_stats(dve, x_tok, 0)
                if t == KT - 2:
                    norm.normalize(dve, x_tok, 0)
            for g in range(1, NORM_GROUPS):
                add_fetched(g)
                norm.take_stats(dve, x_tok, g)
                norm.normalize(dve, x_tok, g)

            def add_out(b):
                for tt in range(ZT):
                    dve.wait_ge(o_ready, ZT * b + tt + 1)
                    xv = x_tok[:, b * ZT + tt, :]
                    dve.tensor_tensor(xv, xv, o_bank[tt][:, 0:D], ALU.add).then_inc(o_done, 1)

            quant.start(dve)
            blocks = NORM_GROUP // ZT
            for g in range(NORM_GROUPS):
                for b in range(blocks * g, blocks * (g + 1)):
                    add_out(b)
                    if g and b == blocks * g:
                        quant.hold(dve, layer.w_mean, g - 1)
                dve.wait_ge(o_done, ZT * blocks * (g + 1) + 2)
                quant.stats_and_norm(dve, x_tok, g)
            quant.hold(dve, layer.w_mean, NORM_GROUPS - 1)


def feed_forward(nc, a, keep, x_tok, layer, quant, out):
    with ExitStack() as scope:
        m = Memory(nc, scope)
        ident_bf = keep["ident_bf"]
        (t1, t2), w_mean = layer.ternary, layer.w_mean
        b1, b2 = m.sb("b1_rows", [P, HID]), m.sb("b2_rows", [P, D])
        q1T = m.sb("q1T", [P, DC, N], BF16)
        h = m.sb("h", [P, NT, HID])
        squares = [m.sb(f"squares{i}", [P, HID]) for i in range(2)]
        q2 = [m.sb(f"q2_{i}", [P, HID], BF16) for i in range(2)]
        q2T = [m.sb(f"q2T_{i}", [P, HC, P], BF16) for i in range(2)]
        ssq, big, root, factor, back = (m.sb(f"hidden_{n}", [P, NT]) for n in ("ssq", "big", "root", "factor", "back"))
        pre = [m.ps(f"pre{i}", [P, 2, BANK]) for i in range(2)]
        turn = [m.ps(f"fturn{i}", [P, 2 * BANK], BF16) for i in range(2)]
        y_bank = [m.ps(f"fy_bank{i}", [P, BANK]) for i in range(2)]

        b_in = m.sem("ff_b_in")
        chain = m.sem("ff_chain")
        squared, rooted = m.sem("squared"), m.sem("rooted")
        t_full = m.sem("ff_t_full")
        t_free = [m.sem(f"ff_t_free{c}") for c in range(DC)]
        b2_added = m.sem("b2_added")
        pre_ready, pre_read = m.sem("pre_ready"), m.sem("pre_read")
        gelu_done, h_seen = m.sem("gelu_done"), m.sem("h_seen")
        factored, rounded, q2_ready = m.sem("factored"), m.sem("rounded"), m.sem("q2_ready")
        turned2, q2T_ready = m.sem("turned2"), m.sem("q2T_ready")
        y_ready, y_done = m.sem("fy_ready"), m.sem("fy_done")
        stored = m.sem("stored")

        GT = 4
        Q_AHEAD = 4
        EARLY, LATE = slice(0, NT - GT), slice(NT - GT, NT)

        block = scope.enter_context(nc.Block())

        @block.sync
        def _(sp):
            sp.dma_start(b1[:, :], a["b1"].partition_broadcast(P)).then_inc(b_in, 16)
            sp.dma_start(b2[:, :], a["b2"].partition_broadcast(P)).then_inc(b_in, 16)
            for g in range(NT // GT):
                sp.wait_ge(y_done, GT * (g + 1) + 2)
                sp.dma_start(out.rearrange("b (t p) d -> p (b t) d", p=P)[:, GT * g:GT * (g + 1), :],
                             x_tok[:, GT * g:GT * (g + 1), :]).then_inc(stored, 16)
            sp.wait_ge(stored, 16 * (NT // GT))

        @block.gpsimd
        def _(pool):
            pool.wait_ge(b_in, 32)
            for t in range(NT):
                if t:
                    pool.wait_ge(b2_added, t)
                pool.tensor_tensor(x_tok[:, t, :], x_tok[:, t, :], b2[:, :], ALU.add).then_inc(b2_added, 1)

        @block.tensor
        def _(pe):
            def turn_group(g):
                pe.wait_ge(quant.quantized, g + 1)
                for c in range(DC):
                    if g:
                        pe.wait_ge(t_free[c], g)
                    for j in range(GT):
                        last = pe.transpose(turn[c][:, j * P:(j + 1) * P], quant.ints[:, GT * g + j, c * P:(c + 1) * P],
                                            ident_bf[:, :])
                    last.then_inc(t_full, 1)

            def up(t, i):
                pe.wait_ge(pre_read, t + 1)
                for half in range(2):
                    for c in range(DC):
                        last = pe.matmul(pre[i][:, half, :], q1T[:, c, bass.ds(t * P, P)],
                                         t1[:, c, half * BANK:(half + 1) * BANK], start=(c == 0), stop=(c == DC - 1))
                last.then_inc(pre_ready, 1)

            turn_group(0)
            turn_group(1)
            up(0, 0)
            turn_group(2)
            up(1, 1)
            turn_group(3)
            for c in range(DC):
                pe.wait_ge(t_free[c], NT // GT)
            with pe.Fori(1, NT // 2) as r:
                for i in range(2):
                    up(2 * r + i, i)

            def turn_hidden(t, i):
                pe.wait_ge(q2_ready, t + 1)
                if not isinstance(t, int) or t >= 2:
                    pe.wait_ge(q2T_ready, t - 1)
                for c in range(HC):
                    last = pe.transpose(turn[i][:, c * P:(c + 1) * P], q2[i][:, c * P:(c + 1) * P], ident_bf[:, :])
                last.then_inc(turned2, 1)

            def down(t, i):
                pe.wait_ge(q2T_ready, t + 1)
                pe.wait_ge(y_done, t + 1)
                for c in range(HC):
                    last = pe.matmul(y_bank[i][:, 0:D], q2T[i][:, c, :], t2[:, c, :], start=(c == 0), stop=(c == HC - 1))
                last.then_inc(y_ready, 1)

            turn_hidden(0, 0)
            turn_hidden(1, 1)
            with pe.Fori(0, NT // 2 - 1) as r:
                for i in range(2):
                    down(2 * r + i, i)
                    turn_hidden(2 * r + i + 2, i)
            down(NT - 2, 0)
            down(NT - 1, 1)

        @block.scalar
        def _(act):
            quant.integers(act, NORM_GROUPS - 1)
            for g in range(NORM_GROUPS):
                act.wait_ge(t_full, DC * g + 1)
                act.activation(q1T[:, 0, g * BANK:(g + 1) * BANK], turn[0][:, 0:BANK], ACT.Copy).then_inc(t_free[0], 1)
            act.sem_inc(squared, 2)

            def gelus(r, part=range(GT)):
                for i in part:
                    t = r * GT + i
                    act.wait_ge(pre_read, t + 3)
                    hv = h[:, bass.ds(t, 1), :].rearrange("p o d -> p (o d)")
                    act.activation(hv, hv, ACT.Gelu).then_inc(gelu_done, 1)

            def square_sums(r):
                for i in range(GT):
                    t = r * GT + i
                    hv = h[:, bass.ds(t, 1), :].rearrange("p o d -> p (o d)")
                    act.wait_ge(gelu_done, t + 1)
                    act.wait_ge(squared, t + 1)
                    act.activation(squares[i % 2][:, :], hv, ACT.Square, accum_out=ssq[:, bass.ds(t, 1)]).then_inc(squared, 1)

            def roots(tiles):
                act.wait_ge(squared, tiles.stop + 2)
                act.activation(root[:, tiles], ssq[:, tiles], ACT.Sqrt, bias=quant.eps[:, 0:1], scale=1.0 / HID
                               ).then_inc(rooted, 1)

            def to_bf16(t, i):
                act.wait_ge(rounded, t + 1)
                act.activation(q2[i][:, :], h[:, bass.ds(t, 1), :].rearrange("p o d -> p (o d)"), ACT.Copy, bias=-ROUND
                               ).then_inc(q2_ready, 1)

            def copy_turned(t, i):
                act.wait_ge(turned2, t + 1)
                act.activation(q2T[i][:, :, :].rearrange("p c n -> p (c n)"), turn[i][:, :], ACT.Copy).then_inc(q2T_ready, 1)

            with act.Fori(0, NT // GT - 1) as r:
                gelus(r)
                square_sums(r)
            roots(EARLY)
            gelus(NT // GT - 1, range(GT - 1))
            to_bf16(0, 0)
            gelus(NT // GT - 1, range(GT - 1, GT))
            to_bf16(1, 1)
            copy_turned(0, 0)
            square_sums(NT // GT - 1)
            roots(LATE)
            with act.Fori(0, NT // 2 - 1) as r:
                for i in range(2):
                    t = 2 * r + i
                    act.wait_ge(turned2, t + 1)
                    to_bf16(t + 2, i)
                    act.wait_ge(y_ready, t + 1)
                    copy_turned(t + 1, 1 - i)
            copy_turned(NT - 1, 1)

        @block.vector
        def _(dve):
            made = 0

            def link(ins):
                nonlocal made
                made += 1
                ins.then_inc(chain, 1)
                dve.wait_ge(chain, made)

            dve.sem_inc(pre_read, 2)
            for g in range(NORM_GROUPS):
                dve.wait_ge(t_full, DC * g + 2)
                dve.tensor_copy(q1T[:, 1, g * BANK:(g + 1) * BANK], turn[1][:, 0:BANK]).then_inc(t_free[1], 1)
            dve.wait_ge(b_in, 32)
            dve.sem_inc(y_done, 2)

            def bias(t, i):
                dve.wait_ge(pre_ready, t + 1)
                dve.scalar_tensor_tensor(h[:, bass.ds(t, 1), :].rearrange("p o (a n) -> p (o a) n", a=2), pre[i][:, :, :],
                                         quant.back[:, bass.ds(t, 1)], b1[:, :].rearrange("p (a n) -> p a n", a=2),
                                         ALU.mult, ALU.add).then_inc(pre_read, 1)

            def largest(t):
                dve.wait_ge(gelu_done, t + 1)
                dve.tensor_reduce(big[:, bass.ds(t, 1)], h[:, bass.ds(t, 1), :].rearrange("p o d -> p (o d)"), AX.X,
                                  ALU.max, apply_absolute_value=True).then_inc(h_seen, 1)

            for t in range(GT):
                bias(t, t % 2)
            with dve.Fori(0, EARLY.stop // 2) as r:
                for i in range(2):
                    largest(2 * r + i)
                    bias(2 * r + i + GT, i)

            def scale(tiles, part):
                dve.wait_ge(rooted, part)
                dve.wait_ge(h_seen, tiles.stop)
                scales(dve, link, root[:, tiles], big[:, tiles], back[:, tiles], factor[:, tiles], w_mean[:, 1:2])

            def quantize(t):
                hv = h[:, bass.ds(t, 1), :].rearrange("p o d -> p (o d)")
                dve.tensor_scalar(hv, hv, factor[:, bass.ds(t, 1)], ROUND, ALU.mult, ALU.add).then_inc(factored, 1)
                dve.wait_ge(factored, t + 1)
                dve.tensor_scalar(hv, hv, ROUND + LEVELS, ROUND - LEVELS - 1, ALU.min, ALU.max
                                  ).then_inc(rounded, 1)

            def finish(t, i):
                dve.wait_ge(y_ready, t + 1)
                xv = x_tok[:, bass.ds(t, 1), :].rearrange("p o d -> p (o d)")
                dve.scalar_tensor_tensor(xv, y_bank[i][:, 0:D], back[:, bass.ds(t, 1)], xv, ALU.mult, ALU.add
                                         ).then_inc(y_done, 1)

            scale(EARLY, 1)
            for t in range(Q_AHEAD // 2):
                quantize(t)
            for t in range(LATE.start, NT):
                largest(t)
            for t in range(Q_AHEAD // 2, Q_AHEAD):
                quantize(t)
            scale(LATE, 2)
            dve.wait_ge(b2_added, NT)
            with dve.Fori(0, (NT - Q_AHEAD) // 2) as r:
                for i in range(2):
                    quantize(2 * r + i + Q_AHEAD)
                    finish(2 * r + i, i)
            for t in range(NT - Q_AHEAD, NT):
                finish(t, t % 2)


def build(nc, a, out):
    q_parts_dram = nc.dram_tensor("q_parts", (3, D, N), BF16, kind="Internal").ap()
    k_parts_dram = nc.dram_tensor("k_parts", (3, D, S), BF16, kind="Internal").ap()
    with ExitStack() as scope:
        m = Memory(nc, scope)
        x_tok = m.sb("x_tok", [P, NT, D])
        ident, ident_bf = m.sb("ident", [P, P]), m.sb("ident_bf", [P, P], BF16)
        with ExitStack() as inner:
            mi = Memory(nc, inner)
            values = mi.sb("values", [P, GROUPS * KT * HG * HEAD_PE])
            q_aug = mi.sb("q_aug", [P, RING, HG * BANK], BF16)
            keep = {
                "ident": ident, "ident_bf": ident_bf,
                "q_aug": q_aug, "q_aug_flat": q_aug[:, :, :].rearrange("p s n -> p (s n)"),
                "k_aug": mi.sb("k_aug", [P, H, S], BF16),
                "aug_in": mi.sem("aug_in"), "rest_in": mi.sem("rest_in"), "q_in": mi.sem("q_in"),
                "values_flat": values,
                "values": values[:, :].rearrange("p (g t h w) -> p g t h w", g=GROUPS, t=KT, h=HG),
            }
            project(nc, a, keep, x_tok, q_parts_dram, k_parts_dram)
            attend(nc, keep, x_tok, q_parts_dram)
        slots_in = nc.dram_tensor("slots_in", (SLOTS + TOP * N, D), F32, kind="Internal").ap()
        slots_out = nc.dram_tensor("slots_out", (SLOTS, D), F32, kind="Internal").ap()
        route = {
            "send": [m.sb(f"send{k}", [P, NT], U32) for k in range(TOP)],
            "fetch": [m.sb(f"fetch{k}", [P, NT], U32) for k in range(TOP)],
            "weight": [m.sb(f"weight{k}", [P, NT]) for k in range(TOP)],
        }
        keep = {"ident": ident, "ident_bf": ident_bf}
        layer = NextLayer(m)
        with ExitStack() as inner:
            normed = Memory(nc, inner).sb("ln2_normed", [P, NT, D])
            route_and_share(nc, a, keep, x_tok, normed, slots_in, route, layer)
        run_experts(nc, a, keep, slots_in, slots_out)
        quant = Quantization(m)
        combine_and_attend(nc, a, keep, x_tok, slots_out, route, layer, quant)
        feed_forward(nc, a, keep, x_tok, layer, quant, out)


def kernel(**inputs):
    import numpy as _np
    import concourse.bacc as _bacc
    from concourse import mybir as _mybir
    from concourse.bass_utils import run_bass_kernel_spmd as _run

    given = {k: _np.asarray(v) for k, v in inputs.items()}
    laid = {
        "x": given["x"],
        "ctxT": given["ctx_1024"][0].T,
        "mask": given["mask_BxS2_ik0"],
        "wqT": given["L0_xattn_Wq"].T,
        "wkT": given["L0_xattn_Wk"].T,
        "wvT": given["L0_xattn_Wv"].T,
        "bq": given["L0_xattn_bq"],
        "bk": given["L0_xattn_bk"],
        "bv": given["L0_xattn_bv"],
        "gate_w": given["L0_ffn_gate_w"],
        "gate_b": given["L0_ffn_gate_b"],
        "ew1": given["L0_ffn_ew1"],
        "ew3": given["L0_ffn_ew3"],
        "ew2": given["L0_ffn_ew2"],
        "sw1": given["L0_ffn_sw1"],
        "sw3": given["L0_ffn_sw3"],
        "sw2": given["L0_ffn_sw2"],
        "wq1T": given["L1_xattn_Wq"].T,
        "wk1T": given["L1_xattn_Wk"].T,
        "wv1T": given["L1_xattn_Wv"].T,
        "bq1": given["L1_xattn_bq"],
        "bk1": given["L1_xattn_bk"],
        "bv1": given["L1_xattn_bv"],
        "w1T": given["L1_ffn_w1"].T,
        "b1": given["L1_ffn_b1"],
        "w2T": given["L1_ffn_w2"].T,
        "b2": given["L1_ffn_b2"],
        "const": shape_constants(_np),
    }
    nc = _bacc.Bacc("TRN2", target_bir_lowering=False, num_devices=1)
    arrays, aps = {}, {}
    for name, a in laid.items():
        a = _np.ascontiguousarray(a)
        arrays[f"in_{name}"] = a
        aps[name] = nc.dram_tensor(f"in_{name}", a.shape, _mybir.dt.from_np(a.dtype), kind="ExternalInput").ap()
    out = nc.dram_tensor("out_x", (1, N, D), F32, kind="ExternalOutput").ap()
    build(nc, aps, out)
    r = _run(nc, [arrays], core_ids=[0])
    return r.results[0]["out_x"]
```
